# Optimizing a Trainium2 kernel written in Bass

```python
import numpy as np
import jax
import jax.numpy as jnp

def _softmax(x, axis=-1):
    return jax.nn.softmax(x, axis=axis)

def _gelu(x):
    return jax.nn.gelu(x, approximate=True)

def _silu(x):
    return jax.nn.silu(x)

def _sigmoid(x):
    return jax.nn.sigmoid(x)

def _layernorm(x, axis=-1, eps=1e-05):
    m = jnp.mean(x, axis=axis, keepdims=True)
    v = jnp.var(x, axis=axis, keepdims=True)
    return (x - m) / jnp.sqrt(v + eps)

def _scatter_add(tgt, idx, src, axis=0):
    return tgt.at[idx].add(src)

def _segment_sum(src, seg, n):
    return jax.ops.segment_sum(src, seg, n)
kernel_name = 'mk_macaron_d1_jaxref_r8_8e9f10'

def setup_inputs(seed: int=0):
    np.random.seed(seed)
    _w = jnp.asarray

    def _L0_attn_setup():
        import jax, jax.numpy as jnp
        import numpy as np
        B, T, C, H = (4, 256, 128, 8)
        D = C // H

        def _rope_tables(t, d, base=10000.0):
            inv = 1.0 / base ** (jnp.arange(0, d, 2, dtype=jnp.float32) / d)
            freqs = jnp.outer(jnp.arange(t, dtype=jnp.float32), inv)
            cos = jnp.concatenate([jnp.cos(freqs)] * 2, axis=-1)
            sin = jnp.concatenate([jnp.sin(freqs)] * 2, axis=-1)
            return (cos, sin)

        def _apply_rope(x, cos, sin):
            d2 = x.shape[-1] // 2
            x1, x2 = (x[..., :d2], x[..., d2:])
            rot = jnp.concatenate([-x2, x1], axis=-1)
            return x * cos + rot * sin
        key = jax.random.key(seed)
        ks = jax.random.split(key, 8)
        x = jax.random.normal(ks[0], (B, T, C), jnp.float32)
        w = lambda k: jax.random.normal(k, (C, C), jnp.float32) * 0.02
        signs = np.array([[1 if i >> b & 1 else -1 for b in range(3)] for i in range(8)], np.float32)
        head_dirs = jnp.asarray(signs / np.sqrt(3.0))
        return {'x': x, 'Wq': w(ks[1]), 'Wk': w(ks[2]), 'Wv': w(ks[3]), 'Wo': w(ks[4]), 'ln_g': jnp.ones((C,), jnp.float32), 'ln_b': jnp.zeros((C,), jnp.float32), 'head_scales': jax.random.normal(ks[5], (H,), jnp.float32) * 0.1, 'head_dirs': head_dirs}
    _L0_attn_in = _L0_attn_setup()

    def _L0_ffn_setup():
        import jax, jax.numpy as jnp
        import numpy as np
        D_MODEL = 128
        D_HIDDEN = 512
        NUM_EXPERTS = 8
        B, T = (2, 256)
        key = jax.random.key(seed)
        ks = jax.random.split(key, 8)
        s = 0.02
        x = jax.random.normal(ks[0], (B, T, D_MODEL), dtype=jnp.float32)
        Wg = jax.random.normal(ks[1], (D_MODEL, NUM_EXPERTS), dtype=jnp.float32) * s
        bg = jnp.zeros((NUM_EXPERTS,), dtype=jnp.float32)
        W1 = jax.random.normal(ks[2], (NUM_EXPERTS, D_MODEL, D_HIDDEN), dtype=jnp.float32) * s
        b1 = jnp.zeros((NUM_EXPERTS, D_HIDDEN), dtype=jnp.float32)
        W2 = jax.random.normal(ks[3], (NUM_EXPERTS, D_HIDDEN, D_MODEL), dtype=jnp.float32) * s
        b2 = jnp.zeros((NUM_EXPERTS, D_MODEL), dtype=jnp.float32)
        return {'x': x, 'Wg': Wg, 'bg': bg, 'W1': W1, 'b1': b1, 'W2': W2, 'b2': b2}
    _L0_ffn_in = _L0_ffn_setup()
    _d = {'L0_attn_x': _L0_attn_in['x'], 'L0_attn_Wq': _L0_attn_in['Wq'], 'L0_attn_Wk': _L0_attn_in['Wk'], 'L0_attn_Wv': _L0_attn_in['Wv'], 'L0_attn_Wo': _L0_attn_in['Wo'], 'L0_attn_ln_g': _L0_attn_in['ln_g'], 'L0_attn_ln_b': _L0_attn_in['ln_b'], 'L0_attn_head_scales': _L0_attn_in['head_scales'], 'L0_attn_head_dirs': _L0_attn_in['head_dirs'], 'L0_ffn_Wg': _L0_ffn_in['Wg'], 'L0_ffn_bg': _L0_ffn_in['bg'], 'L0_ffn_W1': _L0_ffn_in['W1'], 'L0_ffn_b1': _L0_ffn_in['b1'], 'L0_ffn_W2': _L0_ffn_in['W2'], 'L0_ffn_b2': _L0_ffn_in['b2']}
    _x0 = _d['L0_attn_x']
    _d['L0_attn_x'] = jax.random.normal(jax.random.fold_in(jax.random.key(seed), 1), (1, 2048, 128), dtype=_x0.dtype)
    del _x0
    return _d

def reference(L0_attn_x, L0_attn_Wq, L0_attn_Wk, L0_attn_Wv, L0_attn_Wo, L0_attn_ln_g, L0_attn_ln_b, L0_attn_head_scales, L0_attn_head_dirs, L0_ffn_Wg, L0_ffn_bg, L0_ffn_W1, L0_ffn_b1, L0_ffn_W2, L0_ffn_b2):

    def _L0_attn_ref(x, Wq, Wk, Wv, Wo, ln_g, ln_b, head_scales, head_dirs):
        import jax, jax.numpy as jnp
        import numpy as np
        B, T, C, H = (4, 256, 128, 8)
        D = C // H

        def _rope_tables(t, d, base=10000.0):
            inv = 1.0 / base ** (jnp.arange(0, d, 2, dtype=jnp.float32) / d)
            freqs = jnp.outer(jnp.arange(t, dtype=jnp.float32), inv)
            cos = jnp.concatenate([jnp.cos(freqs)] * 2, axis=-1)
            sin = jnp.concatenate([jnp.sin(freqs)] * 2, axis=-1)
            return (cos, sin)

        def _apply_rope(x, cos, sin):
            d2 = x.shape[-1] // 2
            x1, x2 = (x[..., :d2], x[..., d2:])
            rot = jnp.concatenate([-x2, x1], axis=-1)
            return x * cos + rot * sin
        b, t, c = x.shape
        h = head_dirs.shape[0]
        d = c // h
        scale = 1.0 / jnp.sqrt(jnp.asarray(d, x.dtype))
        mu = jnp.mean(x, axis=-1, keepdims=True)
        var = jnp.mean((x - mu) ** 2, axis=-1, keepdims=True)
        xn = (x - mu) * jax.lax.rsqrt(var + 1e-05) * ln_g + ln_b
        q = (xn @ Wq.T).reshape(b, t, h, d).transpose(0, 2, 1, 3)
        k = (xn @ Wk.T).reshape(b, t, h, d).transpose(0, 2, 1, 3)
        v = (xn @ Wv.T).reshape(b, t, h, d).transpose(0, 2, 1, 3)
        cos, sin = _rope_tables(t, d)
        q = _apply_rope(q, cos, sin)
        k = _apply_rope(k, cos, sin)
        causal = jnp.tril(jnp.ones((t, t), bool))
        scores = jnp.einsum('bhqd,bhkd->bhqk', q, k) * scale
        scores = jnp.where(causal, scores, -jnp.inf)
        attn = jax.nn.softmax(scores, axis=-1)
        out = jnp.einsum('bhqk,bhkd->bhqd', attn, v)
        qp = jnp.einsum('bhtd,hd->bht', q[..., :3], head_dirs)
        kp = jnp.einsum('bhtd,hd->bht', k[..., :3], head_dirs)
        geo = qp[..., :, None] * kp[..., None, :]
        geo = jnp.where(causal, geo, -jnp.inf)
        geo_attn = jax.nn.softmax(geo, axis=-1)
        geo_out = jnp.einsum('bhqk,bhkd->bhqd', geo_attn, v)
        out = out + head_scales[None, :, None, None] * jax.lax.stop_gradient(geo_out - out)
        out = out.transpose(0, 2, 1, 3).reshape(b, t, c) @ Wo.T
        return x + out

    def _L0_ffn_ref(x, Wg, bg, W1, b1, W2, b2):
        import jax, jax.numpy as jnp
        import numpy as np
        D_MODEL = 128
        D_HIDDEN = 512
        NUM_EXPERTS = 8
        B, T = (2, 256)
        gate_logits = jnp.einsum('btd,de->bte', x, Wg) + bg
        gate_scores = jax.nn.softmax(gate_logits, axis=-1)
        top1_idx = jnp.argmax(gate_scores, axis=-1)
        top1_mask = jax.nn.one_hot(top1_idx, NUM_EXPERTS, dtype=x.dtype)
        top1_weight = jnp.sum(gate_scores * top1_mask, axis=-1, keepdims=True)
        h = jax.nn.silu(jnp.einsum('btd,edh->bteh', x, W1) + b1)
        o = jnp.einsum('bteh,ehd->bted', h, W2) + b2
        y = jnp.sum(o * top1_mask[..., None], axis=2) * top1_weight
        return y
    x = L0_attn_x
    x = x + 0.5 * _L0_ffn_ref(_layernorm(x, axis=-1), L0_ffn_Wg, L0_ffn_bg, L0_ffn_W1, L0_ffn_b1, L0_ffn_W2, L0_ffn_b2)
    x = x + _L0_attn_ref(_layernorm(x, axis=-1), L0_attn_Wq, L0_attn_Wk, L0_attn_Wv, L0_attn_Wo, L0_attn_ln_g, L0_attn_ln_b, L0_attn_head_scales, L0_attn_head_dirs)
    x = x + 0.5 * _L0_ffn_ref(_layernorm(x, axis=-1), L0_ffn_Wg, L0_ffn_bg, L0_ffn_W1, L0_ffn_b1, L0_ffn_W2, L0_ffn_b2)
    return x

_drawn_inputs = setup_inputs


def setup_inputs(seed=0):
    import zlib

    import numpy as np

    out = dict(_drawn_inputs(seed))
    spreads = {'L0_attn_ln_g': (1.0, 0.6),
     'L0_attn_ln_b': (0.0, 0.8),
     'L0_ffn_bg': (0.0, 0.8),
     'L0_ffn_b1': (0.0, 0.8),
     'L0_ffn_b2': (0.0, 0.614)}
    factors = {'L0_attn_Wq': 8.0,
     'L0_attn_Wk': 8.0,
     'L0_attn_Wv': 8.0,
     'L0_attn_Wo': 8.0,
     'L0_attn_head_scales': 8.0,
     'L0_attn_head_dirs': 8.0,
     'L0_ffn_Wg': 4.091,
     'L0_ffn_W1': 8.0,
     'L0_ffn_W2': 7.531}
    for name, (base, spread) in spreads.items():
        noise = np.random.default_rng([zlib.crc32(name.encode()), seed]).standard_normal(out[name].shape)
        drawn = base * np.exp(spread * noise) if base else spread * noise
        out[name] = jnp.asarray(drawn.astype(out[name].dtype))
    for name, factor in factors.items():
        out[name] = (out[name] * factor).astype(out[name].dtype)
    return out
```

```python
from contextlib import ExitStack

import numpy as np

import concourse.bass as bass
from concourse import mybir
from concourse.alu_op_type import AluOpType as ALU

ACT = mybir.ActivationFunctionType
AX = mybir.AxisListType
F32 = mybir.dt.float32
BF16 = mybir.dt.bfloat16
I32 = mybir.dt.int32

P = 128
T = 2048
NT = T // P
C = 128
H = 8
D = C // H
E = 8
F = 512
KF = F // P
NB = (T + E * (P - 1)) // P
GB = 4
EPS = 1e-5
N_FIRST_LOADS = 5
NEG = -1e38
SKIP = 4096.0

CH = 512
NCH = T // CH
NPAIR = H // 2
PARTS = 3
PRODUCTS = [(0, 0), (0, 1), (0, 2), (1, 0), (1, 1), (2, 0)]
KQ = len(PRODUCTS) * D
KS = KQ + PARTS
GR = PARTS * PARTS + PARTS


class Columns:

    def __init__(self, **widths):
        self.at, self.width = {}, 0
        for name, w in widths.items():
            self.at[name] = (self.width, w)
            self.width += w


FC = Columns(ident=P, lane=P, blocks=NB, thresholds=NT, rank=E, token=1, tile=NT, head_rows=H,
             cos=NT * D, sin=NT * D)
BC = Columns(ident=P, before=P, ones=P, future=P, future_t=P)


def float_constants():
    t = np.zeros((P, FC.width), np.float32)

    def put(name, a):
        o, w = FC.at[name]
        t[:, o:o + w] = a

    p = np.arange(P, dtype=np.float32)[:, None]
    put("ident", np.eye(P))
    put("lane", np.arange(P)[None])
    put("blocks", np.arange(NB)[None])
    put("thresholds", P * np.arange(NT)[None])
    put("rank", E - np.arange(E)[None])
    put("token", p)
    put("tile", np.arange(NT)[None])
    put("head_rows", (np.arange(P)[:, None] // GR) == np.arange(H)[None])
    inverse = np.float32(1.0) / np.float32(10000.0) ** (np.arange(0, D, 2, dtype=np.float32) / np.float32(D))
    angle = np.arange(T, dtype=np.float32)[:, None] * inverse[None].astype(np.float32)
    cos = np.concatenate([np.cos(angle)] * 2, 1).astype(np.float32)
    sin = np.concatenate([-np.sin(angle), np.sin(angle)], 1).astype(np.float32)
    put("cos", cos.reshape(NT, P, D).transpose(1, 0, 2).reshape(P, NT * D))
    put("sin", sin.reshape(NT, P, D).transpose(1, 0, 2).reshape(P, NT * D))
    return t


def bf16_constants(bf16):
    t = np.zeros((P, BC.width), np.float32)
    q = np.arange(P)[:, None]
    k = np.arange(P)[None]
    for name, a in (("ident", q == k), ("before", q < k), ("ones", np.ones((P, P))),
                    ("future", np.where(k > q, NEG, 0.0)), ("future_t", np.where(q > k, NEG, 0.0))):
        o, w = BC.at[name]
        t[:, o:o + w] = a
    return t.astype(bf16)


class Steps:

    def __init__(self, engine, sem):
        self.engine, self.sem, self.n, self.trip, self.per = engine, sem, 0, None, 0

    def value(self):
        return self.n if self.trip is None else self.trip * self.per + self.n

    def mark(self, instruction):
        instruction.then_inc(self.sem, 1)
        self.n += 1

    def link(self, instruction):
        self.mark(instruction)
        self.engine.wait_ge(self.sem, self.value())

    def enter(self, trip, per):
        self.trip, self.per, self.start = trip, per, self.n

    def leave(self, trips):
        assert self.n - self.start == self.per, (self.n - self.start, self.per)
        self.n, self.trip = self.start + self.per * trips, None


class Kernel:

    def __init__(self, nc, ctx, arg):
        self.nc, self.arg = nc, arg

        def sb(name, shape, dt=F32):
            return ctx.enter_context(nc.sbuf_tensor(name, shape, dt))

        self.x = sb("x_res", [P, NT, C])
        self.w1 = sb("w1", [P, E * F])
        self.w2 = sb("w2", [P, E * F])
        self.b1 = sb("b1", [P, E * F])
        self.b2 = sb("b2", [P, E * C])
        self.wg = sb("wg", [C, E])
        self.bg = sb("bg", [P, E])
        self.cf = sb("cf", [P, FC.width])
        self.cb = sb("cb", [P, BC.width], BF16)

    def c(self, name, a=0, b=None):
        o, w = FC.at[name]
        return self.cf[:, o + a:o + (w if b is None else b)]

    def cbf(self, name):
        o, w = BC.at[name]
        return self.cb[:, o:o + w]


def wide(ap, n):
    return ap.unsqueeze(2).broadcast_to([ap.shape[0], ap.shape[1], n])


def each(ap, n):
    return ap.unsqueeze(1).broadcast_to([ap.shape[0], n, ap.shape[1]])


def layernorm(nc, dve, steps, src, dst, square, stat, variance_ready, deviation_ready):
    v = nc.vector
    total, mean, var, inv = (stat[:, k, :] for k in range(4))
    steps.link(v.tensor_reduce(total, src, AX.X, ALU.add))
    steps.link(v.tensor_scalar(mean, total, 1.0 / C, None, ALU.mult))
    steps.link(v.tensor_tensor(dst, src, wide(mean, C), ALU.subtract))
    steps.link(v.tensor_tensor(square, dst, dst, ALU.mult))
    steps.link(v.tensor_reduce(total, square, AX.X, ALU.add))
    v.tensor_scalar(var, total, 1.0 / C, EPS, ALU.mult, ALU.add).then_inc(variance_ready, 1)
    dve.wait_ge(deviation_ready, 1)
    steps.link(v.reciprocal(inv, var))
    return v.tensor_tensor(dst, dst, wide(inv, C), ALU.mult)


def ffn(k, tag, load, result):
    nc = k.nc
    with ExitStack() as ctx:
        def sb(name, shape, dt=F32):
            return ctx.enter_context(nc.sbuf_tensor(f"{name}_{tag}", shape, dt))

        def sem(name):
            return ctx.enter_context(nc.semaphore(f"{name}_{tag}"))

        xn = sb("xn", [P, NT, C])
        stat = sb("stat", [P, 4, NT])
        weight = sb("weight", [P, NT])
        gather_index = sb("gather_index", [P, NB], I32)
        scatter_index = sb("scatter_index", [P, NB], I32)
        expert_offset = sb("expert_offset", [P, NB], I32)
        expert_offset2 = sb("expert_offset2", [P, NB], I32)
        xn_dram = nc.dram_tensor(f"xn_dram_{tag}", [T, C], F32, kind="Internal").ap()
        y_dram = nc.dram_tensor(f"y_dram_{tag}", [T, C], F32, kind="Internal").ap()
        route(k, tag, load, xn, stat, weight, gather_index, scatter_index, expert_offset, expert_offset2, xn_dram)
        experts(k, tag, xn_dram, y_dram, gather_index, scatter_index, expert_offset, expert_offset2)
        combine(k, tag, y_dram, xn, weight, result)


def route(k, tag, load, xn, stat, weight, gather_index, scatter_index, expert_offset, expert_offset2, xn_dram):
    nc = k.nc
    with ExitStack() as ctx:
        def sb(name, shape, dt=F32):
            return ctx.enter_context(nc.sbuf_tensor(f"{name}_{tag}", shape, dt))

        def ps(name, shape, dt=F32):
            return ctx.enter_context(nc.psum_tensor(f"{name}_{tag}", shape, dt))

        def sem(name):
            return ctx.enter_context(nc.semaphore(f"{name}_{tag}"))

        square = sb("square", [P, NT, C])
        xnT = sb("xnT", [C, T])
        logits = sb("logits", [P, NT, E])
        prob = sb("prob", [P, NT, E])
        score = sb("score", [P, NT, E])
        row = sb("row", [P, 4, NT])
        chosen = sb("chosen", [P, E, NT], BF16)
        in_tile = sb("in_tile", [P, E, NT])
        upto = sb("upto", [P, E, NT])
        full = sb("full", [P, E, NT])
        per_e = sb("per_e", [P, 6, E])
        pos = sb("pos", [P, E, NT])
        slot = sb("slot", [P, NT])
        slot_i = sb("slot_i", [P, 3, NT], I32)
        slot_f = sb("slot_f", [P, 2, NT])
        place = sb("place", [P, NT, P], BF16)
        payload = sb("payload", [P, NT, 3, NB], BF16)
        at_slot = sb("at_slot", [P, 3, NB])
        token = sb("token", [P, 2, NB])
        past = sb("past", [P, NB, E])
        block_e = sb("block_e", [P, 3, NB])
        xnT_ps = ps("xnT_ps", [P, 4, 512])
        gate_ps = ps("gate_ps", [P, 512])
        rank_ps = ps("rank_ps", [P, 512])
        total_ps = ps("total_ps", [P, 512])
        slot_ps = ps("slot_ps", [P, 512])

        loaded = sem("loaded")
        var_ready, dev_ready = sem("var_ready"), sem("dev_ready")
        xn_ready = sem("xn_ready")
        xn_stored = sem("xn_stored")
        transposed = sem("transposed")
        xnT_ready = sem("xnT_ready")
        gated = sem("gated")
        exp_in, exp_done = sem("exp_in"), sem("exp_done")
        chosen_ready = sem("chosen_ready")
        ranked = sem("ranked")
        slots_ready = sem("slots_ready")
        inverted = sem("inverted")
        dve_steps = sem("dve_steps")

        block = ctx.enter_context(nc.Block())

        @block.sync
        def _(sp):
            if load:
                load(sp, loaded)
            sp.wait_ge(xn_ready, 1)
            sp.dma_start(xn_dram.rearrange("(i p) c -> p i c", p=P), xn[:]).then_inc(xn_stored, 16)
            sp.wait_ge(xn_stored, 16)

        @block.scalar
        def _(act):
            act.wait_ge(var_ready, 1)
            nc.scalar.activation(stat[:, 2, :], stat[:, 2, :], ACT.Sqrt).then_inc(dev_ready, 1)
            for g in range(NT // GB):
                act.wait_ge(transposed, g + 1)
                nc.scalar.copy(xnT[:, g * 512:(g + 1) * 512], xnT_ps[:, g, :]).then_inc(xnT_ready, 1)
            act.wait_ge(exp_in, 1)
            nc.scalar.activation(prob[:], logits[:], ACT.Exp).then_inc(exp_done, 1)

        @block.tensor
        def _(pe):
            pe.wait_ge(xn_ready, 1)
            for i in range(NT):
                last = nc.tensor.transpose(xnT_ps[:, i // GB, (i % GB) * P:(i % GB + 1) * P], xn[:, i, :], k.c("ident"))
                if i % GB == GB - 1:
                    last.then_inc(transposed, 1)
            for i in range(NT):
                if i % GB == 0:
                    pe.wait_ge(xnT_ready, i // GB + 1)
                last = nc.tensor.matmul(gate_ps[:, i * E:(i + 1) * E], xnT[:, i * P:(i + 1) * P], k.wg[:], start=True, stop=True)
            last.then_inc(gated, 1)
            pe.wait_ge(chosen_ready, 1)
            flat = chosen[:].rearrange("p e i -> p (e i)")
            nc.tensor.matmul(rank_ps[:, 0:P], k.cbf("before"), flat, start=True, stop=True)
            nc.tensor.matmul(total_ps[:, 0:P], k.cbf("ones"), flat, start=True, stop=True).then_inc(ranked, 1)
            pe.wait_ge(slots_ready, 1)
            for i in range(NT):
                last = nc.tensor.matmul(slot_ps[:, 0:3 * NB], place[:, i, :], payload[:, i].rearrange("p a b -> p (a b)"),
                                        start=(i == 0), stop=(i == NT - 1))
            last.then_inc(inverted, 1)

        @block.vector
        def _(dve):
            v = nc.vector
            s = Steps(dve, dve_steps)
            if load:
                dve.wait_ge(loaded, 16 * N_FIRST_LOADS)
            layernorm(nc, dve, s, k.x[:], xn[:], square[:], stat, var_ready, dev_ready).then_inc(xn_ready, 1)

            dve.wait_ge(gated, 1)
            s.link(v.tensor_tensor(logits[:], gate_ps[:, 0:NT * E].rearrange("p (i e) -> p i e", e=E), each(k.bg[:], NT), ALU.add))
            s.link(v.tensor_reduce(row[:, 0, :], logits[:], AX.X, ALU.max))
            v.tensor_tensor(logits[:], logits[:], wide(row[:, 0, :], E), ALU.subtract).then_inc(exp_in, 1)
            dve.wait_ge(exp_done, 1)
            s.link(v.tensor_reduce(row[:, 1, :], prob[:], AX.X, ALU.add))
            s.link(v.tensor_reduce(row[:, 2, :], prob[:], AX.X, ALU.max))
            s.link(v.reciprocal(row[:, 1, :], row[:, 1, :]))
            s.link(v.scalar_tensor_tensor(weight[:], row[:, 1, :], 0.5, row[:, 2, :], ALU.mult, ALU.mult))
            s.link(v.tensor_tensor(score[:], prob[:], wide(row[:, 2, :], E), ALU.is_equal))
            s.link(v.tensor_tensor(score[:], score[:], each(k.c("rank"), NT), ALU.mult))
            s.link(v.tensor_reduce(row[:, 3, :], score[:], AX.X, ALU.max))
            v.tensor_tensor(chosen[:].rearrange("p e i -> p i e"), score[:], wide(row[:, 3, :], E), ALU.is_equal).then_inc(chosen_ready, 1)

            count, blocks, blocks_upto, base, offset, ones = (per_e[:, j, :] for j in range(6))
            s.link(v.memset(full[:], 1.0))
            dve.wait_ge(ranked, 1)
            s.link(v.tensor_copy(in_tile[:].rearrange("p e i -> p (e i)"), total_ps[:, 0:P]))
            s.link(v.tensor_tensor_scan(upto[:].rearrange("p e i -> p (e i)"), full[:].rearrange("p e i -> p (e i)"),
                                        in_tile[:].rearrange("p e i -> p (e i)"), 0.0, ALU.mult, ALU.add))
            s.link(v.tensor_reduce(count, in_tile[:], AX.X, ALU.add))
            s.link(v.tensor_tensor(pos[:], wide(count, NT), each(k.c("thresholds"), E), ALU.is_gt))
            s.link(v.tensor_reduce(blocks, pos[:], AX.X, ALU.add))
            s.link(v.tensor_tensor_scan(blocks_upto, full[:, 0, 0:E], blocks, 0.0, ALU.mult, ALU.add))
            s.link(v.tensor_tensor(base, upto[:, :, 0], in_tile[:, :, 0], ALU.subtract))
            s.link(v.tensor_tensor(offset, blocks_upto, blocks, ALU.subtract))
            s.link(v.scalar_tensor_tensor(offset, offset, float(P), base, ALU.mult, ALU.subtract))
            s.link(v.tensor_tensor(pos[:], upto[:], in_tile[:], ALU.subtract))
            s.link(v.tensor_tensor(pos[:], pos[:], rank_ps[:, 0:P].rearrange("p (e i) -> p e i", e=E), ALU.add))
            s.link(v.tensor_tensor(pos[:], pos[:], wide(offset, NT), ALU.add))
            s.link(v.tensor_tensor(pos[:], pos[:], chosen[:], ALU.mult))
            s.link(v.tensor_reduce(slot[:], pos[:].rearrange("p e i -> p i e"), AX.X, ALU.add))
            s.link(v.tensor_copy(slot_i[:, 0, :], slot[:]))
            s.link(v.tensor_scalar(slot_i[:, 1, :], slot_i[:, 0, :], 7, None, ALU.arith_shift_right))
            s.link(v.tensor_scalar(slot_i[:, 2, :], slot_i[:, 0, :], P - 1, None, ALU.bitwise_and))
            s.link(v.tensor_copy(slot_f[:], slot_i[:, 1:3, :]))

            v.tensor_tensor(place[:], each(k.c("lane"), NT), wide(slot_f[:, 1, :], P), ALU.is_equal)
            s.link(v.tensor_tensor(payload[:, :, 0, :], each(k.c("blocks"), NT), wide(slot_f[:, 0, :], NB), ALU.is_equal))
            s.link(v.tensor_scalar(payload[:, :, 1, :], payload[:, :, 0, :], k.c("token"), None, ALU.mult))
            v.tensor_tensor(payload[:, :, 2, :], payload[:, :, 0, :], wide(k.c("tile"), NB), ALU.mult).then_inc(slots_ready, 1)

            s.link(v.tensor_tensor(past[:], wide(k.c("blocks"), E), each(blocks_upto, NB), ALU.is_ge))
            s.link(v.tensor_reduce(block_e[:, 0, :], past[:], AX.X, ALU.add))
            s.link(v.tensor_scalar(block_e[:, 1, :], block_e[:, 0, :], E - 1.0, float(F), ALU.min, ALU.mult))
            s.link(v.tensor_scalar(block_e[:, 2, :], block_e[:, 0, :], E - 1.0, float(C), ALU.min, ALU.mult))
            s.link(v.tensor_copy(expert_offset[:], block_e[:, 1, :]))
            s.link(v.tensor_copy(expert_offset2[:], block_e[:, 2, :]))

            dve.wait_ge(inverted, 1)
            s.link(v.tensor_copy(at_slot[:].rearrange("p a b -> p (a b)"), slot_ps[:, 0:3 * NB]))
            s.link(v.scalar_tensor_tensor(token[:, 0, :], at_slot[:, 2, :], float(P), at_slot[:, 1, :], ALU.mult, ALU.add))
            s.link(v.tensor_copy(gather_index[:], token[:, 0, :]))
            s.link(v.tensor_scalar(at_slot[:, 0, :], at_slot[:, 0, :], -SKIP, SKIP, ALU.mult, ALU.add))
            s.link(v.tensor_tensor(token[:, 1, :], token[:, 0, :], at_slot[:, 0, :], ALU.add))
            s.link(v.tensor_copy(scatter_index[:], token[:, 1, :]))


def experts(k, tag, xn_dram, y_dram, gather_index, scatter_index, expert_offset, expert_offset2):
    nc = k.nc
    with ExitStack() as ctx:
        def sb(name, shape, dt=F32):
            return ctx.enter_context(nc.sbuf_tensor(f"{name}_{tag}", shape, dt))

        def ps(name, shape, dt=F32):
            return ctx.enter_context(nc.psum_tensor(f"{name}_{tag}", shape, dt))

        def sem(name):
            return ctx.enter_context(nc.semaphore(f"{name}_{tag}"))

        rows = sb("rows", [P, NB, C])
        row_in = sb("row_in", [P, C])
        rowT = sb("rowT", [C, P])
        hid = sb("hid", [P, F])
        act_h = sb("act_h", [P, F])
        hT = [sb(f"hT{n}", [P, KF, P]) for n in range(2)]
        y = sb("y", [P, NB, C])
        rowT_ps = ps("rowT_ps", [P, 512])
        hid_ps = [ps(f"hid_ps{n}", [P, F]) for n in range(2)]
        hT_ps = ps("hT_ps", [P, KF, P])
        y_ps = [ps(f"y_ps{n}", [P, 512]) for n in range(2)]

        gathered = [sem(f"gathered{n}") for n in range(2)]
        row_staged, row_turned, rowT_ready = sem("row_staged"), sem("row_turned"), sem("rowT_ready")
        hid_done, hid_biased, silu_done = sem("hid_done"), sem("hid_biased"), sem("silu_done")
        h_turned, hT_ready = sem("h_turned"), sem("hT_ready")
        y_done, y_ready, y_stored = sem("y_done"), sem("y_ready"), sem("y_stored")

        block = ctx.enter_context(nc.Block())
        AHEAD = 6
        TRIPS = (NB - 3) // 2
        assert NB == 3 + 2 * TRIPS

        @block.gpsimd
        def _(pool):
            def gather(b):
                if b >= 2:
                    pool.wait_ge(gathered[b % 2], 16 * (b // 2))
                at = bass.IndirectOffsetOnAxis(ap=gather_index[:, b:b + 1], axis=0)
                nc.gpsimd.indirect_dma_start(rows[:, b, :], None, xn_dram, at).then_inc(gathered[b % 2], 16)

            for b in range(AHEAD):
                gather(b)
            for b in range(NB):
                if b + AHEAD < NB:
                    gather(b + AHEAD)
                pool.wait_ge(y_ready, b + 1)
                at = bass.IndirectOffsetOnAxis(ap=scatter_index[:, b:b + 1], axis=0)
                nc.gpsimd.indirect_dma_start(y_dram, at, y[:, b, :], None, bounds_check=T - 1, oob_is_err=False
                                             ).then_inc(y_stored, 16)
            pool.wait_ge(y_stored, 16 * NB)

        @block.scalar
        def _(act):
            def rows_out(b):
                act.wait_ge(row_turned, b + 1)
                nc.scalar.copy(rowT[:], rowT_ps[:, 0:P]).then_inc(rowT_ready, 1)

            def silu(b, first=False):
                act.wait_ge(hid_biased, b + 1)
                if not first:
                    act.wait_ge(h_turned, b)
                nc.scalar.activation(act_h[:], hid[:], ACT.Silu).then_inc(silu_done, 1)

            rows_out(0)
            rows_out(1)
            silu(0, first=True)
            rows_out(2)
            with act.Fori(1, NB - 2) as b:
                silu(b)
                rows_out(b + 2)
            silu(NB - 2)
            silu(NB - 1)

        @block.tensor
        def _(pe):
            def turn_rows(b):
                pe.wait_ge(row_staged, b + 1)
                nc.tensor.transpose(rowT_ps[:, 0:P], row_in[:], k.c("ident")).then_inc(row_turned, 1)

            def first_layer(b, n):
                e = pe.value_load(expert_offset[0:1, bass.ds(b, 1)], min_val=0, max_val=(E - 1) * F)
                pe.wait_ge(rowT_ready, b + 1)
                nc.tensor.matmul(hid_ps[n][:], rowT[:], k.w1[:, bass.ds(e, F)], start=True, stop=True).then_inc(hid_done, 1)

            def turn_hidden(b, first=False):
                pe.wait_ge(silu_done, b + 1)
                if not first:
                    pe.wait_ge(hT_ready, b)
                for f in range(KF):
                    last = nc.tensor.transpose(hT_ps[:, f, :], act_h[:, f * P:(f + 1) * P], k.c("ident"))
                last.then_inc(h_turned, 1)

            def second_layer(b, n, drained=True):
                e = pe.value_load(expert_offset[0:1, bass.ds(b, 1)], min_val=0, max_val=(E - 1) * F)
                pe.wait_ge(hT_ready, b + 1)
                if drained:
                    pe.wait_ge(y_ready, b - 1)
                for f in range(KF):
                    last = nc.tensor.matmul(y_ps[n][:, 0:C], hT[n][:, f, :], k.w2[:, bass.ds(e + f * P, P)], start=(f == 0), stop=(f == KF - 1))
                last.then_inc(y_done, 1)

            def work(b, n, turn=True, drained=True):
                first_layer(b, n)
                turn_hidden(b - 1)
                second_layer(b - 2, n, drained)
                if turn:
                    turn_rows(b + 1)

            turn_rows(0)
            pe.wait_ge(k.weights_loaded, k.n_weight_loads * 16)
            first_layer(0, 0)
            turn_rows(1)
            first_layer(1, 1)
            turn_hidden(0, first=True)
            turn_rows(2)
            work(2, 0, drained=False)
            work(3, 1, drained=False)
            work(4, 0)
            with pe.Fori(2, TRIPS) as trip:
                work(trip * 2 + 1, 1)
                work(trip * 2 + 2, 0)
            work(NB - 2, 1)
            work(NB - 1, 0, turn=False)
            turn_hidden(NB - 1)
            second_layer(NB - 2, 1)
            second_layer(NB - 1, 0)

        @block.vector
        def _(dve):
            v = nc.vector

            def stage(b, n, first=False):
                dve.wait_ge(gathered[n], (b // 2) * 16 + 16 if isinstance(b, int) else b * 8 + (16 - 8 * n))
                if not first:
                    dve.wait_ge(row_turned, b)
                v.tensor_copy(row_in[:], rows[:, bass.ds(b, 1), :].rearrange("p a c -> p (a c)")).then_inc(row_staged, 1)

            def bias(b, n, first=False):
                e = dve.value_load(expert_offset[0:1, bass.ds(b, 1)], min_val=0, max_val=(E - 1) * F)
                dve.wait_ge(hid_done, b + 1)
                if not first:
                    dve.wait_ge(silu_done, b)
                v.tensor_tensor(hid[:], hid_ps[n][:], k.b1[:, bass.ds(e, F)], ALU.add).then_inc(hid_biased, 1)

            def hidden_out(b, n, first=False):
                dve.wait_ge(h_turned, b + 1)
                if not first:
                    dve.wait_ge(y_done, b - 1)
                v.tensor_copy(hT[n][:], hT_ps[:]).then_inc(hT_ready, 1)

            def y_out(b, n):
                e = dve.value_load(expert_offset2[0:1, bass.ds(b, 1)], min_val=0, max_val=(E - 1) * C)
                dve.wait_ge(y_done, b + 1)
                v.tensor_tensor(y[:, bass.ds(b, 1), :].rearrange("p a c -> p (a c)"), y_ps[n][:, 0:C], k.b2[:, bass.ds(e, C)], ALU.add
                                ).then_inc(y_ready, 1)

            def work(b, n, ahead=True, first=False):
                bias(b, n)
                if ahead:
                    stage(b + 2, n)
                hidden_out(b - 1, 1 - n, first)
                y_out(b - 2, n)

            stage(0, 0, first=True)
            stage(1, 1)
            dve.wait_ge(k.weights_loaded, k.n_weight_loads * 16)
            bias(0, 0, first=True)
            stage(2, 0)
            bias(1, 1)
            stage(3, 1)
            hidden_out(0, 0, first=True)
            work(2, 0, first=True)
            with dve.Fori(1, TRIPS) as trip:
                work(trip * 2 + 1, 1)
                work(trip * 2 + 2, 0)
            work(NB - 2, 1, ahead=False)
            work(NB - 1, 0, ahead=False)
            hidden_out(NB - 1, 0)
            y_out(NB - 2, 1)
            y_out(NB - 1, 0)


def combine(k, tag, y_dram, y, weight, result):
    nc = k.nc
    with ExitStack() as ctx:
        y_loaded = [ctx.enter_context(nc.semaphore(f"y_loaded{g}_{tag}")) for g in range(NT // GB)]
        x_ready = ctx.enter_context(nc.semaphore(f"x_ready_{tag}"))
        x_stored = ctx.enter_context(nc.semaphore(f"x_stored_{tag}"))
        block = ctx.enter_context(nc.Block())
        y_rows = y_dram.rearrange("(i p) c -> p i c", p=P)

        @block.sync
        def _(sp):
            for g in range(NT // GB):
                sp.dma_start(y[:, g * GB:(g + 1) * GB, :], y_rows[:, g * GB:(g + 1) * GB, :]).then_inc(y_loaded[g], 16)
            if result is not None:
                out_rows = result.rearrange("(i p) c -> p i c", p=P)
                for g in range(NT // GB):
                    sp.wait_ge(x_ready, (g + 1) * GB)
                    sp.dma_start(out_rows[:, g * GB:(g + 1) * GB, :], k.x[:, g * GB:(g + 1) * GB, :]).then_inc(x_stored, 16)
                sp.wait_ge(x_stored, 16 * (NT // GB))

        @block.vector
        def _(dve):
            for i in range(NT):
                if i % GB == 0:
                    dve.wait_ge(y_loaded[i // GB], 16)
                nc.vector.scalar_tensor_tensor(k.x[:, i, :], y[:, i, :], weight[:, i:i + 1], k.x[:, i, :], ALU.mult, ALU.add
                                               ).then_inc(x_ready, 1)


def attention(k):
    nc = k.nc
    with ExitStack() as ctx:
        def sb(name, shape, dt=F32):
            return ctx.enter_context(nc.sbuf_tensor(name, shape, dt))

        k.v = sb("v_rows", [P, NT, C])
        k.mixed = sb("mixed", [P, NT, C])
        k.share = sb("share", [P, H, 2])
        k.gk = sb("gk", [H * GR, T], BF16)
        k.gq = sb("gq", [H * GR, H, T], BF16)
        k.parts_dram = nc.dram_tensor("parts_dram", [2, PARTS, C, T], BF16, kind="Internal").ap()
        k.dots = sb("dots", [P, 2, NT, H])
        project(k)
        with ExitStack() as inner:
            k.qt = inner.enter_context(nc.sbuf_tensor("qt", [KS, H, T], BF16))
            k.kt = inner.enter_context(nc.sbuf_tensor("kt", [KS, H, T], BF16))
            k.va = inner.enter_context(nc.sbuf_tensor("va", [P, NT, 2, 32], F32))
            lay_out(k)
            attend(k)
        mix_out(k)


def project(k):
    nc = k.nc
    with ExitStack() as ctx:
        def sb(name, shape, dt=F32):
            return ctx.enter_context(nc.sbuf_tensor(name, shape, dt))

        def ps(name, shape, dt=F32):
            return ctx.enter_context(nc.psum_tensor(name, shape, dt))

        def sem(name):
            return ctx.enter_context(nc.semaphore(name))

        work = sb("work", [P, 2, NT * C])
        wqkv = sb("wqkv", [C, 3 * C])
        gain, shift = sb("gain", [P, C]), sb("ln_shift", [P, C])
        dirs = sb("dirs", [P, H * 3])
        scales = sb("scales", [P, H])
        stat = sb("stat_a", [P, 2, 4, NT])
        xnT = sb("xnT_a", [C, T])
        qk = sb("qk", [P, NT, 2 * C])
        rot = sb("rot", [P, GB, 2 * C])
        parts = sb("parts", [P, PARTS, NT, 2 * C], BF16)
        partsT = sb("partsT", [P, PARTS, T], BF16)
        dot_in = sb("dot_in", [P, 2 * NT, H, 3])

        big = ps("big", [P, 4, 512])
        qkv_ps = [ps(f"qkv_ps{n}", [P, 512]) for n in range(2)]
        turn_ps = [ps(f"turn_ps{n}", [P, 1024], BF16) for n in range(2)]

        xl = work[:, 0, :].rearrange("p (i c) -> p i c", c=C)
        square = work[:, 1, :].rearrange("p (i c) -> p i c", c=C)
        r = work[:].rearrange("p a b -> p (a b)").rearrange("p (i c) -> p i c", c=2 * C)

        loaded = sem("a_loaded")
        var_ready, dev_ready = [sem(f"a_var{n}") for n in range(2)], [sem(f"a_dev{n}") for n in range(2)]
        xn_ready, xn_turned, xnT_ready = sem("a_xn_ready"), sem("a_xn_turned"), sem("a_xnT_ready")
        projected, qkv_out = sem("a_projected"), sem("a_qkv_out")
        roped, part0, rest, part1, part2 = (sem(f"a_{n}") for n in ("roped", "part0", "rest", "part1", "part2"))
        turned = [sem(f"a_turned{n}") for n in range(2)]
        turned_out = [sem(f"a_turned_out{n}") for n in range(2)]
        parts_stored = [sem(f"a_parts_stored{n}") for n in range(PARTS)]
        dve_steps = sem("a_dve_steps")
        kinds = [(a, w) for a in range(PARTS) for w in range(2)]
        NG = NT // GB

        block = ctx.enter_context(nc.Block())

        @block.sync
        def _(sp):
            for dst, src in ((wqkv[:], k.arg["Wqkv_t"]), (gain[:], k.arg["ln_g"].partition_broadcast(P)),
                             (shift[:], k.arg["ln_b"].partition_broadcast(P)),
                             (dirs[:], k.arg["head_dirs"].rearrange("h d -> (h d)").partition_broadcast(P)),
                             (scales[:], k.arg["head_scales"].partition_broadcast(P))):
                sp.dma_start(dst, src).then_inc(loaded, 16)
            for m, (a, w) in enumerate(kinds):
                for n in range(2):
                    sp.wait_ge(turned_out[n], m + 1)
                sp.dma_start(k.parts_dram[w, a], partsT[:, m % PARTS, :]).then_inc(parts_stored[m % PARTS], 16)
            for stored in parts_stored:
                sp.wait_ge(stored, 16 * len(kinds) // PARTS)

        @block.scalar
        def _(act):
            for n in range(2):
                act.wait_ge(var_ready[n], 1)
                nc.scalar.activation(stat[:, n, 2, :], stat[:, n, 2, :], ACT.Sqrt).then_inc(dev_ready[n], 1)
            for g in range(NG):
                act.wait_ge(xn_turned, g + 1)
                nc.scalar.copy(xnT[:, g * 512:(g + 1) * 512], big[:, g, :]).then_inc(xnT_ready, 1)
            for i in range(NT):
                act.wait_ge(projected, i + 1)
                nc.scalar.copy(qk[:, i, :], qkv_ps[i % 2][:, 0:2 * C])
                nc.scalar.copy(k.v[:, i, :], qkv_ps[i % 2][:, 2 * C:3 * C]).then_inc(qkv_out, 1)
            for g in range(NG):
                tiles = slice(g * GB, (g + 1) * GB)
                act.wait_ge(roped, g + 1)
                nc.scalar.copy(parts[:, 0, tiles, :], r[:, tiles, :]).then_inc(part0, 1)
                act.wait_ge(rest, g + 1)
                nc.scalar.copy(parts[:, 1, tiles, :], qk[:, tiles, :]).then_inc(part1, 1)
            for m in range(len(kinds)):
                act.wait_ge(turned[0], m + 1)
                if m >= PARTS:
                    act.wait_ge(parts_stored[m % PARTS], 16 * (m // PARTS))
                nc.scalar.copy(partsT[:, m % PARTS, 0:1024], turn_ps[0][:]).then_inc(turned_out[0], 1)

        @block.tensor
        def _(pe):
            pe.wait_ge(loaded, 80)
            pe.wait_ge(xn_ready, 1)
            for i in range(NT):
                last = nc.tensor.transpose(big[:, i // GB, (i % GB) * P:(i % GB + 1) * P], xl[:, i, :], k.c("ident"))
                if i % GB == GB - 1:
                    last.then_inc(xn_turned, 1)
            for i in range(NT):
                if i % GB == 0:
                    pe.wait_ge(xnT_ready, i // GB + 1)
                if i >= 2:
                    pe.wait_ge(qkv_out, i - 1)
                nc.tensor.matmul(qkv_ps[i % 2][:, 0:3 * C], xnT[:, i * P:(i + 1) * P], wqkv[:], start=True, stop=True).then_inc(projected, 1)
            for m, (a, w) in enumerate(kinds):
                if a == 0 and w == 0:
                    pe.wait_ge(part0, NG)
                if a == 1 and w == 0:
                    pe.wait_ge(part1, NG)
                if a == 2 and w == 0:
                    pe.wait_ge(part2, NG)
                for n in range(2):
                    if m:
                        pe.wait_ge(turned_out[n], m)
                    for i in range(8):
                        last = nc.tensor.transpose(turn_ps[n][:, i * P:(i + 1) * P], parts[:, a, n * 8 + i, w * C:(w + 1) * C], k.cbf("ident"))
                    last.then_inc(turned[n], 1)

        @block.vector
        def _(dve):
            v = nc.vector
            s = Steps(dve, dve_steps)
            s.link(layernorm(nc, dve, s, k.x[:], xl, square, stat[:, 0], var_ready[0], dev_ready[0]))
            s.mark(v.tensor_tensor(k.x[:], k.x[:], xl, ALU.add))
            s.link(layernorm(nc, dve, s, xl, xl, square, stat[:, 1], var_ready[1], dev_ready[1]))
            dve.wait_ge(loaded, 80)
            s.link(v.tensor_tensor(xl, xl, each(gain[:], NT), ALU.mult))
            v.tensor_tensor(xl, xl, each(shift[:], NT), ALU.add).then_inc(xn_ready, 1)
            v.tensor_copy(k.share[:, :, 1], scales[:])
            v.tensor_scalar(k.share[:, :, 0], scales[:], -1.0, 1.0, ALU.mult, ALU.add)

            half = D // 2
            for g in range(NG):
                tiles = slice(g * GB, (g + 1) * GB)
                dve.wait_ge(qkv_out, (g + 1) * GB)

                def heads(ap):
                    return ap.rearrange("p i (h d) -> p i h d", d=D)

                def table(name):
                    t = k.c(name, g * GB * D, (g + 1) * GB * D).rearrange("p (i d) -> p i d", d=D)
                    return t.unsqueeze(2).broadcast_to([P, GB, 2 * H, D])

                src, dst, turn = heads(qk[:, tiles, :]), heads(r[:, tiles, :]), heads(rot[:])
                if g == 0:
                    dve.wait_ge(xnT_ready, NG)
                s.mark(v.tensor_tensor(dst, src, table("cos"), ALU.mult))
                s.mark(v.tensor_tensor(turn[:, :, :, 0:half], src[:, :, :, half:D], table("sin")[:, :, :, 0:half], ALU.mult))
                s.link(v.tensor_tensor(turn[:, :, :, half:D], src[:, :, :, 0:half], table("sin")[:, :, :, half:D], ALU.mult))
                s.link(v.tensor_tensor(r[:, tiles, :], r[:, tiles, :], rot[:], ALU.add))
                d = dirs[:].rearrange("p (h d) -> p h d", d=3).unsqueeze(1).broadcast_to([P, 2 * GB, H, 3])
                rows = r[:, tiles, :].rearrange("p i c -> p (i c)").rearrange("p (w h d) -> p w h d", h=H, d=D)[:, :, :, 0:3]
                s.link(v.tensor_tensor(dot_in[:, 2 * g * GB:2 * (g + 1) * GB], rows, d, ALU.mult))
                v.tensor_scalar(r[:, tiles, C:2 * C], r[:, tiles, C:2 * C], float(D) ** -0.5, None, ALU.mult).then_inc(roped, 1)
            s.link(v.tensor_reduce(k.dots[:].rearrange("p w i h -> p i w h"), dot_in[:].rearrange("p (i w) h d -> p i w h d", w=2), AX.X, ALU.add))
            for g in range(NG):
                tiles = slice(g * GB, (g + 1) * GB)
                dve.wait_ge(part0, g + 1)
                v.tensor_tensor(qk[:, tiles, :], r[:, tiles, :], parts[:, 0, tiles, :], ALU.subtract).then_inc(rest, 1)
                dve.wait_ge(part1, g + 1)
                v.tensor_tensor(parts[:, 2, tiles, :], qk[:, tiles, :], parts[:, 1, tiles, :], ALU.subtract).then_inc(part2, 1)
            for m in range(len(kinds)):
                dve.wait_ge(turned[1], m + 1)
                if m >= PARTS:
                    dve.wait_ge(parts_stored[m % PARTS], 16 * (m // PARTS))
                v.tensor_copy(partsT[:, m % PARTS, 1024:2048], turn_ps[1][:]).then_inc(turned_out[1], 1)


def lay_out(k):
    nc = k.nc
    with ExitStack() as ctx:
        def sb(name, shape, dt=F32):
            return ctx.enter_context(nc.sbuf_tensor(name, shape, dt))

        def ps(name, shape, dt=F32):
            return ctx.enter_context(nc.psum_tensor(name, shape, dt))

        def sem(name):
            return ctx.enter_context(nc.semaphore(name))

        rest = sb("dot_rest", [P, 3, NT * H])
        parts = sb("dot_parts", [P, PARTS, 3, NT * H], BF16)
        largest = sb("geo_max", [P, 3, NT * H])
        kdT = sb("kdT", [H, T])
        least = k.mixed[0:H].rearrange("h i c -> h (i c)")
        free = k.mixed[:].rearrange("p i c -> p (i c)").bitcast(BF16)
        n_row = NT * H * GR
        gka, gqa = (free[:, m * n_row:(m + 1) * n_row].rearrange("p (j g) -> p j g", g=GR) for m in range(2))
        gqT = sb("gqT", [H * GR, T], BF16)
        kd_ps = ps("kd_ps", [H, 4, 512])
        upto_ps = ps("upto_ps", [P, 512])
        turn_ps = [ps(f"g_turn_ps{n}", [P, 1024], BF16) for n in range(2)]

        laid, cleared = sem("laid"), sem("va_cleared")
        kd_turned, kdT_ready, upto_ready, upto_turned = (sem(f"g_{n}") for n in ("kd_turned", "kdT", "upto", "upto_turned"))
        rows_ready, rows_turned, rows_out = sem("g_rows_ready"), sem("g_rows_turned"), sem("g_rows_out")
        dve_steps = sem("g_steps")
        block = ctx.enter_context(nc.Block())
        n = len(PRODUCTS)

        @block.sync
        def _(sp):
            for j, (a, b) in enumerate(PRODUCTS):
                sp.dma_start(k.qt[j * D:(j + 1) * D], k.parts_dram[0, a].rearrange("(h d) t -> d h t", d=D)).then_inc(laid, 16)
                sp.dma_start(k.kt[j * D:(j + 1) * D], k.parts_dram[1, b].rearrange("(h d) t -> d h t", d=D)).then_inc(laid, 16)
            sp.dma_start(k.kt[KQ:KS].rearrange("a h t -> a (h t)"), k.arg["ones_rows"]).then_inc(laid, 16)
            sp.wait_ge(laid, 16 * (2 * n + 1))

        @block.gpsimd
        def _(pool):
            nc.gpsimd.memset(k.va[:], 0.0).then_inc(cleared, 1)
            pool.wait_ge(cleared, 1)
            nc.gpsimd.memset(k.va[:, :, :, D:D + 1], 1.0)
            nc.gpsimd.tensor_copy(k.va[:, :, :, 0:D], k.v[:, :, 0:2 * D].rearrange("p j (h d) -> p j h d", d=D))

        @block.tensor
        def _(pe):
            for i in range(NT):
                last = nc.tensor.transpose(kd_ps[:, i // GB, (i % GB) * P:(i % GB + 1) * P], k.dots[:, 1, i, :], k.c("ident"))
            last.then_inc(kd_turned, 1)
            pe.wait_ge(upto_ready, 1)
            for m, src in enumerate((kdT[:], least)):
                for i in range(NT):
                    o = (m * NT + i) * H
                    last = nc.tensor.transpose(upto_ps[:, o:o + H], src[:, i * P:(i + 1) * P], k.c("ident")[0:H, 0:H])
            last.then_inc(upto_turned, 1)
            pe.wait_ge(rows_ready, 1)
            for m, rows in enumerate((gka, gqa)):
                if m:
                    pe.wait_ge(rows_out, 2)
                for i in range(NT):
                    last = nc.tensor.transpose(turn_ps[i // 8][0:H * GR, (i % 8) * P:(i % 8 + 1) * P],
                                               rows[:, i * H:(i + 1) * H].rearrange("p h g -> p (h g)"), k.cbf("ident"))
                last.then_inc(rows_turned, 1)

        @block.scalar
        def _(act):
            act.wait_ge(kd_turned, 1)
            nc.scalar.copy(kdT[:], kd_ps[:].rearrange("h a b -> h (a b)")).then_inc(kdT_ready, 1)

        @block.vector
        def _(dve):
            v = nc.vector
            s = Steps(dve, dve_steps)
            dve.wait_ge(kdT_ready, 1)
            s.link(v.tensor_tensor_scan(least, kdT[:], kdT[:], 3e38, ALU.min, ALU.min))
            v.tensor_tensor_scan(kdT[:], kdT[:], kdT[:], -3e38, ALU.max, ALU.max).then_inc(upto_ready, 1)
            dve.wait_ge(upto_turned, 1)
            qd = k.dots[:, 0].rearrange("p i h -> p (i h)")
            s.mark(v.tensor_copy(rest[:, 0:2, :], k.dots[:].rearrange("p w i h -> p w (i h)")))
            s.mark(v.tensor_tensor(largest[:, 0, :], upto_ps[:, 0:NT * H], qd, ALU.mult))
            s.link(v.tensor_tensor(largest[:, 1, :], upto_ps[:, NT * H:2 * NT * H], qd, ALU.mult))
            s.link(v.tensor_tensor(largest[:, 2, :], largest[:, 0, :], largest[:, 1, :], ALU.max))
            s.link(v.tensor_scalar(rest[:, 2, :], largest[:, 2, :], -1.0, None, ALU.mult))
            s.link(v.tensor_copy(parts[:, 0], rest[:]))
            s.link(v.tensor_tensor(rest[:], rest[:], parts[:, 0], ALU.subtract))
            s.link(v.tensor_copy(parts[:, 1], rest[:]))
            s.mark(v.tensor_tensor(parts[:, 2], rest[:], parts[:, 1], ALU.subtract))
            s.link(v.memset(gka, 1.0))
            for a in range(PARTS):
                s.mark(v.tensor_copy(gka[:, :, a * PARTS:(a + 1) * PARTS], wide(parts[:, a, 1, :], PARTS)))
                s.mark(v.tensor_copy(gqa[:, :, a:PARTS * PARTS:PARTS], wide(parts[:, a, 0, :], PARTS)))
                last = v.tensor_copy(gqa[:, :, PARTS * PARTS + a], parts[:, a, 2, :])
                s.mark(last) if a < PARTS - 1 else last.then_inc(rows_ready, 1)
            dve.wait_ge(rows_turned, 1)
            for m in range(2):
                v.tensor_copy(k.gk[:, m * 1024:(m + 1) * 1024], turn_ps[m][0:H * GR, :]).then_inc(rows_out, 1)
            dve.wait_ge(rows_turned, 2)
            for m in range(2):
                s.link(v.tensor_copy(gqT[:, m * 1024:(m + 1) * 1024], turn_ps[m][0:H * GR, :]))
            for h in range(H):
                v.tensor_scalar(k.gq[:, h, :], gqT[:], k.c("head_rows", h, h + 1)[0:H * GR], None, ALU.mult)


STEPS = [(c, j) for c in range(NCH) for j in range(4 * c + 4)]
NSTEP = len(STEPS)
LAST = [4 * (c + 1) * (c + 2) // 2 - 1 for c in range(NCH)]


def unit_items(pair, c):
    return [("scores", pair, c, hd, i, w) for hd in range(2) for i in range(4) for w in range(c + 1)]


def plan(units):
    items, waiting = [], None
    for pair, c in units:
        own = unit_items(pair, c)
        own[-1] = own[-1] + ("ends",)
        for n, item in enumerate(own):
            items.append(item)
            if n == 1 and waiting:
                items.append(waiting)
        waiting = ("turn", pair, c)
    return items + [waiting]


def attend(k):
    nc = k.nc
    with ExitStack() as ctx:
        def sb(name, shape, dt=F32):
            return ctx.enter_context(nc.sbuf_tensor(name, shape, dt))

        def ps(name, shape, dt=F32):
            return ctx.enter_context(nc.psum_tensor(name, shape, dt))

        def sem(name):
            return ctx.enter_context(nc.semaphore(name))

        prob = sb("prob_a", [P, 4, 2, CH])
        part_max = sb("part_max", [P, 2, 8, NCH])
        shift = sb("shift", [P, 8])
        shift_parts = sb("shift_parts", [P, 2, PARTS, 4], BF16)
        shiftT = sb("shiftT", [2 * PARTS * 4, 2, P], BF16)
        acc = sb("acc_rows", [P, CH])
        inv = sb("inv", [P, 4, 4])
        scaled = sb("scaled", [P, 4, 4, D])
        score_ps = ps("score_ps", [P, 2, 2, CH])
        acc_ps = [ps(f"acc_ps{n}", [P, CH]) for n in range(2)]
        max_ps = [ps(f"max_ps{n}", [P, CH]) for n in range(2)]

        scores_ready, exp_done = sem("scores_ready"), sem("exp_done")
        pv_done, acc_out, acc_turned, acc_free = (sem(n) for n in ("pv_done", "acc_out", "acc_turned", "acc_free"))
        va_ready = sem("va_ready")
        item_ready, item_out = sem("item_ready"), sem("item_out")
        parts_ready, shift_stored = sem("shift_parts_ready"), sem("shift_stored")
        dve_steps = sem("attend_steps")

        first = plan([(0, 0), (0, 1)])
        per_pair = plan([(0, 2), (0, 3), (1, 0), (1, 1)])
        last_pair = plan([(0, 2), (0, 3)])
        assert len(per_pair) % 2 == 0 and len(first) % 2 == 0
        quota = [3] * 20 + [2] * 20

        def split(items):
            out, at = [], 0
            for q in quota:
                out.append(items[at:at + q])
                at += q
            assert at >= len(items)
            return out

        def offset(c, j):
            return max(0, j - 4 * c) * P

        GROUPS = {(0, 0): 1, (2, 8): 2, (3, 12): 3}
        CREDIT = 2
        STORED = 16 * 2 * PARTS
        order = first + per_pair * (NPAIR - 1) + last_pair
        turned_at = [n + 1 for n, item in enumerate(order) if item[0] == "turn"]
        block = ctx.enter_context(nc.Block())

        @block.tensor
        def _(pe):
            def scores(pair, st, hd, slots_used=True):
                c, j = STEPS[st]
                off = offset(c, j)
                if j == 0 and hd == 0:
                    pe.wait_ge(shift_stored, (pair * 4 + c + 1) * STORED)
                if slots_used:
                    pe.wait_ge(exp_done, pair * (2 * NSTEP) + (2 * st + hd - 1))
                h = pair * 2 + hd
                q = slice(c * CH + off, (c + 1) * CH)
                diagonal = j >= 4 * c
                nc.tensor.matmul(score_ps[:, hd, 0, off:], k.kt[:, bass.ds(h, 1), j * P:(j + 1) * P].rearrange("k a t -> k (a t)"),
                                 k.qt[:, bass.ds(h, 1), q].rearrange("k a t -> k (a t)"), start=True, stop=not diagonal)
                last = nc.tensor.matmul(score_ps[:, hd, 1, off:], k.gk[:, j * P:(j + 1) * P],
                                        k.gq[:, bass.ds(h, 1), q].rearrange("k a t -> k (a t)"), start=True, stop=not diagonal)
                if diagonal:
                    for kind in range(2):
                        last = nc.tensor.matmul(score_ps[:, hd, kind, off:off + P], k.cbf("ident"), k.cbf("future_t"), start=False, stop=True)
                last.then_inc(scores_ready, 1)

            def run_items(items, pair, count, unit):
                for n, item in enumerate(items):
                    m = max_ps[(n + parity[0]) % 2]
                    if primed[0] >= 2:
                        pe.wait_ge(item_out, count + n - 1)
                    primed[0] += 1
                    if item[0] == "scores":
                        _, dp, c, hd, i, w = item[:6]
                        h = (pair + dp) * 2 + hd
                        width = CH if w < c else (i + 1) * P
                        q0 = c * CH + i * P
                        last = nc.tensor.matmul(m[:, 0:width], k.qt[0:KQ, bass.ds(h, 1), q0:q0 + P].rearrange("k a t -> k (a t)"),
                                                k.kt[0:KQ, bass.ds(h, 1), w * CH:w * CH + width].rearrange("k a t -> k (a t)"), start=True, stop=w < c)
                        if w == c:
                            last = nc.tensor.matmul(m[:, i * P:(i + 1) * P], k.cbf("ident"), k.cbf("future"), start=False, stop=True)
                        last.then_inc(item_ready, 1)
                    else:
                        pe.wait_ge(parts_ready, unit + 1)
                        unit = unit + 1
                        nc.tensor.transpose(m[:].bitcast(BF16)[0:24, 0:P], shift_parts[:].rearrange("p a b c -> p (a b c)"), k.cbf("ident")
                                            ).then_inc(item_ready, 1)
                parity[0] += len(items)
                return unit

            def values(pair, st):
                c, j = STEPS[st]
                off = offset(c, j)
                if (c, j) in GROUPS:
                    pe.wait_ge(va_ready, pair * 3 + GROUPS[c, j])
                if j == 0:
                    pe.wait_ge(acc_free, pair * 4 + c + 1)
                pe.wait_ge(exp_done, pair * (2 * NSTEP) + 2 * (st + 1))
                for hd in range(2):
                    for kind in range(2):
                        o = 32 * (2 * hd + kind)
                        last = nc.tensor.matmul(acc_ps[c % 2][o:o + 32, off:], k.va[:, j, hd, :], prob[:, (st % 2) * 2 + hd, kind, off:],
                                                start=(j == 0), stop=(j == 4 * c + 3))
                last.then_inc(pv_done, 1)

            def turn_acc(pair, c):
                pe.wait_ge(acc_out, pair * 4 + c + 1)
                for t in range(4):
                    last = nc.tensor.transpose(acc_ps[c % 2][:, t * P:(t + 1) * P], acc[:, t * P:(t + 1) * P], k.c("ident"))
                last.then_inc(acc_turned, 1)

            def body(pair, items, more):
                count = pair * len(per_pair) + len(first)
                unit = pair * 4 + 2
                done = 0
                for st in range(NSTEP):
                    for hd in range(2):
                        if st + 1 < NSTEP:
                            scores(pair, st + 1, hd)
                        elif more:
                            scores(pair + 1, 0, hd)
                        unit = run_items(items[st][hd:hd + 1], pair, count + done, unit)
                        done += len(items[st][hd:hd + 1])
                    values(pair, st)
                    unit = run_items(items[st][2:], pair, count + done, unit)
                    done += len(items[st][2:])
                    for c in range(NCH - 1):
                        if st == LAST[c] + 2:
                            turn_acc(pair, c)
                turn_acc(pair, NCH - 1)

            parity, primed = [0], [0]
            run_items(first, 0, 0, 0)
            for hd in range(2):
                scores(0, 0, hd, slots_used=False)
            with pe.Fori(0, NPAIR - 1) as pair:
                body(pair, split(per_pair), True)
            body(NPAIR - 1, split(last_pair), False)

        @block.scalar
        def _(act):
            def body(pair):
                for st, (c, j) in enumerate(STEPS):
                    off = offset(c, j)
                    act.wait_ge(pv_done, pair * NSTEP + st - 1 + CREDIT)
                    for hd in range(2):
                        act.wait_ge(scores_ready, pair * (2 * NSTEP) + 2 * st + hd + 1)
                        nc.scalar.activation(prob[:, (st % 2) * 2 + hd, :, off:], score_ps[:, hd, :, off:], ACT.Exp).then_inc(exp_done, 1)

            with act.Fori(0, NPAIR) as pair:
                body(pair)

        @block.gpsimd
        def _(pool):
            def values_in(pair, j0, j1):
                nc.gpsimd.tensor_copy(k.va[:, j0:j1, :, 0:D], k.v[:, j0:j1, bass.ds((pair + 1) * 2 * D, 2 * D)].rearrange("p j (h d) -> p j h d", d=D)
                                      ).then_inc(va_ready, 1)

            pool.sem_inc(pv_done, CREDIT)
            pool.sem_inc(va_ready, 3)
            with pool.Fori(0, NPAIR - 1) as pair:
                for j0, j1 in ((0, 8), (8, 12), (12, 16)):
                    pool.wait_ge(pv_done, pair * NSTEP + NSTEP - NT + j1 + CREDIT)
                    values_in(pair, j0, j1)

        @block.sync
        def _(sp):
            for u in range(4 * NPAIR):
                pair, c = u // 4, u % 4
                sp.wait_ge(item_out, turned_at[u])
                for hd in range(2):
                    for a in range(PARTS):
                        r0 = (hd * PARTS + a) * 4
                        sp.dma_start(k.qt[KQ + a:KQ + a + 1, 2 * pair + hd, c * CH:(c + 1) * CH], shiftT[r0:r0 + 4, u % 2, :]).then_inc(shift_stored, 16)
                sp.wait_ge(shift_stored, STORED * (u + 1))

        @block.vector
        def _(dve):
            v = nc.vector
            s = Steps(dve, dve_steps)

            def finish_unit(c):
                s.link(v.tensor_reduce(shift[:], part_max[:, c % 2, :, 0:c + 1], AX.X, ALU.max, negate=True))
                rows = shift[:].rearrange("p (h i) -> p h i", i=4)
                s.link(v.tensor_copy(shift_parts[:, :, 0, :], rows))
                s.link(v.tensor_tensor(rows, rows, shift_parts[:, :, 0, :], ALU.subtract))
                s.link(v.tensor_copy(shift_parts[:, :, 1, :], rows))
                v.tensor_tensor(shift_parts[:, :, 2, :], rows, shift_parts[:, :, 1, :], ALU.subtract).then_inc(parts_ready, 1)

            def run_items(items, count, unit):
                for n, item in enumerate(items):
                    m = max_ps[(n + parity[0]) % 2]
                    dve.wait_ge(item_ready, count + n + 1)
                    if item[0] == "scores":
                        _, _, c, hd, i, w = item[:6]
                        width = CH if w < c else (i + 1) * P
                        v.tensor_reduce(part_max[:, c % 2, hd * 4 + i, w:w + 1], m[:, 0:width], AX.X, ALU.max).then_inc(item_out, 1)
                        if item[-1] == "ends":
                            dve.wait_ge(item_out, count + n + 1)
                            finish_unit(c)
                    else:
                        c = item[2]
                        if stored[0]:
                            dve.wait_ge(shift_stored, (unit - 1) * STORED)
                        v.tensor_copy(shiftT[:, c % 2, :], m[:].bitcast(BF16)[0:24, 0:P]).then_inc(item_out, 1)
                        unit = unit + 1
                parity[0] += len(items)
                return unit

            def acc_to_rows(pair, st):
                c = STEPS[st][0]
                dve.wait_ge(pv_done, pair * NSTEP + st + 1 + CREDIT)
                v.tensor_copy(acc[:], acc_ps[c % 2][:]).then_inc(acc_out, 1)

            def mix(pair, c):
                dve.wait_ge(acc_turned, pair * 4 + c + 1)
                sums = acc_ps[c % 2][:].rearrange("p (t q r) -> p t q r", q=4, r=32)
                s.link(v.reciprocal(inv[:], sums[:, :, :, D]))
                share = k.share[:, bass.ds(pair * 2, 2), :].rearrange("p h k -> p (h k)")
                s.link(v.tensor_tensor(inv[:], inv[:], each(share, 4), ALU.mult))
                v.tensor_tensor(scaled[:], sums[:, :, :, 0:D], inv[:].unsqueeze(3).broadcast_to([P, 4, 4, D]), ALU.mult).then_inc(acc_free, 1)
                dve.wait_ge(acc_free, pair * 4 + c + 1 + 2)
                kinds = scaled[:].rearrange("p t (h k) d -> p t h k d", k=2)
                out = k.mixed[:, 4 * c:4 * c + 4, bass.ds(pair * 2 * D, 2 * D)].rearrange("p t (h d) -> p t h d", d=D)
                s.mark(v.tensor_tensor(out, kinds[:, :, :, 0, :], kinds[:, :, :, 1, :], ALU.add))

            def body(pair, items):
                count = pair * len(per_pair) + len(first)
                unit = pair * 4 + 2
                done = 0
                for st in range(NSTEP):
                    for c in range(NCH - 1):
                        if st == LAST[c] + 3:
                            mix(pair, c)
                    unit = run_items(items[st][:2], count + done, unit)
                    done += len(items[st][:2])
                    if st in LAST:
                        acc_to_rows(pair, st)
                    unit = run_items(items[st][2:], count + done, unit)
                    done += len(items[st][2:])
                mix(pair, NCH - 1)

            parity, stored = [0], [False]
            dve.sem_inc(acc_free, 2)
            run_items(first, 0, 0)
            stored[0] = True
            with dve.Fori(0, NPAIR - 1) as pair:
                s.enter(pair, 4 * 4 + 4 * 3)
                body(pair, split(per_pair))
                s.leave(NPAIR - 1)
            body(NPAIR - 1, split(last_pair))


def mix_out(k):
    nc = k.nc
    with ExitStack() as ctx:
        def sem(name):
            return ctx.enter_context(nc.semaphore(name))

        wo = ctx.enter_context(nc.sbuf_tensor("wo", [C, C], F32))
        mixedT = ctx.enter_context(nc.sbuf_tensor("mixedT", [C, T], F32))
        turn_ps = [ctx.enter_context(nc.psum_tensor(f"o_turn_ps{n}", [P, 512], F32)) for n in range(2)]
        out_ps = [ctx.enter_context(nc.psum_tensor(f"o_out_ps{n}", [P, 512], F32)) for n in range(2)]
        wo_loaded, turned, mixedT_ready, multiplied, added = (sem(f"o_{n}") for n in ("loaded", "turned", "ready", "multiplied", "added"))
        block = ctx.enter_context(nc.Block())

        @block.sync
        def _(sp):
            sp.dma_start(wo[:], k.arg["Wo_t"]).then_inc(wo_loaded, 16)

        @block.tensor
        def _(pe):
            def multiply(g):
                pe.wait_ge(mixedT_ready, g + 1)
                if g >= 2:
                    pe.wait_ge(added, g - 1)
                for i in range(GB):
                    t = g * GB + i
                    last = nc.tensor.matmul(out_ps[g % 2][:, i * P:(i + 1) * P], mixedT[:, t * P:(t + 1) * P], wo[:], start=True, stop=True)
                last.then_inc(multiplied, 1)

            pe.wait_ge(wo_loaded, 16)
            for g in range(NT // GB):
                if g >= 2:
                    pe.wait_ge(mixedT_ready, g - 1)
                for i in range(GB):
                    last = nc.tensor.transpose(turn_ps[g % 2][:, i * P:(i + 1) * P], k.mixed[:, g * GB + i, :], k.c("ident"))
                last.then_inc(turned, 1)
                if g:
                    multiply(g - 1)
            multiply(NT // GB - 1)

        @block.scalar
        def _(act):
            for g in range(NT // GB):
                act.wait_ge(turned, g + 1)
                nc.scalar.copy(mixedT[:, g * 512:(g + 1) * 512], turn_ps[g % 2][:]).then_inc(mixedT_ready, 1)

        @block.vector
        def _(dve):
            for g in range(NT // GB):
                dve.wait_ge(multiplied, g + 1)
                rows = k.x[:, g * GB:(g + 1) * GB, :].rearrange("p i c -> p (i c)")
                nc.vector.tensor_tensor(rows, rows, out_ps[g % 2][:], ALU.add).then_inc(added, 1)


def program(nc, a, out):
    with ExitStack() as ctx:
        k = Kernel(nc, ctx, a)

        k.weights_loaded = ctx.enter_context(nc.semaphore("weights_loaded"))
        x_and_tables = [
            (k.x[:], a["x"].rearrange("(i p) c -> p i c", p=P)),
            (k.cf[:], a["constants"]),
            (k.wg[:], a["Wg"]),
            (k.bg[:], a["bg"].partition_broadcast(P)),
            (k.cb[:], a["constants_bf16"]),
        ]
        weights = [
            (k.w1[:, e * F:(e + 1) * F], a["W1"][e]) for e in range(E)
        ] + [
            (k.b1[:], a["b1"].rearrange("e f -> (e f)").partition_broadcast(P)),
            (k.b2[:], a["b2"].rearrange("e c -> (e c)").partition_broadcast(P)),
        ] + [
            (k.w2[:, e * F:(e + 1) * F].rearrange("p (f c) -> p f c", f=KF), a["W2"][e].rearrange("(f p) c -> p f c", p=P))
            for e in range(E)
        ]
        k.n_weight_loads = len(weights)
        assert len(x_and_tables) == N_FIRST_LOADS

        def load_all(sp, loaded):
            for dst, src in x_and_tables:
                sp.dma_start(dst, src).then_inc(loaded, 16)
            for dst, src in weights:
                sp.dma_start(dst, src).then_inc(k.weights_loaded, 16)

        ffn(k, "first", load_all, None)
        attention(k)
        ffn(k, "second", None, out)


def kernel(**inputs):
    import ml_dtypes
    import concourse.bacc as bacc
    from concourse.bass_utils import run_bass_kernel_spmd

    g = {n: np.ascontiguousarray(v) for n, v in inputs.items()}
    bf16 = ml_dtypes.bfloat16
    laid = {
        "x": g["L0_attn_x"].reshape(T, C),
        "Wqkv_t": np.ascontiguousarray(np.concatenate([g["L0_attn_Wq"].T, g["L0_attn_Wk"].T, g["L0_attn_Wv"].T], 1)),
        "Wo_t": np.ascontiguousarray(g["L0_attn_Wo"].T),
        "ln_g": g["L0_attn_ln_g"],
        "ln_b": g["L0_attn_ln_b"],
        "head_scales": g["L0_attn_head_scales"],
        "head_dirs": g["L0_attn_head_dirs"],
        "Wg": g["L0_ffn_Wg"],
        "bg": g["L0_ffn_bg"],
        "W1": g["L0_ffn_W1"],
        "b1": g["L0_ffn_b1"],
        "W2": g["L0_ffn_W2"],
        "b2": g["L0_ffn_b2"],
        "constants": float_constants(),
        "constants_bf16": bf16_constants(bf16),
        "ones_rows": np.ones((PARTS, H * T), bf16),
    }
    nc = bacc.Bacc("TRN2", target_bir_lowering=False, num_devices=1)
    a = {n: nc.dram_tensor(f"in_{n}", v.shape, mybir.dt.from_np(v.dtype), kind="ExternalInput").ap() for n, v in laid.items()}
    out = nc.dram_tensor("out_x", (T, C), F32, kind="ExternalOutput").ap()
    program(nc, a, out)
    r = run_bass_kernel_spmd(nc, [{f"in_{n}": v for n, v in laid.items()}], core_ids=[0])
    return r.results[0]["out_x"].reshape(1, T, C)
```

```python
from contextlib import ExitStack

import numpy as np

import concourse.bass as bass
from concourse import mybir
from concourse.alu_op_type import AluOpType as ALU

ACT = mybir.ActivationFunctionType
AX = mybir.AxisListType
F32 = mybir.dt.float32
BF16 = mybir.dt.bfloat16
I32 = mybir.dt.int32

P = 128
T = 2048
NT = T // P
C = 128
H = 8
D = C // H
E = 8
F = 512
KF = F // P
NB = (T + E * (P - 1)) // P
GB = 4
EPS = 1e-5
N_FIRST_LOADS = 5
NEG = -1e38
SKIP = 4096.0

CH = 512
NCH = T // CH
NPAIR = H // 2
PARTS = 3
PRODUCTS = [(0, 0), (0, 1), (0, 2), (1, 0), (1, 1), (2, 0)]
KQ = len(PRODUCTS) * D
KS = KQ + PARTS
GR = PARTS * PARTS + PARTS


class Columns:

    def __init__(self, **widths):
        self.at, self.width = {}, 0
        for name, w in widths.items():
            self.at[name] = (self.width, w)
            self.width += w


FC = Columns(ident=P, lane=P, blocks=NB, thresholds=NT, rank=E, token=1, tile=NT, head_rows=H,
             cos=NT * D, sin=NT * D)
BC = Columns(ident=P, before=P, ones=P, future=P, future_t=P)


def float_constants():
    t = np.zeros((P, FC.width), np.float32)

    def put(name, a):
        o, w = FC.at[name]
        t[:, o:o + w] = a

    p = np.arange(P, dtype=np.float32)[:, None]
    put("ident", np.eye(P))
    put("lane", np.arange(P)[None])
    put("blocks", np.arange(NB)[None])
    put("thresholds", P * np.arange(NT)[None])
    put("rank", E - np.arange(E)[None])
    put("token", p)
    put("tile", np.arange(NT)[None])
    put("head_rows", (np.arange(P)[:, None] // GR) == np.arange(H)[None])
    inverse = np.float32(1.0) / np.float32(10000.0) ** (np.arange(0, D, 2, dtype=np.float32) / np.float32(D))
    angle = np.arange(T, dtype=np.float32)[:, None] * inverse[None].astype(np.float32)
    cos = np.concatenate([np.cos(angle)] * 2, 1).astype(np.float32)
    sin = np.concatenate([-np.sin(angle), np.sin(angle)], 1).astype(np.float32)
    put("cos", cos.reshape(NT, P, D).transpose(1, 0, 2).reshape(P, NT * D))
    put("sin", sin.reshape(NT, P, D).transpose(1, 0, 2).reshape(P, NT * D))
    return t


def bf16_constants(bf16):
    t = np.zeros((P, BC.width), np.float32)
    q = np.arange(P)[:, None]
    k = np.arange(P)[None]
    for name, a in (("ident", q == k), ("before", q < k), ("ones", np.ones((P, P))),
                    ("future", np.where(k > q, NEG, 0.0)), ("future_t", np.where(q > k, NEG, 0.0))):
        o, w = BC.at[name]
        t[:, o:o + w] = a
    return t.astype(bf16)


class Steps:

    def __init__(self, engine, sem):
        self.engine, self.sem, self.n, self.trip, self.per = engine, sem, 0, None, 0

    def value(self):
        return self.n if self.trip is None else self.trip * self.per + self.n

    def mark(self, instruction):
        instruction.then_inc(self.sem, 1)
        self.n += 1

    def link(self, instruction):
        self.mark(instruction)
        self.engine.wait_ge(self.sem, self.value())

    def enter(self, trip, per):
        self.trip, self.per, self.start = trip, per, self.n

    def leave(self, trips):
        assert self.n - self.start == self.per, (self.n - self.start, self.per)
        self.n, self.trip = self.start + self.per * trips, None


class Kernel:

    def __init__(self, nc, ctx, arg):
        self.nc, self.arg = nc, arg

        def sb(name, shape, dt=F32):
            return ctx.enter_context(nc.sbuf_tensor(name, shape, dt))

        self.x = sb("x_res", [P, NT, C])
        self.w1 = sb("w1", [P, E * F])
        self.w2 = sb("w2", [P, E * F])
        self.b1 = sb("b1", [P, E * F])
        self.b2 = sb("b2", [P, E * C])
        self.wg = sb("wg", [C, E])
        self.bg = sb("bg", [P, E])
        self.cf = sb("cf", [P, FC.width])
        self.cb = sb("cb", [P, BC.width], BF16)

    def c(self, name, a=0, b=None):
        o, w = FC.at[name]
        return self.cf[:, o + a:o + (w if b is None else b)]

    def cbf(self, name):
        o, w = BC.at[name]
        return self.cb[:, o:o + w]


def wide(ap, n):
    return ap.unsqueeze(2).broadcast_to([ap.shape[0], ap.shape[1], n])


def each(ap, n):
    return ap.unsqueeze(1).broadcast_to([ap.shape[0], n, ap.shape[1]])


def layernorm(nc, steps, src, dst, halves, stat, variance_ready, deviation_ready, ready):
    v = nc.vector
    for i in range(NT):
        v.bn_stats(halves[:, i, :], src[:, i, :]).then_inc(steps.sem, 1)
    steps.n += NT
    steps.engine.wait_ge(steps.sem, steps.n)
    for i in range(NT):
        v.bn_aggr(stat[:, i, :], halves[:, i, :]).then_inc(steps.sem, 1)
    steps.n += NT
    steps.engine.wait_ge(steps.sem, steps.n)
    v.tensor_scalar(stat[:, :, 1], stat[:, :, 1], EPS, None, ALU.add).then_inc(variance_ready, 1)
    steps.engine.wait_ge(deviation_ready, 1)
    steps.link(v.reciprocal(stat[:, :, 1], stat[:, :, 1]))
    for i in range(NT):
        v.tensor_scalar(dst[:, i, :], src[:, i, :], stat[:, i, 0:1], stat[:, i, 1:2], ALU.subtract, ALU.mult).then_inc(ready, 1)


def ffn(k, tag, load, result):
    nc = k.nc
    with ExitStack() as ctx:
        def sb(name, shape, dt=F32):
            return ctx.enter_context(nc.sbuf_tensor(f"{name}_{tag}", shape, dt))

        def sem(name):
            return ctx.enter_context(nc.semaphore(f"{name}_{tag}"))

        xn = sb("xn", [P, NT, C])
        stat = sb("stat", [P, NT, 2])
        halves = sb("halves", [P, NT, 6])
        weight = sb("weight", [P, NT])
        gather_index = sb("gather_index", [P, NB], I32)
        scatter_index = sb("scatter_index", [P, NB], I32)
        expert_digits = sb("expert_digits", [P, (NB + 1) // 4], I32)
        xn_dram = nc.dram_tensor(f"xn_dram_{tag}", [T, C], F32, kind="Internal").ap()
        y_dram = nc.dram_tensor(f"y_dram_{tag}", [T, C], F32, kind="Internal").ap()
        route(k, tag, load, xn, halves, stat, weight, gather_index, scatter_index, expert_digits, xn_dram)
        experts(k, tag, xn_dram, y_dram, gather_index, scatter_index, expert_digits)
        combine(k, tag, y_dram, xn, weight, result)


def route(k, tag, load, xn, halves, stat, weight, gather_index, scatter_index, expert_digits, xn_dram):
    nc = k.nc
    with ExitStack() as ctx:
        def sb(name, shape, dt=F32):
            return ctx.enter_context(nc.sbuf_tensor(f"{name}_{tag}", shape, dt))

        def ps(name, shape, dt=F32):
            return ctx.enter_context(nc.psum_tensor(f"{name}_{tag}", shape, dt))

        def sem(name):
            return ctx.enter_context(nc.semaphore(f"{name}_{tag}"))

        xnT = sb("xnT", [C, T])
        logits = sb("logits", [P, NT, E])
        prob = sb("prob", [P, NT, E])
        score = sb("score", [P, NT, E])
        row = sb("row", [P, 4, NT])
        chosen = sb("chosen", [P, E, NT], BF16)
        in_tile = sb("in_tile", [P, E, NT])
        upto = sb("upto", [P, E, NT])
        full = sb("full", [P, E, NT])
        per_e = sb("per_e", [P, 6, E])
        pos = sb("pos", [P, E, NT])
        slot = sb("slot", [P, NT])
        slot_i = sb("slot_i", [P, 3, NT], I32)
        slot_f = sb("slot_f", [P, 2, NT])
        place = sb("place", [P, NT, P], BF16)
        payload = sb("payload", [P, NT, 3, NB], BF16)
        at_slot = sb("at_slot", [P, 3, NB])
        token = sb("token", [P, 2, NB])
        past = sb("past", [P, NB, E])
        block_e = sb("block_e", [P, NB + 3])
        pairs = sb("pairs", [P, (NB + 3) // 2])
        sixes = sb("sixes", [P, (NB + 1) // 4])
        xnT_ps = ps("xnT_ps", [P, 4, 512])
        gate_ps = ps("gate_ps", [P, 512])
        rank_ps = ps("rank_ps", [P, 512])
        total_ps = ps("total_ps", [P, 512])
        slot_ps = ps("slot_ps", [P, 512])

        loaded = sem("loaded")
        var_ready, dev_ready = sem("var_ready"), sem("dev_ready")
        xn_ready = sem("xn_ready")
        xn_stored = sem("xn_stored")
        transposed = sem("transposed")
        xnT_ready = sem("xnT_ready")
        gated = sem("gated")
        exp_in, exp_done = sem("exp_in"), sem("exp_done")
        chosen_ready = sem("chosen_ready")
        ranked = sem("ranked")
        slots_ready = sem("slots_ready")
        inverted = sem("inverted")
        dve_steps = sem("dve_steps")

        block = ctx.enter_context(nc.Block())

        @block.sync
        def _(sp):
            if load:
                load(sp, loaded)
            sp.wait_ge(xn_ready, NT)
            sp.dma_start(xn_dram.rearrange("(i p) c -> p i c", p=P), xn[:]).then_inc(xn_stored, 16)
            sp.wait_ge(xn_stored, 16)

        @block.scalar
        def _(act):
            act.wait_ge(var_ready, 1)
            nc.scalar.activation(stat[:, :, 1], stat[:, :, 1], ACT.Sqrt).then_inc(dev_ready, 1)
            for g in range(NT // GB):
                act.wait_ge(transposed, g + 1)
                nc.scalar.copy(xnT[:, g * 512:(g + 1) * 512], xnT_ps[:, g, :]).then_inc(xnT_ready, 1)
            act.wait_ge(exp_in, 1)
            nc.scalar.activation(prob[:], logits[:], ACT.Exp).then_inc(exp_done, 1)

        @block.tensor
        def _(pe):
            for i in range(NT):
                if i % GB == 0:
                    pe.wait_ge(xn_ready, i + GB)
                last = nc.tensor.transpose(xnT_ps[:, i // GB, (i % GB) * P:(i % GB + 1) * P], xn[:, i, :], k.c("ident"))
                if i % GB == GB - 1:
                    last.then_inc(transposed, 1)
            for i in range(NT):
                if i % GB == 0:
                    pe.wait_ge(xnT_ready, i // GB + 1)
                last = nc.tensor.matmul(gate_ps[:, i * E:(i + 1) * E], xnT[:, i * P:(i + 1) * P], k.wg[:], start=True, stop=True)
            last.then_inc(gated, 1)
            pe.wait_ge(chosen_ready, 1)
            flat = chosen[:].rearrange("p e i -> p (e i)")
            nc.tensor.matmul(rank_ps[:, 0:P], k.cbf("before"), flat, start=True, stop=True)
            nc.tensor.matmul(total_ps[:, 0:P], k.cbf("ones"), flat, start=True, stop=True).then_inc(ranked, 1)
            pe.wait_ge(slots_ready, 1)
            for i in range(NT):
                last = nc.tensor.matmul(slot_ps[:, 0:3 * NB], place[:, i, :], payload[:, i].rearrange("p a b -> p (a b)"),
                                        start=(i == 0), stop=(i == NT - 1))
            last.then_inc(inverted, 1)

        @block.vector
        def _(dve):
            v = nc.vector
            s = Steps(dve, dve_steps)
            if load:
                dve.wait_ge(loaded, 16 * N_FIRST_LOADS)
            layernorm(nc, s, k.x, xn, halves, stat, var_ready, dev_ready, xn_ready)

            dve.wait_ge(gated, 1)
            s.link(v.tensor_tensor(logits[:], gate_ps[:, 0:NT * E].rearrange("p (i e) -> p i e", e=E), each(k.bg[:], NT), ALU.add))
            s.link(v.tensor_reduce(row[:, 0, :], logits[:], AX.X, ALU.max))
            v.tensor_tensor(logits[:], logits[:], wide(row[:, 0, :], E), ALU.subtract).then_inc(exp_in, 1)
            dve.wait_ge(exp_done, 1)
            s.link(v.tensor_reduce(row[:, 1, :], prob[:], AX.X, ALU.add))
            s.link(v.tensor_reduce(row[:, 2, :], prob[:], AX.X, ALU.max))
            s.link(v.reciprocal(row[:, 1, :], row[:, 1, :]))
            s.link(v.scalar_tensor_tensor(weight[:], row[:, 1, :], 0.5, row[:, 2, :], ALU.mult, ALU.mult))
            s.link(v.tensor_tensor(score[:], prob[:], wide(row[:, 2, :], E), ALU.is_equal))
            s.link(v.tensor_tensor(score[:], score[:], each(k.c("rank"), NT), ALU.mult))
            s.link(v.tensor_reduce(row[:, 3, :], score[:], AX.X, ALU.max))
            v.tensor_tensor(chosen[:].rearrange("p e i -> p i e"), score[:], wide(row[:, 3, :], E), ALU.is_equal).then_inc(chosen_ready, 1)

            count, blocks, blocks_upto, base, offset, ones = (per_e[:, j, :] for j in range(6))
            s.link(v.memset(full[:], 1.0))
            dve.wait_ge(ranked, 1)
            s.link(v.tensor_copy(in_tile[:].rearrange("p e i -> p (e i)"), total_ps[:, 0:P]))
            s.link(v.tensor_tensor_scan(upto[:].rearrange("p e i -> p (e i)"), full[:].rearrange("p e i -> p (e i)"),
                                        in_tile[:].rearrange("p e i -> p (e i)"), 0.0, ALU.mult, ALU.add))
            s.link(v.tensor_reduce(count, in_tile[:], AX.X, ALU.add))
            s.link(v.tensor_tensor(pos[:], wide(count, NT), each(k.c("thresholds"), E), ALU.is_gt))
            s.link(v.tensor_reduce(blocks, pos[:], AX.X, ALU.add))
            s.link(v.tensor_tensor_scan(blocks_upto, full[:, 0, 0:E], blocks, 0.0, ALU.mult, ALU.add))
            s.link(v.tensor_tensor(base, upto[:, :, 0], in_tile[:, :, 0], ALU.subtract))
            s.link(v.tensor_tensor(offset, blocks_upto, blocks, ALU.subtract))
            s.link(v.scalar_tensor_tensor(offset, offset, float(P), base, ALU.mult, ALU.subtract))
            s.link(v.tensor_tensor(pos[:], upto[:], in_tile[:], ALU.subtract))
            s.link(v.tensor_tensor(pos[:], pos[:], rank_ps[:, 0:P].rearrange("p (e i) -> p e i", e=E), ALU.add))
            s.link(v.tensor_tensor(pos[:], pos[:], wide(offset, NT), ALU.add))
            s.link(v.tensor_tensor(pos[:], pos[:], chosen[:], ALU.mult))
            s.link(v.tensor_reduce(slot[:], pos[:].rearrange("p e i -> p i e"), AX.X, ALU.add))
            s.link(v.tensor_copy(slot_i[:, 0, :], slot[:]))
            s.link(v.tensor_scalar(slot_i[:, 1, :], slot_i[:, 0, :], 7, None, ALU.arith_shift_right))
            s.link(v.tensor_scalar(slot_i[:, 2, :], slot_i[:, 0, :], P - 1, None, ALU.bitwise_and))
            s.link(v.tensor_copy(slot_f[:], slot_i[:, 1:3, :]))

            v.tensor_tensor(place[:], each(k.c("lane"), NT), wide(slot_f[:, 1, :], P), ALU.is_equal)
            s.link(v.tensor_tensor(payload[:, :, 0, :], each(k.c("blocks"), NT), wide(slot_f[:, 0, :], NB), ALU.is_equal))
            s.link(v.tensor_scalar(payload[:, :, 1, :], payload[:, :, 0, :], k.c("token"), None, ALU.mult))
            v.tensor_tensor(payload[:, :, 2, :], payload[:, :, 0, :], wide(k.c("tile"), NB), ALU.mult).then_inc(slots_ready, 1)

            s.link(v.tensor_tensor(past[:], wide(k.c("blocks"), E), each(blocks_upto, NB), ALU.is_ge))
            s.link(v.memset(block_e[:], 0.0))
            s.link(v.tensor_reduce(block_e[:, 1:NB + 1], past[:], AX.X, ALU.add))
            s.link(v.tensor_scalar(block_e[:], block_e[:], E - 1.0, None, ALU.min))
            two = block_e[:].rearrange("p (j k) -> p k j", k=2)
            s.link(v.scalar_tensor_tensor(pairs[:], two[:, 1, :], 8.0, two[:, 0, :], ALU.mult, ALU.add))
            n = (NB + 1) // 4
            s.link(v.scalar_tensor_tensor(sixes[:], pairs[:, 1:2 * n:2], 64.0, pairs[:, 0:2 * n:2], ALU.mult, ALU.add))
            s.link(v.scalar_tensor_tensor(expert_digits[:], pairs[:, 2:2 * n + 1:2], 4096.0, sixes[:], ALU.mult, ALU.add))

            dve.wait_ge(inverted, 1)
            s.link(v.tensor_copy(at_slot[:].rearrange("p a b -> p (a b)"), slot_ps[:, 0:3 * NB]))
            s.link(v.scalar_tensor_tensor(token[:, 0, :], at_slot[:, 2, :], float(P), at_slot[:, 1, :], ALU.mult, ALU.add))
            s.link(v.tensor_copy(gather_index[:], token[:, 0, :]))
            s.link(v.tensor_scalar(at_slot[:, 0, :], at_slot[:, 0, :], -SKIP, SKIP, ALU.mult, ALU.add))
            s.link(v.tensor_tensor(token[:, 1, :], token[:, 0, :], at_slot[:, 0, :], ALU.add))
            s.link(v.tensor_copy(scatter_index[:], token[:, 1, :]))


def loaded_experts(engine, expert_digits, trip):
    packed = engine.value_load(expert_digits[0:1, bass.ds(trip, 1)], min_val=0, max_val=8 ** 6 - 1)
    return [(packed >> (3 * digit)) & 7 for digit in range(6)]


def experts(k, tag, xn_dram, y_dram, gather_index, scatter_index, expert_digits):
    nc = k.nc
    with ExitStack() as ctx:
        def sb(name, shape, dt=F32):
            return ctx.enter_context(nc.sbuf_tensor(f"{name}_{tag}", shape, dt))

        def ps(name, shape, dt=F32):
            return ctx.enter_context(nc.psum_tensor(f"{name}_{tag}", shape, dt))

        def sem(name):
            return ctx.enter_context(nc.semaphore(f"{name}_{tag}"))

        rows = sb("rows", [P, NB, C])
        row_in = [sb(f"row_in{n}", [P, C]) for n in range(2)]
        rowT = [sb(f"rowT{n}", [C, P]) for n in range(2)]
        hid = sb("hid", [P, F])
        act_h = sb("act_h", [P, F])
        hT = [sb(f"hT{n}", [P, KF, P]) for n in range(2)]
        y = sb("y", [P, NB, C])
        rowT_ps = [ps(f"rowT_ps{n}", [P, 512]) for n in range(2)]
        hid_ps = [ps(f"hid_ps{n}", [P, F]) for n in range(2)]
        hT_ps = ps("hT_ps", [P, KF, P])
        y_ps = [ps(f"y_ps{n}", [P, 512]) for n in range(2)]

        gathered = [sem(f"gathered{n}") for n in range(2)]
        row_staged, row_turned, rowT_ready = sem("row_staged"), sem("row_turned"), sem("rowT_ready")
        hid_done, hid_biased, silu_done = sem("hid_done"), sem("hid_biased"), sem("silu_done")
        h_turned, hT_ready = sem("h_turned"), sem("hT_ready")
        y_done, y_ready, y_stored = sem("y_done"), sem("y_ready"), sem("y_stored")

        block = ctx.enter_context(nc.Block())
        AHEAD = 6
        TRIPS = (NB - 3) // 4
        assert NB == 3 + 4 * TRIPS

        @block.gpsimd
        def _(pool):
            def gather(b):
                if b >= 2:
                    pool.wait_ge(gathered[b % 2], 16 * (b // 2))
                at = bass.IndirectOffsetOnAxis(ap=gather_index[:, b:b + 1], axis=0)
                nc.gpsimd.indirect_dma_start(rows[:, b, :], None, xn_dram, at).then_inc(gathered[b % 2], 16)

            for b in range(AHEAD):
                gather(b)
            for b in range(NB):
                if b + AHEAD < NB:
                    gather(b + AHEAD)
                pool.wait_ge(y_ready, b + 1)
                at = bass.IndirectOffsetOnAxis(ap=scatter_index[:, b:b + 1], axis=0)
                nc.gpsimd.indirect_dma_start(y_dram, at, y[:, b, :], None, bounds_check=T - 1, oob_is_err=False
                                             ).then_inc(y_stored, 16)
            pool.wait_ge(y_stored, 16 * NB)

        @block.scalar
        def _(act):
            def rows_out(b, n, first=False):
                if not first:
                    act.wait_ge(hid_done, b - 1)
                act.wait_ge(row_turned, b + 1)
                nc.scalar.copy(rowT[n][:], rowT_ps[n][:, 0:P]).then_inc(rowT_ready, 1)

            def silu(b, first=False):
                act.wait_ge(hid_biased, b + 1)
                if not first:
                    act.wait_ge(h_turned, b)
                nc.scalar.activation(act_h[:], hid[:], ACT.Silu).then_inc(silu_done, 1)

            def work(b, n):
                rows_out(b + 2, n)
                silu(b)

            rows_out(0, 0, first=True)
            rows_out(1, 1, first=True)
            rows_out(2, 0)
            silu(0, first=True)
            with act.Fori(0, TRIPS) as trip:
                for j in range(1, 5):
                    work(trip * 4 + j, j % 2)
            silu(NB - 2)
            silu(NB - 1)

        @block.tensor
        def _(pe):
            def turn_rows(b, n, first=False):
                pe.wait_ge(row_staged, b + 1)
                if not first:
                    pe.wait_ge(rowT_ready, b - 1)
                nc.tensor.transpose(rowT_ps[n][:, 0:P], row_in[n][:], k.c("ident")).then_inc(row_turned, 1)

            def experts_of(trip):
                return loaded_experts(pe, expert_digits, trip)

            def first_layer(b, n, e):
                pe.wait_ge(rowT_ready, b + 1)
                if not isinstance(b, int) or b >= 2:
                    pe.wait_ge(hid_biased, b - 1)
                nc.tensor.matmul(hid_ps[n][:], rowT[n][:], k.w1[:, bass.ds(e * F, F)], start=True, stop=True).then_inc(hid_done, 1)

            def turn_hidden(b, first=False):
                pe.wait_ge(silu_done, b + 1)
                if not first:
                    pe.wait_ge(hT_ready, b)
                for f in range(KF):
                    last = nc.tensor.transpose(hT_ps[:, f, :], act_h[:, f * P:(f + 1) * P], k.c("ident"))
                last.then_inc(h_turned, 1)

            def second_layer(b, n, e, drained=True):
                pe.wait_ge(hT_ready, b + 1)
                if drained:
                    pe.wait_ge(y_ready, b - 1)
                for f in range(KF):
                    last = nc.tensor.matmul(y_ps[n][:, 0:C], hT[n][:, f, :], k.w2[:, bass.ds(e * F + f * P, P)], start=(f == 0), stop=(f == KF - 1))
                last.then_inc(y_done, 1)

            def work(b, n, e, e_second, turn=True, drained=True):
                first_layer(b, n, e)
                if turn:
                    turn_rows(b + 2, n)
                turn_hidden(b - 1)
                second_layer(b - 2, n, e_second, drained)

            turn_rows(0, 0, first=True)
            turn_rows(1, 1, first=True)
            pe.wait_ge(k.weights_loaded, k.n_weight_loads * 16)
            e = experts_of(0)
            first_layer(0, 0, e[1])
            turn_rows(2, 0)
            first_layer(1, 1, e[2])
            turn_rows(3, 1)
            turn_hidden(0, first=True)
            for b in range(2, 5):
                work(b, b % 2, e[b + 1], e[b - 1], drained=b >= 4)
            with pe.Fori(1, TRIPS) as trip:
                e = experts_of(trip)
                for j in range(1, 5):
                    work(trip * 4 + j, j % 2, e[j + 1], e[j - 1])
            e = experts_of(TRIPS)
            work(NB - 2, 1, e[2], e[0], turn=False)
            work(NB - 1, 0, e[3], e[1], turn=False)
            turn_hidden(NB - 1)
            second_layer(NB - 2, 1, e[2])
            second_layer(NB - 1, 0, e[3])

        @block.vector
        def _(dve):
            v = nc.vector

            def stage(b, n, first=False):
                dve.wait_ge(gathered[n], (b // 2) * 16 + 16 if isinstance(b, int) else b * 8 + (16 - 8 * n))
                if not first:
                    dve.wait_ge(row_turned, b - 1)
                v.tensor_copy(row_in[n][:], rows[:, bass.ds(b, 1), :].rearrange("p a c -> p (a c)")).then_inc(row_staged, 1)

            def experts_of(trip):
                return loaded_experts(dve, expert_digits, trip)

            def bias(b, n, e, first=False):
                dve.wait_ge(hid_done, b + 1)
                if not first:
                    dve.wait_ge(silu_done, b)
                v.tensor_tensor(hid[:], hid_ps[n][:], k.b1[:, bass.ds(e * F, F)], ALU.add).then_inc(hid_biased, 1)

            def hidden_out(b, n, first=False):
                dve.wait_ge(h_turned, b + 1)
                if not first:
                    dve.wait_ge(y_done, b - 1)
                v.tensor_copy(hT[n][:], hT_ps[:]).then_inc(hT_ready, 1)

            def y_out(b, n, e):
                dve.wait_ge(y_done, b + 1)
                v.tensor_tensor(y[:, bass.ds(b, 1), :].rearrange("p a c -> p (a c)"), y_ps[n][:, 0:C], k.b2[:, bass.ds(e * C, C)], ALU.add
                                ).then_inc(y_ready, 1)

            def work(b, n, e, e_second, ahead=True, first=False):
                bias(b, n, e)
                if ahead:
                    stage(b + 3, 1 - n)
                hidden_out(b - 1, 1 - n, first)
                y_out(b - 2, n, e_second)

            stage(0, 0, first=True)
            stage(1, 1, first=True)
            dve.wait_ge(k.weights_loaded, k.n_weight_loads * 16)
            stage(2, 0)
            e = experts_of(0)
            bias(0, 0, e[1], first=True)
            stage(3, 1)
            bias(1, 1, e[2])
            stage(4, 0)
            hidden_out(0, 0, first=True)
            for b in range(2, 5):
                work(b, b % 2, e[b + 1], e[b - 1], first=b == 2)
            with dve.Fori(1, TRIPS - 1) as trip:
                e = experts_of(trip)
                for j in range(1, 5):
                    work(trip * 4 + j, j % 2, e[j + 1], e[j - 1])
            e = experts_of(TRIPS - 1)
            for j in range(1, 5):
                b = 4 * (TRIPS - 1) + j
                work(b, j % 2, e[j + 1], e[j - 1], ahead=b + 3 < NB)
            e = experts_of(TRIPS)
            work(NB - 2, 1, e[2], e[0], ahead=False)
            work(NB - 1, 0, e[3], e[1], ahead=False)
            hidden_out(NB - 1, 0)
            y_out(NB - 2, 1, e[2])
            y_out(NB - 1, 0, e[3])


def combine(k, tag, y_dram, y, weight, result):
    nc = k.nc
    with ExitStack() as ctx:
        y_loaded = [ctx.enter_context(nc.semaphore(f"y_loaded{g}_{tag}")) for g in range(NT // GB)]
        x_ready = ctx.enter_context(nc.semaphore(f"x_ready_{tag}"))
        x_stored = ctx.enter_context(nc.semaphore(f"x_stored_{tag}"))
        block = ctx.enter_context(nc.Block())
        y_rows = y_dram.rearrange("(i p) c -> p i c", p=P)

        @block.sync
        def _(sp):
            for g in range(NT // GB):
                sp.dma_start(y[:, g * GB:(g + 1) * GB, :], y_rows[:, g * GB:(g + 1) * GB, :]).then_inc(y_loaded[g], 16)
            if result is not None:
                out_rows = result.rearrange("(i p) c -> p i c", p=P)
                for g in range(NT // GB):
                    sp.wait_ge(x_ready, (g + 1) * GB)
                    sp.dma_start(out_rows[:, g * GB:(g + 1) * GB, :], k.x[:, g * GB:(g + 1) * GB, :]).then_inc(x_stored, 16)
                sp.wait_ge(x_stored, 16 * (NT // GB))

        @block.vector
        def _(dve):
            for i in range(NT):
                if i % GB == 0:
                    dve.wait_ge(y_loaded[i // GB], 16)
                nc.vector.scalar_tensor_tensor(k.x[:, i, :], y[:, i, :], weight[:, i:i + 1], k.x[:, i, :], ALU.mult, ALU.add
                                               ).then_inc(x_ready, 1)


def attention(k):
    nc = k.nc
    with ExitStack() as ctx:
        def sb(name, shape, dt=F32):
            return ctx.enter_context(nc.sbuf_tensor(name, shape, dt))

        k.v = sb("v_rows", [P, NT, C])
        k.mixed = sb("mixed", [P, NT, C])
        k.share = sb("share", [P, H, 2])
        k.gk = sb("gk", [H * GR, T], BF16)
        k.gq = sb("gq", [H * GR, H, T], BF16)
        k.parts_dram = nc.dram_tensor("parts_dram", [2, PARTS, C, T], BF16, kind="Internal").ap()
        k.dots = sb("dots", [P, 2, NT, H])
        project(k)
        with ExitStack() as inner:
            k.qt = inner.enter_context(nc.sbuf_tensor("qt", [KS, H, T], BF16))
            k.kt = inner.enter_context(nc.sbuf_tensor("kt", [KS, H, T], BF16))
            k.va = inner.enter_context(nc.sbuf_tensor("va", [P, NT, 2, 32], F32))
            lay_out(k)
            attend(k)
        mix_out(k)


def project(k):
    nc = k.nc
    with ExitStack() as ctx:
        def sb(name, shape, dt=F32):
            return ctx.enter_context(nc.sbuf_tensor(name, shape, dt))

        def ps(name, shape, dt=F32):
            return ctx.enter_context(nc.psum_tensor(name, shape, dt))

        def sem(name):
            return ctx.enter_context(nc.semaphore(name))

        work = sb("work", [P, 2, NT * C])
        wqkv = sb("wqkv", [C, 3 * C])
        gain, shift = sb("gain", [C, 1]), sb("ln_shift", [C, 1])
        dirs = sb("dirs", [P, H * 3])
        scales = sb("scales", [P, H])
        stat = sb("stat_a", [P, 2, NT, 2])
        halves = sb("halves_a", [P, NT, 6])
        xnT = sb("xnT_a", [C, T])
        qk = sb("qk", [P, NT, 2 * C])
        rot = sb("rot", [P, GB, 2 * C])
        parts = sb("parts", [P, PARTS, NT, 2 * C], BF16)
        partsT = sb("partsT", [P, PARTS, T], BF16)
        dot_in = sb("dot_in", [P, 2 * NT, H, 3])

        big = ps("big", [P, 4, 512])
        qkv_ps = [ps(f"qkv_ps{n}", [P, 512]) for n in range(2)]
        turn_ps = [ps(f"turn_ps{n}", [P, 1024], BF16) for n in range(2)]

        xl = work[:, 0, :].rearrange("p (i c) -> p i c", c=C)
        xn = work[:, 1, :].rearrange("p (i c) -> p i c", c=C)
        r = work[:].rearrange("p a b -> p (a b)").rearrange("p (i c) -> p i c", c=2 * C)

        loaded = sem("a_loaded")
        var_ready, dev_ready = [sem(f"a_var{n}") for n in range(2)], [sem(f"a_dev{n}") for n in range(2)]
        xl_ready, x_ready, xn_ready, xn_turned, xnT_ready = sem("a_xl_ready"), sem("a_x_ready"), sem("a_xn_ready"), sem("a_xn_turned"), sem("a_xnT_ready")
        projected, qkv_out = sem("a_projected"), sem("a_qkv_out")
        roped, part0, rest, part1, part2 = (sem(f"a_{n}") for n in ("roped", "part0", "rest", "part1", "part2"))
        turned = [sem(f"a_turned{n}") for n in range(2)]
        turned_out = [sem(f"a_turned_out{n}") for n in range(2)]
        parts_stored = [sem(f"a_parts_stored{n}") for n in range(PARTS)]
        dve_steps = sem("a_dve_steps")
        kinds = [(a, w) for a in range(PARTS) for w in range(2)]
        NG = NT // GB

        block = ctx.enter_context(nc.Block())

        @block.sync
        def _(sp):
            for dst, src in ((wqkv[:], k.arg["Wqkv_t"]), (gain[:], k.arg["ln_g"].unsqueeze(1)),
                             (shift[:], k.arg["ln_b"].unsqueeze(1)),
                             (dirs[:], k.arg["head_dirs"].rearrange("h d -> (h d)").partition_broadcast(P)),
                             (scales[:], k.arg["head_scales"].partition_broadcast(P))):
                sp.dma_start(dst, src).then_inc(loaded, 16)
            for m, (a, w) in enumerate(kinds):
                for n in range(2):
                    sp.wait_ge(turned_out[n], m + 1)
                sp.dma_start(k.parts_dram[w, a], partsT[:, m % PARTS, :]).then_inc(parts_stored[m % PARTS], 16)
            for stored in parts_stored:
                sp.wait_ge(stored, 16 * len(kinds) // PARTS)

        @block.scalar
        def _(act):
            for n in range(2):
                act.wait_ge(var_ready[n], 1)
                nc.scalar.activation(stat[:, n, :, 1], stat[:, n, :, 1], ACT.Sqrt).then_inc(dev_ready[n], 1)
            act.wait_ge(loaded, 80)
            for g in range(NG):
                act.wait_ge(xn_turned, g + 1)
                nc.scalar.activation(xnT[:, g * 512:(g + 1) * 512], big[:, g, :], ACT.Identity, bias=shift[:], scale=gain[:]).then_inc(xnT_ready, 1)
            for i in range(NT):
                act.wait_ge(projected, i + 1)
                nc.scalar.copy(qk[:, i, :], qkv_ps[i % 2][:, 0:2 * C])
                nc.scalar.copy(k.v[:, i, :], qkv_ps[i % 2][:, 2 * C:3 * C]).then_inc(qkv_out, 1)
            for g in range(NG):
                tiles = slice(g * GB, (g + 1) * GB)
                act.wait_ge(roped, g + 1)
                nc.scalar.copy(parts[:, 0, tiles, :], r[:, tiles, :]).then_inc(part0, 1)
                act.wait_ge(rest, g + 1)
                nc.scalar.copy(parts[:, 1, tiles, :], qk[:, tiles, :]).then_inc(part1, 1)
            for m in range(len(kinds)):
                act.wait_ge(turned[0], m + 1)
                if m >= PARTS:
                    act.wait_ge(parts_stored[m % PARTS], 16 * (m // PARTS))
                nc.scalar.copy(partsT[:, m % PARTS, 0:1024], turn_ps[0][:]).then_inc(turned_out[0], 1)

        @block.gpsimd
        def _(pool):
            pool.wait_ge(xl_ready, NT)
            nc.gpsimd.tensor_tensor(k.x[:], k.x[:], xl, ALU.add).then_inc(x_ready, 1)

        @block.tensor
        def _(pe):
            pe.wait_ge(loaded, 80)
            for i in range(NT):
                pe.wait_ge(xn_ready, i + 1)
                last = nc.tensor.transpose(big[:, i // GB, (i % GB) * P:(i % GB + 1) * P], xn[:, i, :], k.c("ident"))
                if i % GB == GB - 1:
                    last.then_inc(xn_turned, 1)
            for i in range(NT):
                if i % GB == 0:
                    pe.wait_ge(xnT_ready, i // GB + 1)
                if i >= 2:
                    pe.wait_ge(qkv_out, i - 1)
                nc.tensor.matmul(qkv_ps[i % 2][:, 0:3 * C], xnT[:, i * P:(i + 1) * P], wqkv[:], start=True, stop=True).then_inc(projected, 1)
            for m, (a, w) in enumerate(kinds):
                if a == 0 and w == 0:
                    pe.wait_ge(part0, NG)
                if a == 1 and w == 0:
                    pe.wait_ge(part1, NG)
                if a == 2 and w == 0:
                    pe.wait_ge(part2, NG)
                for n in range(2):
                    if m:
                        pe.wait_ge(turned_out[n], m)
                    for i in range(8):
                        last = nc.tensor.transpose(turn_ps[n][:, i * P:(i + 1) * P], parts[:, a, n * 8 + i, w * C:(w + 1) * C], k.cbf("ident"))
                    last.then_inc(turned[n], 1)

        @block.vector
        def _(dve):
            v = nc.vector
            s = Steps(dve, dve_steps)
            layernorm(nc, s, k.x, xl, halves, stat[:, 0], var_ready[0], dev_ready[0], xl_ready)
            dve.wait_ge(xl_ready, NT)
            layernorm(nc, s, xl, xn, halves, stat[:, 1], var_ready[1], dev_ready[1], xn_ready)
            dve.wait_ge(loaded, 80)
            v.tensor_copy(k.share[:, :, 1], scales[:])
            v.tensor_scalar(k.share[:, :, 0], scales[:], -1.0, 1.0, ALU.mult, ALU.add)

            half = D // 2
            for g in range(NG):
                tiles = slice(g * GB, (g + 1) * GB)
                dve.wait_ge(qkv_out, (g + 1) * GB)

                def heads(ap):
                    return ap.rearrange("p i (h d) -> p i h d", d=D)

                def table(name):
                    t = k.c(name, g * GB * D, (g + 1) * GB * D).rearrange("p (i d) -> p i d", d=D)
                    return t.unsqueeze(2).broadcast_to([P, GB, 2 * H, D])

                src, dst, turn = heads(qk[:, tiles, :]), heads(r[:, tiles, :]), heads(rot[:])
                if g == 0:
                    dve.wait_ge(xn_turned, NG)
                    dve.wait_ge(x_ready, 1)
                s.mark(v.tensor_tensor(dst, src, table("cos"), ALU.mult))
                s.mark(v.tensor_tensor(turn[:, :, :, 0:half], src[:, :, :, half:D], table("sin")[:, :, :, 0:half], ALU.mult))
                s.link(v.tensor_tensor(turn[:, :, :, half:D], src[:, :, :, 0:half], table("sin")[:, :, :, half:D], ALU.mult))
                s.link(v.tensor_tensor(r[:, tiles, :], r[:, tiles, :], rot[:], ALU.add))
                d = dirs[:].rearrange("p (h d) -> p h d", d=3).unsqueeze(1).broadcast_to([P, 2 * GB, H, 3])
                rows = r[:, tiles, :].rearrange("p i c -> p (i c)").rearrange("p (w h d) -> p w h d", h=H, d=D)[:, :, :, 0:3]
                s.link(v.tensor_tensor(dot_in[:, 2 * g * GB:2 * (g + 1) * GB], rows, d, ALU.mult))
                v.tensor_scalar(r[:, tiles, C:2 * C], r[:, tiles, C:2 * C], float(D) ** -0.5, None, ALU.mult).then_inc(roped, 1)
            s.link(v.tensor_reduce(k.dots[:].rearrange("p w i h -> p i w h"), dot_in[:].rearrange("p (i w) h d -> p i w h d", w=2), AX.X, ALU.add))
            for g in range(NG):
                tiles = slice(g * GB, (g + 1) * GB)
                dve.wait_ge(part0, g + 1)
                v.tensor_tensor(qk[:, tiles, :], r[:, tiles, :], parts[:, 0, tiles, :], ALU.subtract).then_inc(rest, 1)
                dve.wait_ge(part1, g + 1)
                v.tensor_tensor(parts[:, 2, tiles, :], qk[:, tiles, :], parts[:, 1, tiles, :], ALU.subtract).then_inc(part2, 1)
            for m in range(len(kinds)):
                dve.wait_ge(turned[1], m + 1)
                if m >= PARTS:
                    dve.wait_ge(parts_stored[m % PARTS], 16 * (m // PARTS))
                v.tensor_copy(partsT[:, m % PARTS, 1024:2048], turn_ps[1][:]).then_inc(turned_out[1], 1)


def lay_out(k):
    nc = k.nc
    with ExitStack() as ctx:
        def sb(name, shape, dt=F32):
            return ctx.enter_context(nc.sbuf_tensor(name, shape, dt))

        def ps(name, shape, dt=F32):
            return ctx.enter_context(nc.psum_tensor(name, shape, dt))

        def sem(name):
            return ctx.enter_context(nc.semaphore(name))

        rest = sb("dot_rest", [P, 3, NT * H])
        parts = sb("dot_parts", [P, PARTS, 3, NT * H], BF16)
        largest = sb("geo_max", [P, 3, NT * H])
        kdT = sb("kdT", [H, T])
        least = k.mixed[0:H].rearrange("h i c -> h (i c)")
        free = k.mixed[:].rearrange("p i c -> p (i c)").bitcast(BF16)
        n_row = NT * H * GR
        gka, gqa = (free[:, m * n_row:(m + 1) * n_row].rearrange("p (j g) -> p j g", g=GR) for m in range(2))
        gqT = sb("gqT", [H * GR, T], BF16)
        kd_ps = ps("kd_ps", [H, 4, 512])
        upto_ps = ps("upto_ps", [P, 512])
        turn_ps = [ps(f"g_turn_ps{n}", [P, 1024], BF16) for n in range(2)]

        laid, cleared = sem("laid"), sem("va_cleared")
        kd_turned, kdT_ready, upto_ready, upto_turned = (sem(f"g_{n}") for n in ("kd_turned", "kdT", "upto", "upto_turned"))
        rows_ready, rows_turned, rows_out = sem("g_rows_ready"), sem("g_rows_turned"), sem("g_rows_out")
        dve_steps = sem("g_steps")
        block = ctx.enter_context(nc.Block())
        n = len(PRODUCTS)

        @block.sync
        def _(sp):
            for j, (a, b) in enumerate(PRODUCTS):
                sp.dma_start(k.qt[j * D:(j + 1) * D], k.parts_dram[0, a].rearrange("(h d) t -> d h t", d=D)).then_inc(laid, 16)
                sp.dma_start(k.kt[j * D:(j + 1) * D], k.parts_dram[1, b].rearrange("(h d) t -> d h t", d=D)).then_inc(laid, 16)
            sp.dma_start(k.kt[KQ:KS].rearrange("a h t -> a (h t)"), k.arg["ones_rows"]).then_inc(laid, 16)
            sp.wait_ge(laid, 16 * (2 * n + 1))

        @block.gpsimd
        def _(pool):
            nc.gpsimd.memset(k.va[:], 0.0).then_inc(cleared, 1)
            pool.wait_ge(cleared, 1)
            nc.gpsimd.memset(k.va[:, :, :, D:D + 1], 1.0)
            nc.gpsimd.tensor_copy(k.va[:, :, :, 0:D], k.v[:, :, 0:2 * D].rearrange("p j (h d) -> p j h d", d=D))

        @block.tensor
        def _(pe):
            for i in range(NT):
                last = nc.tensor.transpose(kd_ps[:, i // GB, (i % GB) * P:(i % GB + 1) * P], k.dots[:, 1, i, :], k.c("ident"))
            last.then_inc(kd_turned, 1)
            pe.wait_ge(upto_ready, 1)
            for m, src in enumerate((kdT[:], least)):
                for i in range(NT):
                    o = (m * NT + i) * H
                    last = nc.tensor.transpose(upto_ps[:, o:o + H], src[:, i * P:(i + 1) * P], k.c("ident")[0:H, 0:H])
            last.then_inc(upto_turned, 1)
            pe.wait_ge(rows_ready, 1)
            for m, rows in enumerate((gka, gqa)):
                if m:
                    pe.wait_ge(rows_out, 2)
                for i in range(NT):
                    last = nc.tensor.transpose(turn_ps[i // 8][0:H * GR, (i % 8) * P:(i % 8 + 1) * P],
                                               rows[:, i * H:(i + 1) * H].rearrange("p h g -> p (h g)"), k.cbf("ident"))
                last.then_inc(rows_turned, 1)

        @block.scalar
        def _(act):
            act.wait_ge(kd_turned, 1)
            nc.scalar.copy(kdT[:], kd_ps[:].rearrange("h a b -> h (a b)")).then_inc(kdT_ready, 1)

        @block.vector
        def _(dve):
            v = nc.vector
            s = Steps(dve, dve_steps)
            dve.wait_ge(kdT_ready, 1)
            s.link(v.tensor_tensor_scan(least, kdT[:], kdT[:], 3e38, ALU.min, ALU.min))
            v.tensor_tensor_scan(kdT[:], kdT[:], kdT[:], -3e38, ALU.max, ALU.max).then_inc(upto_ready, 1)
            dve.wait_ge(upto_turned, 1)
            qd = k.dots[:, 0].rearrange("p i h -> p (i h)")
            s.mark(v.tensor_copy(rest[:, 0:2, :], k.dots[:].rearrange("p w i h -> p w (i h)")))
            s.mark(v.tensor_tensor(largest[:, 0, :], upto_ps[:, 0:NT * H], qd, ALU.mult))
            s.link(v.tensor_tensor(largest[:, 1, :], upto_ps[:, NT * H:2 * NT * H], qd, ALU.mult))
            s.link(v.tensor_tensor(largest[:, 2, :], largest[:, 0, :], largest[:, 1, :], ALU.max))
            s.link(v.tensor_scalar(rest[:, 2, :], largest[:, 2, :], -1.0, None, ALU.mult))
            s.link(v.tensor_copy(parts[:, 0], rest[:]))
            s.link(v.tensor_tensor(rest[:], rest[:], parts[:, 0], ALU.subtract))
            s.link(v.tensor_copy(parts[:, 1], rest[:]))
            s.mark(v.tensor_tensor(parts[:, 2], rest[:], parts[:, 1], ALU.subtract))
            s.link(v.memset(gka, 1.0))
            for a in range(PARTS):
                s.mark(v.tensor_copy(gka[:, :, a * PARTS:(a + 1) * PARTS], wide(parts[:, a, 1, :], PARTS)))
                s.mark(v.tensor_copy(gqa[:, :, a:PARTS * PARTS:PARTS], wide(parts[:, a, 0, :], PARTS)))
                last = v.tensor_copy(gqa[:, :, PARTS * PARTS + a], parts[:, a, 2, :])
                s.mark(last) if a < PARTS - 1 else last.then_inc(rows_ready, 1)
            dve.wait_ge(rows_turned, 1)
            for m in range(2):
                v.tensor_copy(k.gk[:, m * 1024:(m + 1) * 1024], turn_ps[m][0:H * GR, :]).then_inc(rows_out, 1)
            dve.wait_ge(rows_turned, 2)
            for m in range(2):
                s.link(v.tensor_copy(gqT[:, m * 1024:(m + 1) * 1024], turn_ps[m][0:H * GR, :]))
            for h in range(H):
                v.tensor_scalar(k.gq[:, h, :], gqT[:], k.c("head_rows", h, h + 1)[0:H * GR], None, ALU.mult)


STEPS = [(c, j) for c in range(NCH) for j in range(4 * c + 4)]
NSTEP = len(STEPS)
LAST = [4 * (c + 1) * (c + 2) // 2 - 1 for c in range(NCH)]


def unit_items(pair, c):
    return [("scores", pair, c, hd, i, w) for hd in range(2) for i in range(4) for w in range(c + 1)]


def plan(units):
    items, waiting = [], None
    for pair, c in units:
        own = unit_items(pair, c)
        own[-1] = own[-1] + ("ends",)
        for n, item in enumerate(own):
            items.append(item)
            if n == 1 and waiting:
                items.append(waiting)
        waiting = ("turn", pair, c)
    return items + [waiting]


def attend(k):
    nc = k.nc
    with ExitStack() as ctx:
        def sb(name, shape, dt=F32):
            return ctx.enter_context(nc.sbuf_tensor(name, shape, dt))

        def ps(name, shape, dt=F32):
            return ctx.enter_context(nc.psum_tensor(name, shape, dt))

        def sem(name):
            return ctx.enter_context(nc.semaphore(name))

        prob = sb("prob_a", [P, 4, 2, CH])
        part_max = sb("part_max", [P, 2, 8, NCH])
        shift = sb("shift", [P, 8])
        shift_parts = sb("shift_parts", [P, 2, PARTS, 4], BF16)
        shiftT = sb("shiftT", [2 * PARTS * 4, 2, P], BF16)
        acc = sb("acc_rows", [P, CH])
        inv = sb("inv", [P, 4, 4])
        scaled = sb("scaled", [P, 4, 4, D])
        score_ps = ps("score_ps", [P, 2, 2, CH])
        acc_ps = [ps(f"acc_ps{n}", [P, CH]) for n in range(2)]
        max_ps = [ps(f"max_ps{n}", [P, CH]) for n in range(2)]

        scores_ready, exp_done = sem("scores_ready"), sem("exp_done")
        pv_done, acc_out, acc_turned, acc_free = (sem(n) for n in ("pv_done", "acc_out", "acc_turned", "acc_free"))
        va_ready = sem("va_ready")
        item_ready, item_out = sem("item_ready"), sem("item_out")
        parts_ready, shift_stored = sem("shift_parts_ready"), sem("shift_stored")
        dve_steps = sem("attend_steps")

        first = plan([(0, 0), (0, 1)])
        per_pair = plan([(0, 2), (0, 3), (1, 0), (1, 1)])
        last_pair = plan([(0, 2), (0, 3)])
        assert len(per_pair) % 2 == 0 and len(first) % 2 == 0
        quota = [3] * 20 + [2] * 20

        def split(items):
            out, at = [], 0
            for q in quota:
                out.append(items[at:at + q])
                at += q
            assert at >= len(items)
            return out

        def offset(c, j):
            return max(0, j - 4 * c) * P

        GROUPS = {(0, 0): 1, (2, 8): 2, (3, 12): 3}
        CREDIT = 2
        STORED = 16 * 2 * PARTS
        order = first + per_pair * (NPAIR - 1) + last_pair
        turned_at = [n + 1 for n, item in enumerate(order) if item[0] == "turn"]
        block = ctx.enter_context(nc.Block())

        @block.tensor
        def _(pe):
            def scores(pair, st, hd, slots_used=True):
                c, j = STEPS[st]
                off = offset(c, j)
                if j == 0 and hd == 0:
                    pe.wait_ge(shift_stored, (pair * 4 + c + 1) * STORED)
                if slots_used:
                    pe.wait_ge(exp_done, pair * (2 * NSTEP) + (2 * st + hd - 1))
                h = pair * 2 + hd
                q = slice(c * CH + off, (c + 1) * CH)
                diagonal = j >= 4 * c
                nc.tensor.matmul(score_ps[:, hd, 0, off:], k.kt[:, bass.ds(h, 1), j * P:(j + 1) * P].rearrange("k a t -> k (a t)"),
                                 k.qt[:, bass.ds(h, 1), q].rearrange("k a t -> k (a t)"), start=True, stop=not diagonal)
                last = nc.tensor.matmul(score_ps[:, hd, 1, off:], k.gk[:, j * P:(j + 1) * P],
                                        k.gq[:, bass.ds(h, 1), q].rearrange("k a t -> k (a t)"), start=True, stop=not diagonal)
                if diagonal:
                    for kind in range(2):
                        last = nc.tensor.matmul(score_ps[:, hd, kind, off:off + P], k.cbf("ident"), k.cbf("future_t"), start=False, stop=True)
                last.then_inc(scores_ready, 1)

            def run_items(items, pair, count, unit):
                for n, item in enumerate(items):
                    m = max_ps[(n + parity[0]) % 2]
                    if primed[0] >= 2:
                        pe.wait_ge(item_out, count + n - 1)
                    primed[0] += 1
                    if item[0] == "scores":
                        _, dp, c, hd, i, w = item[:6]
                        h = (pair + dp) * 2 + hd
                        width = CH if w < c else (i + 1) * P
                        q0 = c * CH + i * P
                        last = nc.tensor.matmul(m[:, 0:width], k.qt[0:KQ, bass.ds(h, 1), q0:q0 + P].rearrange("k a t -> k (a t)"),
                                                k.kt[0:KQ, bass.ds(h, 1), w * CH:w * CH + width].rearrange("k a t -> k (a t)"), start=True, stop=w < c)
                        if w == c:
                            last = nc.tensor.matmul(m[:, i * P:(i + 1) * P], k.cbf("ident"), k.cbf("future"), start=False, stop=True)
                        last.then_inc(item_ready, 1)
                    else:
                        pe.wait_ge(parts_ready, unit + 1)
                        unit = unit + 1
                        nc.tensor.transpose(m[:].bitcast(BF16)[0:24, 0:P], shift_parts[:].rearrange("p a b c -> p (a b c)"), k.cbf("ident")
                                            ).then_inc(item_ready, 1)
                parity[0] += len(items)
                return unit

            def values(pair, st):
                c, j = STEPS[st]
                off = offset(c, j)
                if (c, j) in GROUPS:
                    pe.wait_ge(va_ready, pair * 3 + GROUPS[c, j])
                if j == 0:
                    pe.wait_ge(acc_free, pair * 4 + c + 1)
                pe.wait_ge(exp_done, pair * (2 * NSTEP) + 2 * (st + 1))
                for hd in range(2):
                    for kind in range(2):
                        o = 32 * (2 * hd + kind)
                        last = nc.tensor.matmul(acc_ps[c % 2][o:o + 32, off:], k.va[:, j, hd, :], prob[:, (st % 2) * 2 + hd, kind, off:],
                                                start=(j == 0), stop=(j == 4 * c + 3))
                last.then_inc(pv_done, 1)

            def turn_acc(pair, c):
                pe.wait_ge(acc_out, pair * 4 + c + 1)
                for t in range(4):
                    last = nc.tensor.transpose(acc_ps[c % 2][:, t * P:(t + 1) * P], acc[:, t * P:(t + 1) * P], k.c("ident"))
                last.then_inc(acc_turned, 1)

            def body(pair, items, more):
                count = pair * len(per_pair) + len(first)
                unit = pair * 4 + 2
                done = 0
                for st in range(NSTEP):
                    for hd in range(2):
                        if st + 1 < NSTEP:
                            scores(pair, st + 1, hd)
                        elif more:
                            scores(pair + 1, 0, hd)
                        unit = run_items(items[st][hd:hd + 1], pair, count + done, unit)
                        done += len(items[st][hd:hd + 1])
                    values(pair, st)
                    unit = run_items(items[st][2:], pair, count + done, unit)
                    done += len(items[st][2:])
                    for c in range(NCH - 1):
                        if st == LAST[c] + 2:
                            turn_acc(pair, c)
                turn_acc(pair, NCH - 1)

            parity, primed = [0], [0]
            run_items(first, 0, 0, 0)
            for hd in range(2):
                scores(0, 0, hd, slots_used=False)
            with pe.Fori(0, NPAIR - 1) as pair:
                body(pair, split(per_pair), True)
            body(NPAIR - 1, split(last_pair), False)

        @block.scalar
        def _(act):
            def body(pair):
                for st, (c, j) in enumerate(STEPS):
                    off = offset(c, j)
                    act.wait_ge(pv_done, pair * NSTEP + st - 1 + CREDIT)
                    for hd in range(2):
                        act.wait_ge(scores_ready, pair * (2 * NSTEP) + 2 * st + hd + 1)
                        nc.scalar.activation(prob[:, (st % 2) * 2 + hd, :, off:], score_ps[:, hd, :, off:], ACT.Exp).then_inc(exp_done, 1)

            with act.Fori(0, NPAIR) as pair:
                body(pair)

        @block.gpsimd
        def _(pool):
            def values_in(pair, j0, j1):
                nc.gpsimd.tensor_copy(k.va[:, j0:j1, :, 0:D], k.v[:, j0:j1, bass.ds((pair + 1) * 2 * D, 2 * D)].rearrange("p j (h d) -> p j h d", d=D)
                                      ).then_inc(va_ready, 1)

            pool.sem_inc(pv_done, CREDIT)
            pool.sem_inc(va_ready, 3)
            with pool.Fori(0, NPAIR - 1) as pair:
                for j0, j1 in ((0, 8), (8, 12), (12, 16)):
                    pool.wait_ge(pv_done, pair * NSTEP + NSTEP - NT + j1 + CREDIT)
                    values_in(pair, j0, j1)

        @block.sync
        def _(sp):
            for u in range(4 * NPAIR):
                pair, c = u // 4, u % 4
                sp.wait_ge(item_out, turned_at[u])
                for hd in range(2):
                    for a in range(PARTS):
                        r0 = (hd * PARTS + a) * 4
                        sp.dma_start(k.qt[KQ + a:KQ + a + 1, 2 * pair + hd, c * CH:(c + 1) * CH], shiftT[r0:r0 + 4, u % 2, :]).then_inc(shift_stored, 16)
                sp.wait_ge(shift_stored, STORED * (u + 1))

        @block.vector
        def _(dve):
            v = nc.vector
            s = Steps(dve, dve_steps)

            def finish_unit(c):
                s.link(v.tensor_reduce(shift[:], part_max[:, c % 2, :, 0:c + 1], AX.X, ALU.max, negate=True))
                rows = shift[:].rearrange("p (h i) -> p h i", i=4)
                s.link(v.tensor_copy(shift_parts[:, :, 0, :], rows))
                s.link(v.tensor_tensor(rows, rows, shift_parts[:, :, 0, :], ALU.subtract))
                s.link(v.tensor_copy(shift_parts[:, :, 1, :], rows))
                v.tensor_tensor(shift_parts[:, :, 2, :], rows, shift_parts[:, :, 1, :], ALU.subtract).then_inc(parts_ready, 1)

            def run_items(items, count, unit):
                for n, item in enumerate(items):
                    m = max_ps[(n + parity[0]) % 2]
                    dve.wait_ge(item_ready, count + n + 1)
                    if item[0] == "scores":
                        _, _, c, hd, i, w = item[:6]
                        width = CH if w < c else (i + 1) * P
                        v.tensor_reduce(part_max[:, c % 2, hd * 4 + i, w:w + 1], m[:, 0:width], AX.X, ALU.max).then_inc(item_out, 1)
                        if item[-1] == "ends":
                            dve.wait_ge(item_out, count + n + 1)
                            finish_unit(c)
                    else:
                        c = item[2]
                        if stored[0]:
                            dve.wait_ge(shift_stored, (unit - 1) * STORED)
                        v.tensor_copy(shiftT[:, c % 2, :], m[:].bitcast(BF16)[0:24, 0:P]).then_inc(item_out, 1)
                        unit = unit + 1
                parity[0] += len(items)
                return unit

            def acc_to_rows(pair, st):
                c = STEPS[st][0]
                dve.wait_ge(pv_done, pair * NSTEP + st + 1 + CREDIT)
                v.tensor_copy(acc[:], acc_ps[c % 2][:]).then_inc(acc_out, 1)

            def mix(pair, c):
                dve.wait_ge(acc_turned, pair * 4 + c + 1)
                sums = acc_ps[c % 2][:].rearrange("p (t q r) -> p t q r", q=4, r=32)
                s.link(v.reciprocal(inv[:], sums[:, :, :, D]))
                share = k.share[:, bass.ds(pair * 2, 2), :].rearrange("p h k -> p (h k)")
                s.link(v.tensor_tensor(inv[:], inv[:], each(share, 4), ALU.mult))
                v.tensor_tensor(scaled[:], sums[:, :, :, 0:D], inv[:].unsqueeze(3).broadcast_to([P, 4, 4, D]), ALU.mult).then_inc(acc_free, 1)
                dve.wait_ge(acc_free, pair * 4 + c + 1 + 2)
                kinds = scaled[:].rearrange("p t (h k) d -> p t h k d", k=2)
                out = k.mixed[:, 4 * c:4 * c + 4, bass.ds(pair * 2 * D, 2 * D)].rearrange("p t (h d) -> p t h d", d=D)
                s.mark(v.tensor_tensor(out, kinds[:, :, :, 0, :], kinds[:, :, :, 1, :], ALU.add))

            def body(pair, items):
                count = pair * len(per_pair) + len(first)
                unit = pair * 4 + 2
                done = 0
                for st in range(NSTEP):
                    for c in range(NCH - 1):
                        if st == LAST[c] + 3:
                            mix(pair, c)
                    unit = run_items(items[st][:2], count + done, unit)
                    done += len(items[st][:2])
                    if st in LAST:
                        acc_to_rows(pair, st)
                    unit = run_items(items[st][2:], count + done, unit)
                    done += len(items[st][2:])
                mix(pair, NCH - 1)

            parity, stored = [0], [False]
            dve.sem_inc(acc_free, 2)
            run_items(first, 0, 0)
            stored[0] = True
            with dve.Fori(0, NPAIR - 1) as pair:
                s.enter(pair, 4 * 4 + 4 * 3)
                body(pair, split(per_pair))
                s.leave(NPAIR - 1)
            body(NPAIR - 1, split(last_pair))


def mix_out(k):
    nc = k.nc
    with ExitStack() as ctx:
        def sem(name):
            return ctx.enter_context(nc.semaphore(name))

        wo = ctx.enter_context(nc.sbuf_tensor("wo", [C, C], F32))
        mixedT = ctx.enter_context(nc.sbuf_tensor("mixedT", [C, T], F32))
        turn_ps = [ctx.enter_context(nc.psum_tensor(f"o_turn_ps{n}", [P, 512], F32)) for n in range(2)]
        out_ps = [ctx.enter_context(nc.psum_tensor(f"o_out_ps{n}", [P, 512], F32)) for n in range(2)]
        wo_loaded, turned, mixedT_ready, multiplied, added = (sem(f"o_{n}") for n in ("loaded", "turned", "ready", "multiplied", "added"))
        block = ctx.enter_context(nc.Block())

        @block.sync
        def _(sp):
            sp.dma_start(wo[:], k.arg["Wo_t"]).then_inc(wo_loaded, 16)

        @block.tensor
        def _(pe):
            def multiply(g):
                pe.wait_ge(mixedT_ready, g + 1)
                if g >= 2:
                    pe.wait_ge(added, g - 1)
                for i in range(GB):
                    t = g * GB + i
                    last = nc.tensor.matmul(out_ps[g % 2][:, i * P:(i + 1) * P], mixedT[:, t * P:(t + 1) * P], wo[:], start=True, stop=True)
                last.then_inc(multiplied, 1)

            pe.wait_ge(wo_loaded, 16)
            for g in range(NT // GB):
                if g >= 2:
                    pe.wait_ge(mixedT_ready, g - 1)
                for i in range(GB):
                    last = nc.tensor.transpose(turn_ps[g % 2][:, i * P:(i + 1) * P], k.mixed[:, g * GB + i, :], k.c("ident"))
                last.then_inc(turned, 1)
                if g:
                    multiply(g - 1)
            multiply(NT // GB - 1)

        @block.scalar
        def _(act):
            for g in range(NT // GB):
                act.wait_ge(turned, g + 1)
                nc.scalar.copy(mixedT[:, g * 512:(g + 1) * 512], turn_ps[g % 2][:]).then_inc(mixedT_ready, 1)

        @block.vector
        def _(dve):
            for g in range(NT // GB):
                dve.wait_ge(multiplied, g + 1)
                rows = k.x[:, g * GB:(g + 1) * GB, :].rearrange("p i c -> p (i c)")
                nc.vector.tensor_tensor(rows, rows, out_ps[g % 2][:], ALU.add).then_inc(added, 1)


def program(nc, a, out):
    with ExitStack() as ctx:
        k = Kernel(nc, ctx, a)

        k.weights_loaded = ctx.enter_context(nc.semaphore("weights_loaded"))
        x_and_tables = [
            (k.x[:], a["x"].rearrange("(i p) c -> p i c", p=P)),
            (k.cf[:], a["constants"]),
            (k.wg[:], a["Wg"]),
            (k.bg[:], a["bg"].partition_broadcast(P)),
            (k.cb[:], a["constants_bf16"]),
        ]
        weights = [
            (k.w1[:, e * F:(e + 1) * F], a["W1"][e]) for e in range(E)
        ] + [
            (k.b1[:], a["b1"].rearrange("e f -> (e f)").partition_broadcast(P)),
            (k.b2[:], a["b2"].rearrange("e c -> (e c)").partition_broadcast(P)),
        ] + [
            (k.w2[:, e * F:(e + 1) * F].rearrange("p (f c) -> p f c", f=KF), a["W2"][e].rearrange("(f p) c -> p f c", p=P))
            for e in range(E)
        ]
        k.n_weight_loads = len(weights)
        assert len(x_and_tables) == N_FIRST_LOADS

        def load_all(sp, loaded):
            for dst, src in x_and_tables:
                sp.dma_start(dst, src).then_inc(loaded, 16)
            for dst, src in weights:
                sp.dma_start(dst, src).then_inc(k.weights_loaded, 16)

        ffn(k, "first", load_all, None)
        attention(k)
        ffn(k, "second", None, out)


def kernel(**inputs):
    import ml_dtypes
    import concourse.bacc as bacc
    from concourse.bass_utils import run_bass_kernel_spmd

    g = {n: np.ascontiguousarray(v) for n, v in inputs.items()}
    bf16 = ml_dtypes.bfloat16
    laid = {
        "x": g["L0_attn_x"].reshape(T, C),
        "Wqkv_t": np.ascontiguousarray(np.concatenate([g["L0_attn_Wq"].T, g["L0_attn_Wk"].T, g["L0_attn_Wv"].T], 1)),
        "Wo_t": np.ascontiguousarray(g["L0_attn_Wo"].T),
        "ln_g": g["L0_attn_ln_g"],
        "ln_b": g["L0_attn_ln_b"],
        "head_scales": g["L0_attn_head_scales"],
        "head_dirs": g["L0_attn_head_dirs"],
        "Wg": g["L0_ffn_Wg"],
        "bg": g["L0_ffn_bg"],
        "W1": g["L0_ffn_W1"],
        "b1": g["L0_ffn_b1"],
        "W2": g["L0_ffn_W2"],
        "b2": g["L0_ffn_b2"],
        "constants": float_constants(),
        "constants_bf16": bf16_constants(bf16),
        "ones_rows": np.ones((PARTS, H * T), bf16),
    }
    nc = bacc.Bacc("TRN2", target_bir_lowering=False, num_devices=1)
    a = {n: nc.dram_tensor(f"in_{n}", v.shape, mybir.dt.from_np(v.dtype), kind="ExternalInput").ap() for n, v in laid.items()}
    out = nc.dram_tensor("out_x", (T, C), F32, kind="ExternalOutput").ap()
    program(nc, a, out)
    r = run_bass_kernel_spmd(nc, [{f"in_{n}": v for n, v in laid.items()}], core_ids=[0])
    return r.results[0]["out_x"].reshape(1, T, C)
```

```python
from contextlib import ExitStack

import numpy as np

import concourse.bass as bass
from concourse import mybir
from concourse.alu_op_type import AluOpType as ALU

ACT = mybir.ActivationFunctionType
AX = mybir.AxisListType
F32 = mybir.dt.float32
BF16 = mybir.dt.bfloat16
I32 = mybir.dt.int32

P = 128
T = 2048
NT = T // P
C = 128
H = 8
D = C // H
E = 8
F = 512
KF = F // P
NB = (T + E * (P - 1)) // P
GB = 4
EPS = 1e-5
N_FIRST_LOADS = 4
NEG = -1e38
SKIP = 4096.0

CH = 512
NCH = T // CH
NPAIR = H // 2
PARTS = 3
PRODUCTS = [(0, 0), (1, 1), (2, 0), (0, 1), (1, 0), (0, 2)]
KQ = len(PRODUCTS) * D
KS = KQ + PARTS
GR = PARTS * PARTS + PARTS


class Columns:

    def __init__(self, **widths):
        self.at, self.width = {}, 0
        for name, w in widths.items():
            self.at[name] = (self.width, w)
            self.width += w


FC = Columns(ident=P, lane=P, blocks=NB, thresholds=NT, rank=E, token=1, tile=NT, head_rows=H,
             cos=NT * D, sin=NT * D)
BC = Columns(ident=P, before=P, ones=P, future=P, future_t=P)


def float_constants():
    t = np.zeros((P, FC.width), np.float32)

    def put(name, a):
        o, w = FC.at[name]
        t[:, o:o + w] = a

    p = np.arange(P, dtype=np.float32)[:, None]
    put("ident", np.eye(P))
    put("lane", np.arange(P)[None])
    put("blocks", np.arange(NB)[None])
    put("thresholds", P * np.arange(NT)[None])
    put("rank", E - np.arange(E)[None])
    put("token", p)
    put("tile", np.arange(NT)[None])
    put("head_rows", (np.arange(P)[:, None] // GR) == np.arange(H)[None])
    inverse = np.float32(1.0) / np.float32(10000.0) ** (np.arange(0, D, 2, dtype=np.float32) / np.float32(D))
    angle = np.arange(T, dtype=np.float32)[:, None] * inverse[None].astype(np.float32)
    cos = np.concatenate([np.cos(angle)] * 2, 1).astype(np.float32)
    sin = np.concatenate([-np.sin(angle), np.sin(angle)], 1).astype(np.float32)
    put("cos", cos.reshape(NT, P, D).transpose(1, 0, 2).reshape(P, NT * D))
    put("sin", sin.reshape(NT, P, D).transpose(1, 0, 2).reshape(P, NT * D))
    return t


def bf16_constants(bf16):
    t = np.zeros((P, BC.width), np.float32)
    q = np.arange(P)[:, None]
    k = np.arange(P)[None]
    for name, a in (("ident", q == k), ("before", q < k), ("ones", np.ones((P, P))),
                    ("future", np.where(k > q, NEG, 0.0)), ("future_t", np.where(q > k, NEG, 0.0))):
        o, w = BC.at[name]
        t[:, o:o + w] = a
    return t.astype(bf16)


class Steps:

    def __init__(self, engine, sem):
        self.engine, self.sem, self.n, self.trip, self.per = engine, sem, 0, None, 0

    def value(self):
        return self.n if self.trip is None else self.trip * self.per + self.n

    def mark(self, instruction):
        instruction.then_inc(self.sem, 1)
        self.n += 1

    def link(self, instruction):
        self.mark(instruction)
        self.engine.wait_ge(self.sem, self.value())

    def enter(self, trip, per):
        self.trip, self.per, self.start = trip, per, self.n

    def leave(self, trips):
        assert self.n - self.start == self.per, (self.n - self.start, self.per)
        self.n, self.trip = self.start + self.per * trips, None


class Kernel:

    def __init__(self, nc, ctx, arg):
        self.nc, self.arg = nc, arg

        def sb(name, shape, dt=F32):
            return ctx.enter_context(nc.sbuf_tensor(name, shape, dt))

        self.x = sb("x_res", [P, NT, C])
        self.w1 = sb("w1", [P, E * F])
        self.w2 = sb("w2", [P, E * F])
        self.b1 = sb("b1", [P, E * F])
        self.b2 = sb("b2", [P, E * C])
        self.wg = sb("wg", [C, E])
        self.bg = sb("bg", [P, E])
        self.wo = sb("wo", [C, C])
        self.cf = sb("cf", [P, FC.width])
        self.cb = sb("cb", [P, BC.width], BF16)

    def c(self, name, a=0, b=None):
        o, w = FC.at[name]
        return self.cf[:, o + a:o + (w if b is None else b)]

    def cbf(self, name):
        o, w = BC.at[name]
        return self.cb[:, o:o + w]


def wide(ap, n):
    return ap.unsqueeze(2).broadcast_to([ap.shape[0], ap.shape[1], n])


def each(ap, n):
    return ap.unsqueeze(1).broadcast_to([ap.shape[0], n, ap.shape[1]])


class LayernormSems:
    def __init__(self, sem, tag):
        self.variance_ready = sem(f"variance_ready_{tag}")
        self.deviation_ready = sem(f"deviation_ready_{tag}")
        self.inverse_ready = sem(f"inverse_ready_{tag}")
        self.by_vector = sem(f"by_vector_{tag}")
        self.by_scalar = sem(f"by_scalar_{tag}")

    def wait(self, engine, fours):
        engine.wait_ge(self.by_vector, 3 * fours)
        engine.wait_ge(self.by_scalar, fours)


def layernorm(nc, steps, sems, src, dst, halves, stat, arrived=None):
    v, dve = nc.vector, steps.engine
    for i in range(NT):
        if arrived and i % GB == 0:
            dve.wait_ge(arrived[i // GB], 16)
        v.bn_stats(halves[:, i, :], src[:, i, :]).then_inc(steps.sem, 1)
    steps.n += NT
    dve.wait_ge(steps.sem, steps.n)
    for i in range(NT):
        v.bn_aggr(stat[:, i, 0:2], halves[:, i, :]).then_inc(steps.sem, 1)
    steps.n += NT
    dve.wait_ge(steps.sem, steps.n)
    v.tensor_scalar(stat[:, :, 1], stat[:, :, 1], EPS, None, ALU.add).then_inc(sems.variance_ready, 1)
    dve.wait_ge(sems.deviation_ready, 1)
    steps.link(v.reciprocal(stat[:, :, 1], stat[:, :, 1]))
    v.scalar_tensor_tensor(stat[:, :, 2], stat[:, :, 0], -1.0, stat[:, :, 1], ALU.mult, ALU.mult).then_inc(sems.inverse_ready, 1)
    for i in [i for i in range(NT) if i % 4 < 3]:
        v.tensor_scalar(dst[:, i, :], src[:, i, :], stat[:, i, 0:1], stat[:, i, 1:2], ALU.subtract, ALU.mult).then_inc(sems.by_vector, 1)


def layernorm_scalar(nc, act, sems, src, dst, stat):
    act.wait_ge(sems.variance_ready, 1)
    nc.scalar.activation(stat[:, :, 1], stat[:, :, 1], ACT.Sqrt).then_inc(sems.deviation_ready, 1)
    act.wait_ge(sems.inverse_ready, 1)
    for i in range(3, NT, 4):
        nc.scalar.activation(dst[:, i, :], src[:, i, :], ACT.Identity, bias=stat[:, i, 2:3], scale=stat[:, i, 1:2]).then_inc(sems.by_scalar, 1)


def ffn(k, tag, load, result):
    nc = k.nc
    with ExitStack() as ctx:
        def sb(name, shape, dt=F32):
            return ctx.enter_context(nc.sbuf_tensor(f"{name}_{tag}", shape, dt))

        def sem(name):
            return ctx.enter_context(nc.semaphore(f"{name}_{tag}"))

        xn = sb("xn", [P, NT, C])
        stat = sb("stat", [P, NT, 3])
        halves = sb("halves", [P, NT, 6])
        weight = sb("weight", [P, NT])
        gather_index = sb("gather_index", [P, NB], I32)
        scatter_index = sb("scatter_index", [P, NB], I32)
        expert_digits = sb("expert_digits", [P, (NB + 1) // 4], I32)
        xn_dram = nc.dram_tensor(f"xn_dram_{tag}", [T, C], F32, kind="Internal").ap()
        y_dram = nc.dram_tensor(f"y_dram_{tag}", [T, C], F32, kind="Internal").ap()
        route(k, tag, load, xn, halves, stat, weight, gather_index, scatter_index, expert_digits, xn_dram)
        experts(k, tag, xn_dram, y_dram, gather_index, scatter_index, expert_digits)
        combine(k, tag, y_dram, xn, weight, result)


def route(k, tag, load, xn, halves, stat, weight, gather_index, scatter_index, expert_digits, xn_dram):
    nc = k.nc
    with ExitStack() as ctx:
        def sb(name, shape, dt=F32):
            return ctx.enter_context(nc.sbuf_tensor(f"{name}_{tag}", shape, dt))

        def ps(name, shape, dt=F32):
            return ctx.enter_context(nc.psum_tensor(f"{name}_{tag}", shape, dt))

        def sem(name):
            return ctx.enter_context(nc.semaphore(f"{name}_{tag}"))

        xnT = sb("xnT", [C, T])
        logits = sb("logits", [P, NT, E])
        prob = sb("prob", [P, NT, E])
        score = sb("score", [P, NT, E])
        row = sb("row", [P, 4, NT])
        chosen = sb("chosen", [P, E, NT], BF16)
        in_tile = sb("in_tile", [P, E, NT])
        upto = sb("upto", [P, E, NT])
        full = sb("full", [P, E, NT])
        per_e = sb("per_e", [P, 6, E])
        pos = sb("pos", [P, E, NT])
        slot = sb("slot", [P, NT])
        slot_i = sb("slot_i", [P, 3, NT], I32)
        slot_f = sb("slot_f", [P, 2, NT])
        place = sb("place", [P, NT, P], BF16)
        payload = sb("payload", [P, NT, 3, NB], BF16)
        at_slot = sb("at_slot", [P, 3, NB])
        token = sb("token", [P, 2, NB])
        past = sb("past", [P, NB, E])
        block_e = sb("block_e", [P, NB + 3])
        pairs = sb("pairs", [P, (NB + 3) // 2])
        sixes = sb("sixes", [P, (NB + 1) // 4])
        xnT_ps = ps("xnT_ps", [P, 4, 512])
        gate_ps = ps("gate_ps", [P, 512])
        rank_ps = ps("rank_ps", [P, 512])
        total_ps = ps("total_ps", [P, 512])
        slot_ps = ps("slot_ps", [P, 512])

        loaded = sem("loaded")
        norm = LayernormSems(sem, "norm")
        xn_stored = sem("xn_stored")
        transposed = sem("transposed")
        xnT_ready = sem("xnT_ready")
        gated = sem("gated")
        exp_in, exp_done = sem("exp_in"), sem("exp_done")
        chosen_ready = sem("chosen_ready")
        ranked = sem("ranked")
        slots_ready = sem("slots_ready")
        inverted = sem("inverted")
        dve_steps = sem("dve_steps")

        block = ctx.enter_context(nc.Block())

        @block.sync
        def _(sp):
            if load:
                load(sp, loaded)
            norm.wait(sp, NT // 4)
            sp.dma_start(xn_dram.rearrange("(i p) c -> p i c", p=P), xn[:]).then_inc(xn_stored, 16)
            sp.wait_ge(xn_stored, 16)

        @block.scalar
        def _(act):
            layernorm_scalar(nc, act, norm, k.x, xn, stat)
            for g in range(NT // GB):
                act.wait_ge(transposed, g + 1)
                nc.scalar.copy(xnT[:, g * 512:(g + 1) * 512], xnT_ps[:, g, :]).then_inc(xnT_ready, 1)
            act.wait_ge(exp_in, 1)
            nc.scalar.activation(prob[:], logits[:], ACT.Exp).then_inc(exp_done, 1)

        @block.tensor
        def _(pe):
            def turn(g):
                norm.wait(pe, g + 1)
                for i in range(GB):
                    last = nc.tensor.transpose(xnT_ps[:, g, i * P:(i + 1) * P], xn[:, g * GB + i, :], k.c("ident"))
                last.then_inc(transposed, 1)

            def gate(g):
                pe.wait_ge(xnT_ready, g + 1)
                for i in range(g * GB, (g + 1) * GB):
                    nc.tensor.matmul(gate_ps[:, i * E:(i + 1) * E], xnT[:, i * P:(i + 1) * P], k.wg[:], start=True, stop=True).then_inc(gated, 1)

            if load:
                pe.wait_ge(loaded, 16 * N_FIRST_LOADS)
            for g in range(NT // GB):
                turn(g)
                if g:
                    gate(g - 1)
            gate(NT // GB - 1)
            pe.wait_ge(chosen_ready, 1)
            flat = chosen[:].rearrange("p e i -> p (e i)")
            nc.tensor.matmul(rank_ps[:, 0:P], k.cbf("before"), flat, start=True, stop=True)
            nc.tensor.matmul(total_ps[:, 0:P], k.cbf("ones"), flat, start=True, stop=True).then_inc(ranked, 1)
            pe.wait_ge(slots_ready, 1)
            for i in range(NT):
                last = nc.tensor.matmul(slot_ps[:, 0:3 * NB], place[:, i, :], payload[:, i].rearrange("p a b -> p (a b)"),
                                        start=(i == 0), stop=(i == NT - 1))
            last.then_inc(inverted, 1)

        @block.vector
        def _(dve):
            v = nc.vector
            s = Steps(dve, dve_steps)
            layernorm(nc, s, norm, k.x, xn, halves, stat, k.x_loaded if load else None)
            if load:
                dve.wait_ge(loaded, 16 * N_FIRST_LOADS)

            dve.wait_ge(gated, NT)
            s.link(v.tensor_tensor(logits[:], gate_ps[:, 0:NT * E].rearrange("p (i e) -> p i e", e=E), each(k.bg[:], NT), ALU.add))
            s.link(v.tensor_reduce(row[:, 0, :], logits[:], AX.X, ALU.max))
            v.tensor_tensor(logits[:], logits[:], wide(row[:, 0, :], E), ALU.subtract).then_inc(exp_in, 1)
            dve.wait_ge(exp_done, 1)
            s.link(v.tensor_reduce(row[:, 1, :], prob[:], AX.X, ALU.add))
            s.link(v.tensor_reduce(row[:, 2, :], prob[:], AX.X, ALU.max))
            s.link(v.reciprocal(row[:, 1, :], row[:, 1, :]))
            s.link(v.scalar_tensor_tensor(weight[:], row[:, 1, :], 0.5, row[:, 2, :], ALU.mult, ALU.mult))
            s.link(v.tensor_tensor(score[:], prob[:], wide(row[:, 2, :], E), ALU.is_equal))
            s.link(v.tensor_tensor(score[:], score[:], each(k.c("rank"), NT), ALU.mult))
            s.link(v.tensor_reduce(row[:, 3, :], score[:], AX.X, ALU.max))
            v.tensor_tensor(chosen[:].rearrange("p e i -> p i e"), score[:], wide(row[:, 3, :], E), ALU.is_equal).then_inc(chosen_ready, 1)

            count, blocks, blocks_upto, base, offset, ones = (per_e[:, j, :] for j in range(6))
            s.link(v.memset(full[:], 1.0))
            dve.wait_ge(ranked, 1)
            s.link(v.tensor_copy(in_tile[:].rearrange("p e i -> p (e i)"), total_ps[:, 0:P]))
            s.link(v.tensor_tensor_scan(upto[:].rearrange("p e i -> p (e i)"), full[:].rearrange("p e i -> p (e i)"),
                                        in_tile[:].rearrange("p e i -> p (e i)"), 0.0, ALU.mult, ALU.add))
            s.link(v.tensor_reduce(count, in_tile[:], AX.X, ALU.add))
            s.link(v.tensor_tensor(pos[:], wide(count, NT), each(k.c("thresholds"), E), ALU.is_gt))
            s.link(v.tensor_reduce(blocks, pos[:], AX.X, ALU.add))
            s.link(v.tensor_tensor_scan(blocks_upto, full[:, 0, 0:E], blocks, 0.0, ALU.mult, ALU.add))
            s.link(v.tensor_tensor(base, upto[:, :, 0], in_tile[:, :, 0], ALU.subtract))
            s.link(v.tensor_tensor(offset, blocks_upto, blocks, ALU.subtract))
            s.link(v.scalar_tensor_tensor(offset, offset, float(P), base, ALU.mult, ALU.subtract))
            s.link(v.tensor_tensor(pos[:], upto[:], in_tile[:], ALU.subtract))
            s.link(v.tensor_tensor(pos[:], pos[:], rank_ps[:, 0:P].rearrange("p (e i) -> p e i", e=E), ALU.add))
            s.link(v.tensor_tensor(pos[:], pos[:], wide(offset, NT), ALU.add))
            s.link(v.tensor_tensor(pos[:], pos[:], chosen[:], ALU.mult))
            s.link(v.tensor_reduce(slot[:], pos[:].rearrange("p e i -> p i e"), AX.X, ALU.add))
            s.link(v.tensor_copy(slot_i[:, 0, :], slot[:]))
            s.link(v.tensor_scalar(slot_i[:, 1, :], slot_i[:, 0, :], 7, None, ALU.arith_shift_right))
            s.link(v.tensor_scalar(slot_i[:, 2, :], slot_i[:, 0, :], P - 1, None, ALU.bitwise_and))
            s.link(v.tensor_copy(slot_f[:], slot_i[:, 1:3, :]))

            v.tensor_tensor(place[:], each(k.c("lane"), NT), wide(slot_f[:, 1, :], P), ALU.is_equal)
            s.link(v.tensor_tensor(payload[:, :, 0, :], each(k.c("blocks"), NT), wide(slot_f[:, 0, :], NB), ALU.is_equal))
            s.link(v.tensor_scalar(payload[:, :, 1, :], payload[:, :, 0, :], k.c("token"), None, ALU.mult))
            v.tensor_tensor(payload[:, :, 2, :], payload[:, :, 0, :], wide(k.c("tile"), NB), ALU.mult).then_inc(slots_ready, 1)

            s.link(v.tensor_tensor(past[:], wide(k.c("blocks"), E), each(blocks_upto, NB), ALU.is_ge))
            s.link(v.memset(block_e[:], 0.0))
            s.link(v.tensor_reduce(block_e[:, 1:NB + 1], past[:], AX.X, ALU.add))
            s.link(v.tensor_scalar(block_e[:], block_e[:], E - 1.0, None, ALU.min))
            two = block_e[:].rearrange("p (j k) -> p k j", k=2)
            s.link(v.scalar_tensor_tensor(pairs[:], two[:, 1, :], 8.0, two[:, 0, :], ALU.mult, ALU.add))
            n = (NB + 1) // 4
            s.link(v.scalar_tensor_tensor(sixes[:], pairs[:, 1:2 * n:2], 64.0, pairs[:, 0:2 * n:2], ALU.mult, ALU.add))
            s.link(v.scalar_tensor_tensor(expert_digits[:], pairs[:, 2:2 * n + 1:2], 4096.0, sixes[:], ALU.mult, ALU.add))

            dve.wait_ge(inverted, 1)
            s.link(v.tensor_copy(at_slot[:].rearrange("p a b -> p (a b)"), slot_ps[:, 0:3 * NB]))
            s.link(v.scalar_tensor_tensor(token[:, 0, :], at_slot[:, 2, :], float(P), at_slot[:, 1, :], ALU.mult, ALU.add))
            s.link(v.tensor_copy(gather_index[:], token[:, 0, :]))
            s.link(v.tensor_scalar(at_slot[:, 0, :], at_slot[:, 0, :], -SKIP, SKIP, ALU.mult, ALU.add))
            s.link(v.tensor_tensor(token[:, 1, :], token[:, 0, :], at_slot[:, 0, :], ALU.add))
            s.link(v.tensor_copy(scatter_index[:], token[:, 1, :]))


def loaded_experts(engine, expert_digits, trip):
    packed = engine.value_load(expert_digits[0:1, bass.ds(trip, 1)], min_val=0, max_val=8 ** 6 - 1)
    return [(packed >> (3 * digit)) & 7 for digit in range(6)]


def experts(k, tag, xn_dram, y_dram, gather_index, scatter_index, expert_digits):
    nc = k.nc
    with ExitStack() as ctx:
        def sb(name, shape, dt=F32):
            return ctx.enter_context(nc.sbuf_tensor(f"{name}_{tag}", shape, dt))

        def ps(name, shape, dt=F32):
            return ctx.enter_context(nc.psum_tensor(f"{name}_{tag}", shape, dt))

        def sem(name):
            return ctx.enter_context(nc.semaphore(f"{name}_{tag}"))

        rows = sb("rows", [P, NB, C])
        row_in = [sb(f"row_in{n}", [P, C]) for n in range(2)]
        rowT = [sb(f"rowT{n}", [C, P]) for n in range(2)]
        hid = sb("hid", [P, F])
        act_h = sb("act_h", [P, F])
        hT = [sb(f"hT{n}", [P, KF, P]) for n in range(2)]
        y = sb("y", [P, NB, C])
        rowT_ps = [ps(f"rowT_ps{n}", [P, 512]) for n in range(2)]
        hid_ps = [ps(f"hid_ps{n}", [P, F]) for n in range(2)]
        hT_ps = ps("hT_ps", [P, KF, P])
        y_ps = [ps(f"y_ps{n}", [P, 512]) for n in range(2)]

        gathered = [sem(f"gathered{n}") for n in range(2)]
        row_staged, row_turned, rowT_ready = sem("row_staged"), sem("row_turned"), sem("rowT_ready")
        hid_done, hid_biased, silu_done = sem("hid_done"), sem("hid_biased"), sem("silu_done")
        h_turned, hT_ready = sem("h_turned"), sem("hT_ready")
        y_done, y_ready, y_stored = sem("y_done"), sem("y_ready"), sem("y_stored")

        block = ctx.enter_context(nc.Block())
        AHEAD = 6
        TRIPS = (NB - 3) // 4
        assert NB == 3 + 4 * TRIPS

        @block.gpsimd
        def _(pool):
            def gather(b):
                if b >= 2:
                    pool.wait_ge(gathered[b % 2], 16 * (b // 2))
                at = bass.IndirectOffsetOnAxis(ap=gather_index[:, b:b + 1], axis=0)
                nc.gpsimd.indirect_dma_start(rows[:, b, :], None, xn_dram, at).then_inc(gathered[b % 2], 16)

            for b in range(AHEAD):
                gather(b)
            for b in range(NB):
                if b + AHEAD < NB:
                    gather(b + AHEAD)
                pool.wait_ge(y_ready, b + 1)
                at = bass.IndirectOffsetOnAxis(ap=scatter_index[:, b:b + 1], axis=0)
                nc.gpsimd.indirect_dma_start(y_dram, at, y[:, b, :], None, bounds_check=T - 1, oob_is_err=False
                                             ).then_inc(y_stored, 16)
            pool.wait_ge(y_stored, 16 * NB)

        @block.scalar
        def _(act):
            def rows_out(b, n, first=False):
                if not first:
                    act.wait_ge(hid_done, b - 1)
                act.wait_ge(row_turned, b + 1)
                nc.scalar.copy(rowT[n][:], rowT_ps[n][:, 0:P]).then_inc(rowT_ready, 1)

            def silu(b, first=False):
                act.wait_ge(hid_biased, b + 1)
                if not first:
                    act.wait_ge(h_turned, b)
                nc.scalar.activation(act_h[:], hid[:], ACT.Silu).then_inc(silu_done, 1)

            def work(b, n):
                rows_out(b + 2, n)
                silu(b)

            rows_out(0, 0, first=True)
            rows_out(1, 1, first=True)
            rows_out(2, 0)
            silu(0, first=True)
            with act.Fori(0, TRIPS) as trip:
                for j in range(1, 5):
                    work(trip * 4 + j, j % 2)
            silu(NB - 2)
            silu(NB - 1)

        @block.tensor
        def _(pe):
            def turn_rows(b, n, first=False):
                pe.wait_ge(row_staged, b + 1)
                if not first:
                    pe.wait_ge(rowT_ready, b - 1)
                nc.tensor.transpose(rowT_ps[n][:, 0:P], row_in[n][:], k.c("ident")).then_inc(row_turned, 1)

            def experts_of(trip):
                return loaded_experts(pe, expert_digits, trip)

            def first_layer(b, n, e):
                pe.wait_ge(rowT_ready, b + 1)
                if not isinstance(b, int) or b >= 2:
                    pe.wait_ge(hid_biased, b - 1)
                nc.tensor.matmul(hid_ps[n][:], rowT[n][:], k.w1[:, bass.ds(e * F, F)], start=True, stop=True).then_inc(hid_done, 1)

            def turn_hidden(b, first=False):
                pe.wait_ge(silu_done, b + 1)
                if not first:
                    pe.wait_ge(hT_ready, b)
                for f in range(KF):
                    last = nc.tensor.transpose(hT_ps[:, f, :], act_h[:, f * P:(f + 1) * P], k.c("ident"))
                last.then_inc(h_turned, 1)

            def second_layer(b, n, e, drained=True):
                pe.wait_ge(hT_ready, b + 1)
                if drained:
                    pe.wait_ge(y_ready, b - 1)
                for f in range(KF):
                    last = nc.tensor.matmul(y_ps[n][:, 0:C], hT[n][:, f, :], k.w2[:, bass.ds(e * F + f * P, P)], start=(f == 0), stop=(f == KF - 1))
                last.then_inc(y_done, 1)

            def work(b, n, e, e_second, turn=True, drained=True):
                first_layer(b, n, e)
                if turn:
                    turn_rows(b + 2, n)
                turn_hidden(b - 1)
                second_layer(b - 2, n, e_second, drained)

            turn_rows(0, 0, first=True)
            turn_rows(1, 1, first=True)
            pe.wait_ge(k.weights_loaded, k.n_weight_loads * 16)
            e = experts_of(0)
            first_layer(0, 0, e[1])
            turn_rows(2, 0)
            first_layer(1, 1, e[2])
            turn_rows(3, 1)
            turn_hidden(0, first=True)
            for b in range(2, 5):
                work(b, b % 2, e[b + 1], e[b - 1], drained=b >= 4)
            with pe.Fori(1, TRIPS) as trip:
                e = experts_of(trip)
                for j in range(1, 5):
                    work(trip * 4 + j, j % 2, e[j + 1], e[j - 1])
            e = experts_of(TRIPS)
            work(NB - 2, 1, e[2], e[0], turn=False)
            work(NB - 1, 0, e[3], e[1], turn=False)
            turn_hidden(NB - 1)
            second_layer(NB - 2, 1, e[2])
            second_layer(NB - 1, 0, e[3])

        @block.vector
        def _(dve):
            v = nc.vector

            def stage(b, n, first=False):
                dve.wait_ge(gathered[n], (b // 2) * 16 + 16 if isinstance(b, int) else b * 8 + (16 - 8 * n))
                if not first:
                    dve.wait_ge(row_turned, b - 1)
                v.tensor_copy(row_in[n][:], rows[:, bass.ds(b, 1), :].rearrange("p a c -> p (a c)")).then_inc(row_staged, 1)

            def experts_of(trip):
                return loaded_experts(dve, expert_digits, trip)

            def bias(b, n, e, first=False):
                dve.wait_ge(hid_done, b + 1)
                if not first:
                    dve.wait_ge(silu_done, b)
                v.tensor_tensor(hid[:], hid_ps[n][:], k.b1[:, bass.ds(e * F, F)], ALU.add).then_inc(hid_biased, 1)

            def hidden_out(b, n, first=False):
                dve.wait_ge(h_turned, b + 1)
                if not first:
                    dve.wait_ge(y_done, b - 1)
                v.tensor_copy(hT[n][:], hT_ps[:]).then_inc(hT_ready, 1)

            def y_out(b, n, e):
                dve.wait_ge(y_done, b + 1)
                v.tensor_tensor(y[:, bass.ds(b, 1), :].rearrange("p a c -> p (a c)"), y_ps[n][:, 0:C], k.b2[:, bass.ds(e * C, C)], ALU.add
                                ).then_inc(y_ready, 1)

            def work(b, n, e, e_second, ahead=True, first=False):
                bias(b, n, e)
                if ahead:
                    stage(b + 3, 1 - n)
                hidden_out(b - 1, 1 - n, first)
                y_out(b - 2, n, e_second)

            stage(0, 0, first=True)
            stage(1, 1, first=True)
            dve.wait_ge(k.weights_loaded, k.n_weight_loads * 16)
            stage(2, 0)
            e = experts_of(0)
            bias(0, 0, e[1], first=True)
            stage(3, 1)
            bias(1, 1, e[2])
            stage(4, 0)
            hidden_out(0, 0, first=True)
            for b in range(2, 5):
                work(b, b % 2, e[b + 1], e[b - 1], first=b == 2)
            with dve.Fori(1, TRIPS - 1) as trip:
                e = experts_of(trip)
                for j in range(1, 5):
                    work(trip * 4 + j, j % 2, e[j + 1], e[j - 1])
            e = experts_of(TRIPS - 1)
            for j in range(1, 5):
                b = 4 * (TRIPS - 1) + j
                work(b, j % 2, e[j + 1], e[j - 1], ahead=b + 3 < NB)
            e = experts_of(TRIPS)
            work(NB - 2, 1, e[2], e[0], ahead=False)
            work(NB - 1, 0, e[3], e[1], ahead=False)
            hidden_out(NB - 1, 0)
            y_out(NB - 2, 1, e[2])
            y_out(NB - 1, 0, e[3])


def combine(k, tag, y_dram, y, weight, result):
    nc = k.nc
    with ExitStack() as ctx:
        y_loaded = [ctx.enter_context(nc.semaphore(f"y_loaded{g}_{tag}")) for g in range(NT // GB)]
        x_ready = ctx.enter_context(nc.semaphore(f"x_ready_{tag}"))
        x_stored = ctx.enter_context(nc.semaphore(f"x_stored_{tag}"))
        block = ctx.enter_context(nc.Block())
        y_rows = y_dram.rearrange("(i p) c -> p i c", p=P)

        @block.sync
        def _(sp):
            for g in range(NT // GB):
                sp.dma_start(y[:, g * GB:(g + 1) * GB, :], y_rows[:, g * GB:(g + 1) * GB, :]).then_inc(y_loaded[g], 16)
            if result is not None:
                out_rows = result.rearrange("(i p) c -> p i c", p=P)
                for g in range(NT // GB):
                    sp.wait_ge(x_ready, (g + 1) * GB)
                    sp.dma_start(out_rows[:, g * GB:(g + 1) * GB, :], k.x[:, g * GB:(g + 1) * GB, :]).then_inc(x_stored, 16)
                sp.wait_ge(x_stored, 16 * (NT // GB))

        @block.vector
        def _(dve):
            for i in range(NT):
                if i % GB == 0:
                    dve.wait_ge(y_loaded[i // GB], 16)
                nc.vector.scalar_tensor_tensor(k.x[:, i, :], y[:, i, :], weight[:, i:i + 1], k.x[:, i, :], ALU.mult, ALU.add
                                               ).then_inc(x_ready, 1)


def attention(k):
    nc = k.nc
    with ExitStack() as ctx:
        def sb(name, shape, dt=F32):
            return ctx.enter_context(nc.sbuf_tensor(name, shape, dt))

        k.v = sb("v_rows", [P, NT, C])
        k.mixed = sb("mixed", [P, NT, C])
        k.share = sb("share", [P, H, 2])
        k.gk = sb("gk", [H * GR, T], BF16)
        k.parts_dram = nc.dram_tensor("parts_dram", [2, PARTS, C, T], BF16, kind="Internal").ap()
        k.dots = sb("dots", [P, 2, NT, H])
        k.parts_stored = [ctx.enter_context(nc.semaphore(f"parts_stored{g}")) for g in range(NT // GB)]
        k.laid = [ctx.enter_context(nc.semaphore(f"laid{g}")) for g in range(NT // GB)]
        k.ones_laid = ctx.enter_context(nc.semaphore("ones_laid"))
        with ExitStack() as inner:
            k.qt = inner.enter_context(nc.sbuf_tensor("qt", [KS, H, T], BF16))
            k.kt = inner.enter_context(nc.sbuf_tensor("kt", [KS, H, T], BF16))
            k.gq_memory = inner.enter_context(nc.sbuf_tensor("gq", [P, H * T], BF16))
            k.gq = k.gq_memory[0:H * GR].rearrange("g (h t) -> g h t", t=T)
            k.gq_written = inner.enter_context(nc.semaphore("gq_written"))
            project(k)
            k.va = inner.enter_context(nc.sbuf_tensor("va", [P, NT, 2, 32], F32))
            k.gqT = k.mixed[0:H * GR].rearrange("p i c -> p (i c)").bitcast(BF16)[:, 0:T]
            lay_out(k)
            attend(k)
        mix_out(k)


def runs(parts):
    out = []
    for j, a in enumerate(parts):
        if out and a == out[-1][1] + out[-1][2]:
            out[-1][2] += 1
        else:
            out.append([j, a, 1])
    return out


Q_RUNS, K_RUNS = (runs([product[w] for product in PRODUCTS]) for w in range(2))
LAID = 16 * (len(Q_RUNS) + len(K_RUNS))


def load_parts(k, sp, g):
    tokens = slice(g * GB * P, (g + 1) * GB * P)
    sp.wait_ge(k.parts_stored[g], 16)
    for w, to, places in ((0, k.qt, Q_RUNS), (1, k.kt, K_RUNS)):
        for j, a, n in places:
            src = k.parts_dram[w, a:a + n, :, tokens].rearrange("a (d h) t -> (a d) h t", h=H)
            sp.dma_start(to[j * D:(j + n) * D, :, tokens], src).then_inc(k.laid[g], 16)


def project(k):
    nc = k.nc
    with ExitStack() as ctx:
        def sb(name, shape, dt=F32):
            return ctx.enter_context(nc.sbuf_tensor(name, shape, dt))

        def ps(name, shape, dt=F32):
            return ctx.enter_context(nc.psum_tensor(name, shape, dt))

        def sem(name):
            return ctx.enter_context(nc.semaphore(name))

        xl = k.mixed
        xn = k.v
        wqkv = sb("wqkv", [C, 3 * C])
        gain, shift = sb("gain", [C, 1]), sb("ln_shift", [C, 1])
        dirs = sb("dirs", [P, H * 3])
        scales = sb("scales", [P, H])
        stat = sb("stat_a", [P, 2, NT, 3])
        halves = sb("halves_a", [P, NT, 6])
        qk = [sb(f"qk{n}", [P, GB, 2 * C]) for n in range(2)]
        parts = [sb(f"parts{n}", [P, PARTS, GB, 2 * C], BF16) for n in range(2)]
        n_partsT, n_r = 2 * PARTS * GB * P, GB * 2 * C
        partsT = [k.gq_memory[:, n * n_partsT:(n + 1) * n_partsT].rearrange("p (w a t) -> p w a t", w=2, a=PARTS) for n in range(2)]
        after = k.gq_memory[:, 2 * n_partsT:].bitcast(F32)
        n_xnT, n_dot = GB * P, 2 * GB * H * 3
        xnT = [sb("xnT_a", [C, n_xnT])[:], after[:, 4 * n_r:4 * n_r + n_xnT]]
        dot_in = after[:, 4 * n_r + n_xnT:4 * n_r + n_xnT + n_dot].rearrange("p (m h d) -> p m h d", h=H, d=3)
        r, rot = ([after[:, (2 * m + n) * n_r:(2 * m + n + 1) * n_r].rearrange("p (i c) -> p i c", c=2 * C) for n in range(2)] for m in range(2))

        xnT_ps = [ps(f"xnT_a_ps{n}", [P, 512]) for n in range(2)]
        qkv_ps = [ps(f"qkv_ps{n}", [P, 512]) for n in range(2)]
        TB = 4
        turn_ps = [ps(f"turn_ps{n}", [P, 2, GB * P], BF16) for n in range(TB)]

        loaded = sem("a_loaded")
        norm_xl, norm_xn = LayernormSems(sem, "xl"), LayernormSems(sem, "xn")
        x_ready, xn_turned, xnT_ready = (sem(f"a_{n}") for n in ("x_ready", "xn_turned", "xnT_ready"))
        projected, qkv_out, swapped = sem("a_projected"), sem("a_qkv_out"), sem("a_swapped")
        roped, part0, rest, part1, part2 = (sem(f"a_{n}") for n in ("roped", "part0", "rest", "part1", "part2"))
        turned = sem("a_turned")
        out0, out12 = sem("a_out0"), sem("a_out12")
        dve_steps = sem("a_dve_steps")
        NG = NT // GB
        half = D // 2

        def heads(ap, m):
            return ap[:, :, m * C:(m + 1) * C].rearrange("p i (h d) -> p i h d", d=D)

        def heads_inner(ap, m):
            return ap[:, :, m * C:(m + 1) * C].rearrange("p i (d h) -> p i h d", d=D)

        def table(name, g):
            t = k.c(name, g * GB * D, (g + 1) * GB * D).rearrange("p (i d) -> p i d", d=D)
            return t.unsqueeze(2).broadcast_to([P, GB, H, D])

        block = ctx.enter_context(nc.Block())

        @block.sync
        def _(sp):
            for dst, src in ((wqkv[:], k.arg["Wqkv_t"]), (gain[:], k.arg["ln_g"].unsqueeze(1)),
                             (shift[:], k.arg["ln_b"].unsqueeze(1)),
                             (dirs[:], k.arg["head_dirs"].rearrange("h d -> (h d)").partition_broadcast(P)),
                             (scales[:], k.arg["head_scales"].partition_broadcast(P))):
                sp.dma_start(dst, src).then_inc(loaded, 16)
            sp.dma_start(k.kt[KQ:KS].rearrange("a h t -> a (h t)"), k.arg["ones_rows"]).then_inc(k.ones_laid, 16)
            for g in range(NG):
                sp.wait_ge(out0, g + 1)
                sp.wait_ge(out12, 2 * (g + 1))
                tokens = slice(g * GB * P, (g + 1) * GB * P)
                sp.dma_start(k.parts_dram[:, :, :, tokens].rearrange("w a c t -> c (w a) t"),
                             partsT[g % 2].rearrange("p w a t -> p (w a) t")).then_inc(k.parts_stored[g], 16)
                if g == 1:
                    load_parts(k, sp, 0)

        @block.gpsimd
        def _(pool):
            v = nc.gpsimd
            norm_xl.wait(pool, NT // 4)
            v.tensor_tensor(k.x[:], k.x[:], xl[:], ALU.add).then_inc(x_ready, 1)
            for g in range(NG + 1):
                if g < NG:
                    pool.wait_ge(qkv_out, (g + 1) * GB)
                    if g >= 2:
                        pool.wait_ge(roped, g - 1)
                    for m in range(2):
                        src, dst, sin = heads(qk[g % 2][:], m), heads_inner(rot[g % 2], m), table("sin", g)
                        v.tensor_tensor(dst[..., 0:half], src[..., half:D], sin[..., 0:half], ALU.mult).then_inc(swapped, 1)
                        v.tensor_tensor(dst[..., half:D], src[..., 0:half], sin[..., half:D], ALU.mult).then_inc(swapped, 1)
                if g:
                    n = (g - 1) % 2
                    pool.wait_ge(part1, g)
                    if g >= 3:
                        pool.wait_ge(turned, PARTS * (g - 2))
                    v.tensor_tensor(parts[n][:, 2], r[n], parts[n][:, 1], ALU.subtract).then_inc(part2, 1)

        @block.scalar
        def _(act):
            layernorm_scalar(nc, act, norm_xl, k.x, xl, stat[:, 0])
            norm_xl.wait(act, NT // 4)
            layernorm_scalar(nc, act, norm_xn, xl, xn, stat[:, 1])
            act.wait_ge(loaded, 80)

            def normalised_out(g):
                act.wait_ge(xn_turned, g + 1)
                nc.scalar.activation(xnT[g % 2], xnT_ps[g % 2][:], ACT.Identity, bias=shift[:], scale=gain[:]).then_inc(xnT_ready, 1)

            normalised_out(0)
            for g in range(NG + 2):
                if g < NG:
                    if g >= 2:
                        act.wait_ge(roped, g - 1)
                    for i in range(GB):
                        t = g * GB + i
                        act.wait_ge(projected, t + 1)
                        nc.scalar.copy(qk[g % 2][:, i, :], qkv_ps[t % 2][:, 0:2 * C])
                        nc.scalar.copy(k.v[:, t, :], qkv_ps[t % 2][:, 2 * C:3 * C]).then_inc(qkv_out, 1)
                if g + 1 < NG:
                    normalised_out(g + 1)
                if 1 <= g <= NG:
                    n = (g - 1) % 2
                    act.wait_ge(roped, g)
                    if g >= 3:
                        act.wait_ge(turned, PARTS * (g - 2))
                    nc.scalar.copy(parts[n][:, 0], r[n]).then_inc(part0, 1)
                    act.wait_ge(rest, g)
                    nc.scalar.copy(parts[n][:, 1], r[n]).then_inc(part1, 1)
                if g >= 2:
                    act.wait_ge(turned, PARTS * (g - 2) + 1)
                    if g >= 4:
                        act.wait_ge(k.parts_stored[g - 4], 16)
                    nc.scalar.copy(partsT[g % 2][:, :, 0], turn_ps[PARTS * (g - 2) % TB][:]).then_inc(out0, 1)

        @block.tensor
        def _(pe):
            pe.wait_ge(loaded, 80)

            def turn_normalised(g):
                if g >= 2:
                    pe.wait_ge(xnT_ready, g - 1)
                norm_xn.wait(pe, g + 1)
                for i in range(GB):
                    last = nc.tensor.transpose(xnT_ps[g % 2][:, i * P:(i + 1) * P], xn[:, g * GB + i, :], k.c("ident"))
                last.then_inc(xn_turned, 1)

            turn_normalised(0)
            for g in range(NG + 2):
                if g < NG:
                    pe.wait_ge(xnT_ready, g + 1)
                    for i in range(GB):
                        t = g * GB + i
                        if t >= 2:
                            pe.wait_ge(qkv_out, t - 1)
                        nc.tensor.matmul(qkv_ps[t % 2][:, 0:3 * C], xnT[g % 2][:, i * P:(i + 1) * P], wqkv[:], start=True, stop=True).then_inc(projected, 1)
                if g + 1 < NG:
                    turn_normalised(g + 1)
                if g >= 2:
                    for a, ready in enumerate((part0, part1, part2)):
                        m = PARTS * (g - 2) + a
                        pe.wait_ge(ready, g - 1)
                        if m >= TB:
                            g_last, a_last = divmod(m - TB, PARTS)
                            if a_last:
                                pe.wait_ge(out12, 2 * g_last + a_last)
                            else:
                                pe.wait_ge(out0, g_last + 1)
                        for w in range(2):
                            for i in range(GB):
                                last = nc.tensor.transpose(turn_ps[m % TB][:, w, i * P:(i + 1) * P],
                                                           parts[g % 2][:, a, i, w * C:(w + 1) * C], k.cbf("ident"))
                        last.then_inc(turned, 1)

        @block.vector
        def _(dve):
            v = nc.vector
            s = Steps(dve, dve_steps)
            layernorm(nc, s, norm_xl, k.x, xl, halves, stat[:, 0])
            norm_xl.wait(dve, NT // 4)
            layernorm(nc, s, norm_xn, xl, xn, halves, stat[:, 1])
            dve.wait_ge(loaded, 80)
            v.tensor_copy(k.share[:, :, 1], scales[:])
            v.tensor_scalar(k.share[:, :, 0], scales[:], -1.0, 1.0, ALU.mult, ALU.add)

            for g in range(NG + 2):
                n = g % 2
                if g < NG:
                    dve.wait_ge(qkv_out, (g + 1) * GB)
                    if g >= 2:
                        dve.wait_ge(part2, g - 1)
                    for m in range(2):
                        s.mark(v.tensor_tensor(heads_inner(r[n], m), heads(qk[n][:], m), table("cos", g), ALU.mult))
                if 1 <= g <= NG:
                    dve.wait_ge(part0, g)
                    v.tensor_tensor(r[1 - n], r[1 - n], parts[1 - n][:, 0], ALU.subtract).then_inc(rest, 1)
                if g < NG:
                    dve.wait_ge(swapped, 4 * (g + 1))
                    dve.wait_ge(dve_steps, s.value())
                    s.link(v.tensor_tensor(r[n], r[n], rot[n], ALU.add))
                    d = dirs[:].rearrange("p (h d) -> p h d", d=3).unsqueeze(1).broadcast_to([P, 2 * GB, H, 3])
                    rows = r[n].rearrange("p i (m d h) -> p (i m) h d", m=2, d=D)[:, :, :, 0:3]
                    s.link(v.tensor_tensor(dot_in, rows, d, ALU.mult))
                    v.tensor_scalar(r[n][:, :, C:2 * C], r[n][:, :, C:2 * C], float(D) ** -0.5, None, ALU.mult).then_inc(roped, 1)
                    s.mark(v.tensor_reduce(k.dots[:, :, g * GB:(g + 1) * GB, :].rearrange("p w i h -> p i w h"),
                                           dot_in.rearrange("p (i w) h d -> p i w h d", w=2), AX.X, ALU.add))
                if g >= 2:
                    for a in (1, 2):
                        dve.wait_ge(turned, PARTS * (g - 2) + a + 1)
                        if g >= 4:
                            dve.wait_ge(k.parts_stored[g - 4], 16)
                        v.tensor_copy(partsT[n][:, :, a], turn_ps[(PARTS * (g - 2) + a) % TB][:]).then_inc(out12, 1)


def lay_out(k):
    nc = k.nc
    with ExitStack() as ctx:
        def sb(name, shape, dt=F32):
            return ctx.enter_context(nc.sbuf_tensor(name, shape, dt))

        def ps(name, shape, dt=F32):
            return ctx.enter_context(nc.psum_tensor(name, shape, dt))

        def sem(name):
            return ctx.enter_context(nc.semaphore(name))

        rest = sb("dot_rest", [P, 3, NT * H])
        parts = sb("dot_parts", [P, PARTS, 3, NT * H], BF16)
        largest = sb("geo_max", [P, 3, NT * H])
        kdT, upto = sb("kdT", [NT * H, 2, P]), sb("kd_upto", [NT * H, 2, P])
        PAD = NT * H // 2
        tiles = [sb(f"tile_max{n}", [2, PAD + NT * H]) for n in range(2)]
        before = sb("kd_before", [NT * H, 2])
        gka = sb("gka", [P, NT * H, GR], BF16)
        gqa = sb("gqa", [P, NT * H, GR], BF16)
        kd_ps, last_ps, before_ps, upto_ps = (ps(f"g_{n}_ps", [P, 512]) for n in ("kd", "last", "before", "upto"))
        turn_ps = [ps(f"g_turn_ps{n}", [P, 1024], BF16) for n in range(4)]

        cleared = sem("va_cleared")
        kd_turned, kd_scanned, last_turned, tiles_scanned, before_turned, upto_ready, upto_turned = (
            sem(f"g_{n}") for n in ("kd_turned", "kd_scanned", "last_turned", "tiles_scanned", "before_turned", "upto", "upto_turned"))
        parts_ready, key_rows, query_rows, rows_turned = (
            sem(f"g_{n}") for n in ("parts_ready", "key_rows", "query_rows", "rows_turned"))
        dve_steps = sem("g_steps")
        block = ctx.enter_context(nc.Block())

        @block.sync
        def _(sp):
            for g in range(1, NT // GB):
                load_parts(k, sp, g)

        @block.gpsimd
        def _(pool):
            nc.gpsimd.memset(gka[:], 1.0).then_inc(cleared, 1)
            nc.gpsimd.memset(k.va[:], 0.0).then_inc(cleared, 1)
            pool.wait_ge(cleared, 2)
            nc.gpsimd.memset(k.va[:, :, :, D:D + 1], 1.0)
            nc.gpsimd.tensor_copy(k.va[:, :, :, 0:D], k.v[:, :, 0:2 * D].rearrange("p j (h d) -> p j h d", d=D))

        @block.tensor
        def _(pe):
            ident = k.c("ident")
            nc.tensor.transpose(kd_ps[:, 0:P], k.dots[:, 1].rearrange("p i h -> p (i h)"), ident).then_inc(kd_turned, 1)
            pe.wait_ge(kd_scanned, 1)
            nc.tensor.transpose(last_ps[0:2, 0:P], upto[:, :, P - 1], ident).then_inc(last_turned, 1)
            pe.wait_ge(tiles_scanned, 1)
            nc.tensor.transpose(before_ps[:, 0:2], tiles[0][:, PAD:], ident[0:2, 0:2]).then_inc(before_turned, 1)
            pe.wait_ge(upto_ready, 2)
            for m in range(2):
                last = nc.tensor.transpose(upto_ps[:, m * P:(m + 1) * P], upto[:, m, :], ident)
            last.then_inc(upto_turned, 1)
            for m, (rows, ready, n) in enumerate(((gqa, query_rows, 2 * PARTS), (gka, key_rows, PARTS))):
                pe.wait_ge(ready, n)
                for i in range(NT):
                    last = nc.tensor.transpose(turn_ps[2 * m + i // 8][0:H * GR, (i % 8) * P:(i % 8 + 1) * P],
                                               rows[:, i * H:(i + 1) * H].rearrange("p h g -> p (h g)"), k.cbf("ident"))
                last.then_inc(rows_turned, 1)

        @block.scalar
        def _(act):
            act.wait_ge(cleared, 1)
            act.wait_ge(parts_ready, 1)
            for a in range(PARTS):
                nc.scalar.copy(gka[:, :, a * PARTS:(a + 1) * PARTS], wide(parts[:, a, 1, :], PARTS)).then_inc(key_rows, 1)
            act.wait_ge(rows_turned, 1)
            nc.scalar.copy(k.gqT[:, 1024:2048], turn_ps[1][0:H * GR, :])
            act.wait_ge(rows_turned, 2)
            nc.scalar.copy(k.gk[:, 1024:2048], turn_ps[3][0:H * GR, :])

        @block.vector
        def _(dve):
            v = nc.vector
            s = Steps(dve, dve_steps)
            for buffer in tiles:
                s.mark(v.memset(buffer[:], -3e38))
            dve.wait_ge(kd_turned, 1)
            s.mark(v.tensor_copy(kdT[:, 0, :], kd_ps[:, 0:P]))
            s.link(v.tensor_scalar(kdT[:, 1, :], kd_ps[:, 0:P], -1.0, None, ALU.mult))
            s.mark(v.tensor_tensor_scan(upto[:, 0, :], kdT[:, 0, :], kdT[:, 0, :], -3e38, ALU.max, ALU.max))
            s.link(v.tensor_tensor_scan(upto[:, 1, :], kdT[:, 1, :], kdT[:, 1, :], -3e38, ALU.max, ALU.max))
            v.sem_inc(kd_scanned, 1)
            dve.wait_ge(last_turned, 1)
            s.link(v.tensor_copy(tiles[0][:, PAD + H:], last_ps[0:2, 0:P - H]))
            for n, back in enumerate((1, 2, 4, 8)):
                src, dst = tiles[n % 2], tiles[1 - n % 2]
                last = v.tensor_tensor(dst[:, PAD:], src[:, PAD:], src[:, PAD - back * H:(PAD + NT * H) - back * H], ALU.max)
                s.link(last) if back < 8 else last.then_inc(tiles_scanned, 1)
            dve.wait_ge(before_turned, 1)
            s.link(v.tensor_copy(before[:], before_ps[:, 0:2]))
            for m in range(2):
                v.tensor_scalar(upto[:, m, :], upto[:, m, :], before[:, m:m + 1], None, ALU.max).then_inc(upto_ready, 1)
            qd = k.dots[:, 0].rearrange("p i h -> p (i h)")
            s.mark(v.tensor_copy(rest[:, 0:2, :], k.dots[:].rearrange("p w i h -> p w (i h)")))
            dve.wait_ge(upto_turned, 1)
            s.mark(v.tensor_tensor(largest[:, 0, :], upto_ps[:, 0:P], qd, ALU.mult))
            s.link(v.scalar_tensor_tensor(largest[:, 1, :], upto_ps[:, P:2 * P], -1.0, qd, ALU.mult, ALU.mult))
            s.link(v.tensor_tensor(largest[:, 2, :], largest[:, 0, :], largest[:, 1, :], ALU.max))
            s.link(v.tensor_scalar(rest[:, 2, :], largest[:, 2, :], -1.0, None, ALU.mult))
            s.link(v.tensor_copy(parts[:, 0], rest[:]))
            s.link(v.tensor_tensor(rest[:], rest[:], parts[:, 0], ALU.subtract))
            s.link(v.tensor_copy(parts[:, 1], rest[:]))
            s.link(v.tensor_tensor(parts[:, 2], rest[:], parts[:, 1], ALU.subtract))
            v.sem_inc(parts_ready, 1)
            for a in range(PARTS):
                v.tensor_copy(gqa[:, :, a:PARTS * PARTS:PARTS], wide(parts[:, a, 0, :], PARTS)).then_inc(query_rows, 1)
                v.tensor_copy(gqa[:, :, PARTS * PARTS + a], parts[:, a, 2, :]).then_inc(query_rows, 1)
            dve.wait_ge(rows_turned, 1)
            v.tensor_copy(k.gqT[:, 0:1024], turn_ps[0][0:H * GR, :])
            dve.wait_ge(rows_turned, 2)
            v.tensor_copy(k.gk[:, 0:1024], turn_ps[2][0:H * GR, :])


STEPS = [(c, j) for c in range(NCH) for j in range(4 * c + 4)]
NSTEP = len(STEPS)
LAST = [4 * (c + 1) * (c + 2) // 2 - 1 for c in range(NCH)]


def unit_items(pair, c):
    return [("scores", pair, c, hd, i, w) for hd in range(2) for i in range(4) for w in range(c + 1)]


def plan(units):
    items, waiting = [], None
    for pair, c in units:
        own = unit_items(pair, c)
        own[-1] = own[-1] + ("ends",)
        for n, item in enumerate(own):
            items.append(item)
            if n == 3 and waiting:
                items.append(waiting)
        waiting = ("turn", pair, c)
    return items + [waiting]


def attend(k):
    nc = k.nc
    with ExitStack() as ctx:
        def sb(name, shape, dt=F32):
            return ctx.enter_context(nc.sbuf_tensor(name, shape, dt))

        def ps(name, shape, dt=F32):
            return ctx.enter_context(nc.psum_tensor(name, shape, dt))

        def sem(name):
            return ctx.enter_context(nc.semaphore(name))

        prob = sb("prob_a", [P, 4, 2, CH])
        part_max = sb("part_max", [P, 2, 8, NCH])
        shift = sb("shift", [P, 8])
        one = sb("one", [P, 1])
        shift_parts = sb("shift_parts", [P, 2, PARTS, 4], BF16)
        shiftT = sb("shiftT", [2 * PARTS * 4, 2, P], BF16)
        acc = sb("acc_rows", [P, CH])
        inv = sb("inv", [P, 4, 4])
        scaled = sb("scaled", [P, 4, 4, D])
        score_ps = ps("score_ps", [P, 2, 2, CH])
        acc_ps = [ps(f"acc_ps{n}", [P, CH]) for n in range(2)]
        max_ps = [ps(f"max_ps{n}", [P, CH]) for n in range(2)]

        first_banks = [m[:] for m in max_ps] + [score_ps[:, hd, kind, :] for hd in range(2) for kind in range(2)]
        max_ps = [m[:] for m in max_ps]

        scores_ready, exp_done = sem("scores_ready"), sem("exp_done")
        pv_done, acc_out, acc_turned, acc_free = (sem(n) for n in ("pv_done", "acc_out", "acc_turned", "acc_free"))
        va_ready = sem("va_ready")
        item_ready, item_out = sem("item_ready"), sem("item_out")
        parts_ready, shift_stored = sem("shift_parts_ready"), sem("shift_stored")
        dve_steps = sem("attend_steps")

        first = plan([(0, 0), (0, 1)])
        per_pair = plan([(0, 2), (0, 3), (1, 0), (1, 1)])
        last_pair = plan([(0, 2), (0, 3)])
        assert len(per_pair) % 2 == 0 and len(first) % 2 == 0
        quota = [4] * 3 + [3] * 14 + [2] * 8 + [1] * 14 + [0] * 1

        def split(items):
            out, at = [], 0
            for q in quota:
                out.append(items[at:at + q])
                at += q
            assert at >= len(items)
            busy = [st for st in range(NSTEP) if out[st]]
            out[busy[-1] + 1] = [out[busy[-1]].pop()]
            return out

        def offset(c, j):
            return max(0, j - 4 * c) * P

        GROUPS = {(0, 0): 1, (2, 8): 2, (3, 12): 3}
        CREDIT = 2
        N_ACT = 6
        STORED = 16 * 2
        order = first + per_pair * (NPAIR - 1) + last_pair
        turned_at = [n + 1 for n, item in enumerate(order) if item[0] == "turn"]
        block = ctx.enter_context(nc.Block())

        @block.tensor
        def _(pe):
            def scores(pair, st, hd, slots_used=True):
                c, j = STEPS[st]
                off = offset(c, j)
                if j == 0 and hd == 0:
                    pe.wait_ge(shift_stored, (pair * 4 + c + 1) * STORED)
                if slots_used:
                    pe.wait_ge(exp_done, pair * (2 * NSTEP) + (2 * st + hd - 1))
                h = pair * 2 + hd
                q = slice(c * CH + off, (c + 1) * CH)
                diagonal = j >= 4 * c
                nc.tensor.matmul(score_ps[:, hd, 0, off:], k.kt[:, bass.ds(h, 1), j * P:(j + 1) * P].rearrange("k a t -> k (a t)"),
                                 k.qt[:, bass.ds(h, 1), q].rearrange("k a t -> k (a t)"), start=True, stop=not diagonal)
                last = nc.tensor.matmul(score_ps[:, hd, 1, off:], k.gk[:, j * P:(j + 1) * P],
                                        k.gq[:, bass.ds(h, 1), q].rearrange("k a t -> k (a t)"), start=True, stop=not diagonal)
                if diagonal:
                    for kind in range(2):
                        last = nc.tensor.matmul(score_ps[:, hd, kind, off:off + P], k.cbf("ident"), k.cbf("future_t"), start=False, stop=True)
                last.then_inc(scores_ready, 1)

            def run_items(items, pair, count, unit):
                for n, item in enumerate(items):
                    m = banks[(n + parity[0]) % len(banks)]
                    if primed[0] >= len(banks):
                        pe.wait_ge(item_out, count + n + 1 - len(banks))
                    primed[0] += 1
                    if item[0] == "scores":
                        _, dp, c, hd, i, w = item[:6]
                        h = (pair + dp) * 2 + hd
                        width = CH if w < c else (i + 1) * P
                        q0 = c * CH + i * P
                        last = nc.tensor.matmul(m[:, 0:width], k.qt[0:KQ, bass.ds(h, 1), q0:q0 + P].rearrange("k a t -> k (a t)"),
                                                k.kt[0:KQ, bass.ds(h, 1), w * CH:w * CH + width].rearrange("k a t -> k (a t)"), start=True, stop=w < c)
                        if w == c:
                            last = nc.tensor.matmul(m[:, i * P:(i + 1) * P], k.cbf("ident"), k.cbf("future"), start=False, stop=True)
                        last.then_inc(item_ready, 1)
                    else:
                        pe.wait_ge(parts_ready, unit + 1)
                        unit = unit + 1
                        nc.tensor.transpose(m.bitcast(BF16)[0:24, 0:P], shift_parts[:].rearrange("p a b c -> p (a b c)"), k.cbf("ident")
                                            ).then_inc(item_ready, 1)
                parity[0] += len(items)
                return unit

            def values(pair, st):
                c, j = STEPS[st]
                off = offset(c, j)
                if (c, j) in GROUPS:
                    pe.wait_ge(va_ready, pair * 3 + GROUPS[c, j])
                if j == 0:
                    pe.wait_ge(acc_free, pair * 4 + c + 1)
                pe.wait_ge(exp_done, pair * (2 * NSTEP) + 2 * (st + 1))
                for hd in range(2):
                    for kind in range(2):
                        o = 32 * (2 * hd + kind)
                        last = nc.tensor.matmul(acc_ps[c % 2][o:o + 32, off:], k.va[:, j, hd, :], prob[:, (st % 2) * 2 + hd, kind, off:],
                                                start=(j == 0), stop=(j == 4 * c + 3))
                last.then_inc(pv_done, 1)

            def turn_acc(pair, c):
                pe.wait_ge(acc_out, pair * 4 + c + 1)
                for t in range(4):
                    last = nc.tensor.transpose(acc_ps[c % 2][:, t * P:(t + 1) * P], acc[:, t * P:(t + 1) * P], k.c("ident"))
                last.then_inc(acc_turned, 1)

            def body(pair, items, more):
                count = pair * len(per_pair) + len(first)
                unit = pair * 4 + 2
                done = 0
                for st in range(NSTEP):
                    for hd in range(2):
                        if st + 1 < NSTEP:
                            scores(pair, st + 1, hd)
                        elif more:
                            scores(pair + 1, 0, hd)
                        unit = run_items(items[st][hd:hd + 1], pair, count + done, unit)
                        done += len(items[st][hd:hd + 1])
                    values(pair, st)
                    unit = run_items(items[st][2:], pair, count + done, unit)
                    done += len(items[st][2:])
                    for c in range(NCH - 1):
                        if st == LAST[c] + 2:
                            turn_acc(pair, c)
                turn_acc(pair, NCH - 1)

            parity, primed = [0], [0]
            banks = first_banks
            pe.wait_ge(k.laid[0], LAID)
            at = len(unit_items(0, 0))
            run_items(first[:at], 0, 0, 0)
            pe.wait_ge(k.laid[1], LAID)
            run_items(first[at:-1], 0, at, 0)
            pe.wait_ge(k.laid[2], LAID)
            pe.wait_ge(k.laid[3], LAID)
            pe.wait_ge(k.ones_laid, 16)
            pe.wait_ge(item_out, len(first) - 1)
            pe.wait_ge(k.gq_written, H)
            for hd in range(2):
                scores(0, 0, hd, slots_used=False)
            banks, parity[0] = max_ps, 0
            run_items(first[-1:], 0, len(first) - 1, 1)
            with pe.Fori(0, NPAIR - 1) as pair:
                body(pair, split(per_pair), True)
            body(NPAIR - 1, split(last_pair), False)

        @block.scalar
        def _(act):
            def body(pair):
                for st, (c, j) in enumerate(STEPS):
                    off = offset(c, j)
                    act.wait_ge(pv_done, pair * NSTEP + st - 1 + CREDIT)
                    for hd in range(2):
                        act.wait_ge(scores_ready, pair * (2 * NSTEP) + 2 * st + hd + 1)
                        nc.scalar.activation(prob[:, (st % 2) * 2 + hd, :, off:], score_ps[:, hd, :, off:], ACT.Exp).then_inc(exp_done, 1)

            act.wait_ge(k.parts_stored[-1], 16)
            for h in range(N_ACT):
                nc.scalar.activation(k.gq[:, h, :], k.gqT, ACT.Copy, scale=k.c("head_rows", h, h + 1)[0:H * GR]).then_inc(k.gq_written, 1)
            nc.scalar.activation(one[:], k.c("lane", 0, 1), ACT.Exp)
            with act.Fori(0, NPAIR) as pair:
                body(pair)

        @block.gpsimd
        def _(pool):
            def values_in(pair, j0, j1):
                nc.gpsimd.tensor_copy(k.va[:, j0:j1, :, 0:D], k.v[:, j0:j1, bass.ds((pair + 1) * 2 * D, 2 * D)].rearrange("p j (h d) -> p j h d", d=D)
                                      ).then_inc(va_ready, 1)

            pool.wait_ge(k.parts_stored[-1], 16)
            for h in range(N_ACT, H):
                own = k.c("head_rows", h, h + 1)[0:H * GR].broadcast_to([H * GR, T])
                nc.gpsimd.tensor_tensor(k.gq[:, h, :], k.gqT, own, ALU.mult).then_inc(k.gq_written, 1)
            pool.sem_inc(pv_done, CREDIT)
            pool.sem_inc(va_ready, 3)
            with pool.Fori(0, NPAIR - 1) as pair:
                for j0, j1 in ((0, 8), (8, 12), (12, 16)):
                    pool.wait_ge(pv_done, pair * NSTEP + NSTEP - NT + j1 + CREDIT)
                    values_in(pair, j0, j1)

        @block.sync
        def _(sp):
            for u in range(4 * NPAIR):
                pair, c = u // 4, u % 4
                sp.wait_ge(item_out, turned_at[u])
                for hd in range(2):
                    rows = shiftT[hd * PARTS * 4:(hd + 1) * PARTS * 4, u % 2, :]
                    sp.dma_start(k.qt[KQ:KS, 2 * pair + hd, c * CH:(c + 1) * CH], rows).then_inc(shift_stored, 16)
                sp.wait_ge(shift_stored, STORED * (u + 1))

        @block.vector
        def _(dve):
            v = nc.vector
            s = Steps(dve, dve_steps)

            def finish_unit(c):
                s.link(v.tensor_reduce(shift[:], part_max[:, c % 2, :, 0:c + 1], AX.X, ALU.max, negate=True))
                rows = shift[:].rearrange("p (h i) -> p h i", i=4)
                s.link(v.tensor_copy(shift_parts[:, :, 0, :], rows))
                s.link(v.tensor_tensor(rows, rows, shift_parts[:, :, 0, :], ALU.subtract))
                s.link(v.tensor_copy(shift_parts[:, :, 1, :], rows))
                v.tensor_tensor(shift_parts[:, :, 2, :], rows, shift_parts[:, :, 1, :], ALU.subtract).then_inc(parts_ready, 1)

            def run_items(items, count, unit):
                for n, item in enumerate(items):
                    m = banks[(n + parity[0]) % len(banks)]
                    dve.wait_ge(item_ready, count + n + 1)
                    if item[0] == "scores":
                        _, _, c, hd, i, w = item[:6]
                        width = CH if w < c else (i + 1) * P
                        v.tensor_reduce(part_max[:, c % 2, hd * 4 + i, w:w + 1], m[:, 0:width], AX.X, ALU.max).then_inc(item_out, 1)
                        if item[-1] == "ends":
                            dve.wait_ge(item_out, count + n + 1)
                            finish_unit(c)
                    else:
                        c = item[2]
                        if stored[0]:
                            dve.wait_ge(shift_stored, (unit - 1) * STORED)
                        v.tensor_copy(shiftT[:, c % 2, :], m.bitcast(BF16)[0:24, 0:P]).then_inc(item_out, 1)
                        unit = unit + 1
                parity[0] += len(items)
                return unit

            def acc_to_rows(pair, st):
                c = STEPS[st][0]
                dve.wait_ge(pv_done, pair * NSTEP + st + 1 + CREDIT)
                v.tensor_copy(acc[:], acc_ps[c % 2][:]).then_inc(acc_out, 1)

            def mix(pair, c):
                dve.wait_ge(acc_turned, pair * 4 + c + 1)
                sums = acc_ps[c % 2][:].rearrange("p (t q r) -> p t q r", q=4, r=32)
                s.link(v.reciprocal(inv[:], sums[:, :, :, D]))
                share = k.share[:, bass.ds(pair * 2, 2), :].rearrange("p h k -> p (h k)")
                s.link(v.tensor_tensor(inv[:], inv[:], each(share, 4), ALU.mult))
                v.tensor_tensor(scaled[:], sums[:, :, :, 0:D], inv[:].unsqueeze(3).broadcast_to([P, 4, 4, D]), ALU.mult).then_inc(acc_free, 1)
                dve.wait_ge(acc_free, pair * 4 + c + 1 + 2)
                kinds = scaled[:].rearrange("p t (h k) d -> p t h k d", k=2)
                out = k.mixed[:, 4 * c:4 * c + 4, bass.ds(pair * 2 * D, 2 * D)].rearrange("p t (h d) -> p t h d", d=D)
                s.mark(v.tensor_tensor(out, kinds[:, :, :, 0, :], kinds[:, :, :, 1, :], ALU.add))

            def body(pair, items):
                count = pair * len(per_pair) + len(first)
                unit = pair * 4 + 2
                done = 0
                for st in range(NSTEP):
                    for c in range(NCH - 1):
                        if st == LAST[c] + 3:
                            mix(pair, c)
                    unit = run_items(items[st][:2], count + done, unit)
                    done += len(items[st][:2])
                    if st in LAST:
                        acc_to_rows(pair, st)
                    unit = run_items(items[st][2:], count + done, unit)
                    done += len(items[st][2:])
                mix(pair, NCH - 1)

            parity, stored = [0], [False]
            dve.sem_inc(acc_free, 2)
            banks = first_banks
            unit = run_items(first[:-1], 0, 0)
            banks, parity[0] = max_ps, 0
            run_items(first[-1:], len(first) - 1, unit)
            stored[0] = True
            with dve.Fori(0, NPAIR - 1) as pair:
                s.enter(pair, 4 * 4 + 4 * 3)
                body(pair, split(per_pair))
                s.leave(NPAIR - 1)
            body(NPAIR - 1, split(last_pair))


def mix_out(k):
    nc = k.nc
    with ExitStack() as ctx:
        def sem(name):
            return ctx.enter_context(nc.semaphore(name))

        mixedT = ctx.enter_context(nc.sbuf_tensor("mixedT", [C, T], F32))
        turn_ps = [ctx.enter_context(nc.psum_tensor(f"o_turn_ps{n}", [P, 512], F32)) for n in range(2)]
        out_ps = [ctx.enter_context(nc.psum_tensor(f"o_out_ps{n}", [P, 512], F32)) for n in range(2)]
        turned, mixedT_ready, multiplied, added = (sem(f"o_{n}") for n in ("turned", "ready", "multiplied", "added"))
        block = ctx.enter_context(nc.Block())

        @block.tensor
        def _(pe):
            def multiply(g):
                pe.wait_ge(mixedT_ready, g + 1)
                if g >= 2:
                    pe.wait_ge(added, g - 1)
                for i in range(GB):
                    t = g * GB + i
                    last = nc.tensor.matmul(out_ps[g % 2][:, i * P:(i + 1) * P], mixedT[:, t * P:(t + 1) * P], k.wo[:], start=True, stop=True)
                last.then_inc(multiplied, 1)

            for g in range(NT // GB):
                if g >= 2:
                    pe.wait_ge(mixedT_ready, g - 1)
                for i in range(GB):
                    last = nc.tensor.transpose(turn_ps[g % 2][:, i * P:(i + 1) * P], k.mixed[:, g * GB + i, :], k.c("ident"))
                last.then_inc(turned, 1)
                if g:
                    multiply(g - 1)
            multiply(NT // GB - 1)

        @block.scalar
        def _(act):
            for g in range(NT // GB):
                act.wait_ge(turned, g + 1)
                nc.scalar.copy(mixedT[:, g * 512:(g + 1) * 512], turn_ps[g % 2][:]).then_inc(mixedT_ready, 1)

        @block.vector
        def _(dve):
            for g in range(NT // GB):
                dve.wait_ge(multiplied, g + 1)
                rows = k.x[:, g * GB:(g + 1) * GB, :].rearrange("p i c -> p (i c)")
                nc.vector.tensor_tensor(rows, rows, out_ps[g % 2][:], ALU.add).then_inc(added, 1)


def program(nc, a, out):
    with ExitStack() as ctx:
        k = Kernel(nc, ctx, a)

        k.weights_loaded = ctx.enter_context(nc.semaphore("weights_loaded"))
        k.x_loaded = [ctx.enter_context(nc.semaphore(f"x_loaded{g}")) for g in range(NT // GB)]
        tables = [
            (k.cf[:], a["constants"]),
            (k.wg[:], a["Wg"]),
            (k.bg[:], a["bg"].partition_broadcast(P)),
            (k.cb[:], a["constants_bf16"]),
        ]
        weights = [
            (k.w1[:, e * F:(e + 1) * F], a["W1"][e]) for e in range(E)
        ] + [
            (k.b1[:], a["b1"].rearrange("e f -> (e f)").partition_broadcast(P)),
            (k.b2[:], a["b2"].rearrange("e c -> (e c)").partition_broadcast(P)),
        ] + [
            (k.w2[:, e * F:(e + 1) * F].rearrange("p (f c) -> p f c", f=KF), a["W2"][e].rearrange("(f p) c -> p f c", p=P))
            for e in range(E)
        ]
        weights.append((k.wo[:], a["Wo_t"]))
        k.n_weight_loads = len(weights)
        assert len(tables) == N_FIRST_LOADS

        def load_all(sp, loaded):
            rows = a["x"].rearrange("(i p) c -> p i c", p=P)
            for g in range(NT // GB):
                sp.dma_start(k.x[:, g * GB:(g + 1) * GB, :], rows[:, g * GB:(g + 1) * GB, :]).then_inc(k.x_loaded[g], 16)
            for dst, src in tables:
                sp.dma_start(dst, src).then_inc(loaded, 16)
            for dst, src in weights:
                sp.dma_start(dst, src).then_inc(k.weights_loaded, 16)

        ffn(k, "first", load_all, None)
        attention(k)
        ffn(k, "second", None, out)


def kernel(**inputs):
    import ml_dtypes
    import concourse.bacc as bacc
    from concourse.bass_utils import run_bass_kernel_spmd

    g = {n: np.ascontiguousarray(v) for n, v in inputs.items()}
    bf16 = ml_dtypes.bfloat16
    laid = {
        "x": g["L0_attn_x"].reshape(T, C),
        "Wqkv_t": np.ascontiguousarray(np.concatenate([g["L0_attn_Wq"].T, g["L0_attn_Wk"].T, g["L0_attn_Wv"].T], 1)),
        "Wo_t": np.ascontiguousarray(g["L0_attn_Wo"].T),
        "ln_g": g["L0_attn_ln_g"],
        "ln_b": g["L0_attn_ln_b"],
        "head_scales": g["L0_attn_head_scales"],
        "head_dirs": g["L0_attn_head_dirs"],
        "Wg": g["L0_ffn_Wg"],
        "bg": g["L0_ffn_bg"],
        "W1": g["L0_ffn_W1"],
        "b1": g["L0_ffn_b1"],
        "W2": g["L0_ffn_W2"],
        "b2": g["L0_ffn_b2"],
        "constants": float_constants(),
        "constants_bf16": bf16_constants(bf16),
        "ones_rows": np.ones((PARTS, H * T), bf16),
    }
    nc = bacc.Bacc("TRN2", target_bir_lowering=False, num_devices=1)
    a = {n: nc.dram_tensor(f"in_{n}", v.shape, mybir.dt.from_np(v.dtype), kind="ExternalInput").ap() for n, v in laid.items()}
    out = nc.dram_tensor("out_x", (T, C), F32, kind="ExternalOutput").ap()
    program(nc, a, out)
    r = run_bass_kernel_spmd(nc, [{f"in_{n}": v for n, v in laid.items()}], core_ids=[0])
    return r.results[0]["out_x"].reshape(1, T, C)
```
